# Optimizing a Trainium2 kernel written in Bass

```python
import numpy as np
import jax
import jax.numpy as jnp

def _softmax(x, axis=-1):
    return jax.nn.softmax(x, axis=axis)

def _gelu(x):
    return jax.nn.gelu(x, approximate=True)

def _silu(x):
    return jax.nn.silu(x)

def _sigmoid(x):
    return jax.nn.sigmoid(x)

def _layernorm(x, axis=-1, eps=1e-05):
    m = jnp.mean(x, axis=axis, keepdims=True)
    v = jnp.var(x, axis=axis, keepdims=True)
    return (x - m) / jnp.sqrt(v + eps)

def _scatter_add(tgt, idx, src, axis=0):
    return tgt.at[idx].add(src)

def _segment_sum(src, seg, n):
    return jax.ops.segment_sum(src, seg, n)
kernel_name = 'mk_adaln_d2_jaxref_r8_89b478'

def setup_inputs(seed: int=0):
    np.random.seed(seed)
    _w = jnp.asarray

    def _L0_attn_setup():
        import jax, jax.numpy as jnp
        import numpy as np
        HIDDEN = 128
        HEADS = 16
        HEAD_DIM = HIDDEN // HEADS
        SCALE = HEAD_DIM ** (-0.5)
        key = jax.random.key(seed)
        ks = jax.random.split(key, 9)
        init = 1.0 / np.sqrt(HIDDEN)
        hidden_states = jax.random.normal(ks[0], (8, 128, HIDDEN), dtype=jnp.float32)

        def lin(k):
            kw, kb = jax.random.split(k)
            W = jax.random.uniform(kw, (HIDDEN, HIDDEN), jnp.float32, -init, init)
            b = jax.random.uniform(kb, (HIDDEN,), jnp.float32, -init, init)
            return (W, b)
        Wq, bq = lin(ks[1])
        Wk, bk = lin(ks[2])
        Wv, bv = lin(ks[3])
        Wo, bo = lin(ks[4])
        return {'hidden_states': hidden_states, 'Wq': Wq, 'bq': bq, 'Wk': Wk, 'bk': bk, 'Wv': Wv, 'bv': bv, 'Wo': Wo, 'bo': bo}
    _L0_attn_in = _L0_attn_setup()

    def _L0_ffn_setup():
        import jax, jax.numpy as jnp
        import numpy as np
        DIM = 128
        DEPTH = 6
        HEADS = 16
        DIM_HEAD = 64
        WINDOW = 32
        INNER = HEADS * DIM_HEAD
        DIM_INNER = int(DIM * 4 * 2 / 3)
        QK_SCALE = 8.0

        def shift_tokens(t):
            a, s = jnp.split(t, 2, -1)
            s = jnp.pad(s, ((0, 0), (1, 0), (0, 0)))[:, :-1]
            return jnp.concatenate([a, s], -1)

        def l2norm(t):
            return t / jnp.maximum(jnp.linalg.norm(t, axis=-1, keepdims=True), 1e-12)

        def rotate_half(x):
            x1, x2 = jnp.split(x, 2, -1)
            return jnp.concatenate([-x2, x1], -1)

        def rotary_tables(n):
            half = jnp.arange(0, DIM_HEAD, 2, dtype=jnp.float32)
            inv_freq = 1.0 / 10000.0 ** (half / DIM_HEAD)
            t = jnp.arange(n, dtype=jnp.float32)
            freqs = t[:, None] * inv_freq[None, :]
            freqs = jnp.concatenate([freqs, freqs], -1)
            base_scale = (half + 0.4 * DIM_HEAD) / (1.4 * DIM_HEAD)
            power = (t - n // 2) / (WINDOW // 2)
            scale = base_scale[None, :] ** power[:, None]
            scale = jnp.concatenate([scale, scale], -1)
            return (freqs, scale)

        def local_attention(q, k, v):
            b, h, n, d = q.shape
            w = WINDOW
            nw = n // w
            bq = q.reshape(b, h, nw, w, d)
            bk = k.reshape(b, h, nw, w, d)
            bv = v.reshape(b, h, nw, w, d)

            def look(t):
                p = jnp.pad(t, ((0, 0), (0, 0), (1, 0), (0, 0), (0, 0)))
                return jnp.concatenate([p[:, :, :nw], p[:, :, 1:]], axis=3)
            bk2, bv2 = (look(bk), look(bv))
            seq = jnp.arange(n).reshape(nw, w)
            seq_p = jnp.pad(seq, ((1, 0), (0, 0)), constant_values=-1)
            jt = jnp.concatenate([seq_p[:nw], seq_p[1:]], axis=1)
            it = seq[:, :, None]
            jb = jt[:, None, :]
            mask = (it < jb) | (it > jb + w) | (jb == -1)
            sim = jnp.einsum('bhwie,bhwje->bhwij', bq, bk2) * QK_SCALE
            sim = jnp.where(mask, -jnp.finfo(sim.dtype).max, sim)
            attn = jax.nn.softmax(sim, -1)
            out = jnp.einsum('bhwij,bhwje->bhwie', attn, bv2)
            return out.reshape(b, h, n, d)

        def attn_layer(x, Wqkv, qs, ksc, Wo):
            b, n, _ = x.shape
            qkv = x @ Wqkv
            q, k, v = jnp.split(qkv, 3, -1)
            sh = lambda t: t.reshape(b, n, HEADS, DIM_HEAD).transpose(0, 2, 1, 3)
            q, k, v = (sh(q), sh(k), sh(v))
            q = l2norm(q) * qs
            k = l2norm(k) * ksc
            freqs, scale = rotary_tables(n)
            cos, sin = (jnp.cos(freqs), jnp.sin(freqs))
            q = q * cos * scale + rotate_half(q) * sin * scale
            inv = 1.0 / scale
            k = k * cos * inv + rotate_half(k) * sin * inv
            out = local_attention(q, k, v)
            out = out.transpose(0, 2, 1, 3).reshape(b, n, INNER)
            return out @ Wo

        def ffn_layer(x, g, bln, W1, b1, W2, b2):
            mu = x.mean(-1, keepdims=True)
            var = ((x - mu) ** 2).mean(-1, keepdims=True)
            xn = (x - mu) / jnp.sqrt(var + 1e-05) * g + bln
            hg = xn @ W1 + b1
            a, gate = jnp.split(hg, 2, -1)
            return a * jax.nn.gelu(gate, approximate=False) @ W2 + b2
        key = jax.random.key(seed)
        ks = jax.random.split(key, 8)
        B, N = (2, 256)
        init = lambda k, shape: jax.random.normal(k, shape, jnp.float32) * 0.02
        return {'x': jax.random.normal(ks[0], (B, N, DIM), jnp.float32), 'Wqkv': init(ks[1], (DEPTH, DIM, 3 * INNER)), 'q_scale': jnp.ones((DEPTH, DIM_HEAD), jnp.float32), 'k_scale': jnp.ones((DEPTH, DIM_HEAD), jnp.float32), 'Wo': init(ks[2], (DEPTH, INNER, DIM)), 'ln_g': jnp.ones((DEPTH, DIM), jnp.float32), 'ln_b': jnp.zeros((DEPTH, DIM), jnp.float32), 'W1': init(ks[3], (DEPTH, DIM, 2 * DIM_INNER)), 'b1': jnp.zeros((DEPTH, 2 * DIM_INNER), jnp.float32), 'W2': init(ks[4], (DEPTH, DIM_INNER, DIM)), 'b2': jnp.zeros((DEPTH, DIM), jnp.float32)}
    _L0_ffn_in = _L0_ffn_setup()
    _L0_c = _w((lambda *s: np.random.randn(*s).astype(np.float32) * 0.05)(16, 128))
    _L0_wmod = _w((lambda *s: np.random.randn(*s).astype(np.float32) * 0.05)(128, 6 * 128) * 128 ** (-0.5))

    def _L1_attn_setup():
        import jax, jax.numpy as jnp
        import numpy as np
        DIM, D_INNER, D_STATE, DT_RANK, D_CONV = (128, 256, 16, 64, 4)
        BATCH, SEQ = (2, 128)

        def _silu(v):
            return v * jax.nn.sigmoid(v)

        def _ssm_forward(x, in_proj_w, conv_w, conv_b, x_proj_w, dt_proj_w, dt_proj_b, A_log, D_param, out_proj_w):
            b, l, _ = x.shape
            d_inner, d_conv = (conv_w.shape[0], conv_w.shape[2])
            dt_rank, n = (dt_proj_w.shape[0], A_log.shape[1])
            x_and_res = x @ in_proj_w
            xp, res = (x_and_res[..., :d_inner], x_and_res[..., d_inner:])
            h = jax.lax.conv_general_dilated(xp.transpose(0, 2, 1), conv_w, window_strides=(1,), padding=[(d_conv - 1, 0)], dimension_numbers=('NCH', 'OIH', 'NCH'), feature_group_count=d_inner) + conv_b[None, :, None]
            h = _silu(h.transpose(0, 2, 1))
            A = -jnp.exp(A_log)
            x_dbl = h @ x_proj_w
            dlt, Bm, Cm = (x_dbl[..., :dt_rank], x_dbl[..., dt_rank:dt_rank + n], x_dbl[..., dt_rank + n:])
            delta = jax.nn.softplus(dlt @ dt_proj_w + dt_proj_b)
            deltaA = jnp.exp(jnp.einsum('bld,dn->bldn', delta, A))
            deltaB_u = (delta * h)[..., None] * Bm[:, :, None, :]

            def step(state, t):
                dA_t, dBu_t, c_t = t
                state = dA_t * state + dBu_t
                y_t = jnp.einsum('bdn,bn->bd', state, c_t)
                return (state, y_t)
            init = jnp.zeros((b, d_inner, n), h.dtype)
            _, ys = jax.lax.scan(step, init, (deltaA.transpose(1, 0, 2, 3), deltaB_u.transpose(1, 0, 2, 3), Cm.transpose(1, 0, 2)))
            y = ys.transpose(1, 0, 2) + h * D_param
            y = y * _silu(res)
            return y @ out_proj_w
        key = jax.random.key(seed)
        ks = jax.random.split(key, 9)
        s = 0.02
        A = jnp.tile(jnp.arange(1, D_STATE + 1, dtype=jnp.float32), (D_INNER, 1))
        return {'x': jax.random.normal(ks[0], (BATCH, SEQ, DIM), jnp.float32), 'in_proj_w': jax.random.normal(ks[1], (DIM, 2 * D_INNER), jnp.float32) * s, 'conv_w': jax.random.normal(ks[2], (D_INNER, 1, D_CONV), jnp.float32) * 0.2, 'conv_b': jax.random.normal(ks[3], (D_INNER,), jnp.float32) * 0.1, 'x_proj_w': jax.random.normal(ks[4], (D_INNER, DT_RANK + 2 * D_STATE), jnp.float32) * s, 'dt_proj_w': jax.random.normal(ks[5], (DT_RANK, D_INNER), jnp.float32) * s, 'dt_proj_b': jax.random.normal(ks[6], (D_INNER,), jnp.float32) * 0.1, 'A_log': jnp.log(A), 'D_param': jnp.ones((D_INNER,), jnp.float32), 'out_proj_w': jax.random.normal(ks[7], (D_INNER, DIM), jnp.float32) * s}
    _L1_attn_in = _L1_attn_setup()

    def _L1_ffn_setup():
        import jax, jax.numpy as jnp
        import numpy as np
        ALPHA = 1.0
        key = jax.random.key(seed)
        ks = jax.random.split(key, 7)
        B, S, IN, OUT = (8, 1024, 128, 128)
        RANK, DDIM, UDIM = (4, 100, 50)
        return {'hidden_states': jax.random.normal(ks[0], (B, S, IN), dtype=jnp.float32), 'W': jax.random.normal(ks[1], (OUT, IN), dtype=jnp.float32) * 0.02, 'b': jax.random.normal(ks[2], (OUT,), dtype=jnp.float32) * 0.02, 'lora_down': jax.random.normal(ks[3], (RANK, DDIM), dtype=jnp.float32) * 0.1, 'lora_up': jax.random.normal(ks[4], (UDIM, RANK), dtype=jnp.float32) * 0.1, 'down_aux': jax.random.normal(ks[5], (DDIM, IN), dtype=jnp.float32) * 0.03, 'up_aux': jax.random.normal(ks[6], (OUT, UDIM), dtype=jnp.float32) * 0.03}
    _L1_ffn_in = _L1_ffn_setup()
    _L1_c = _w((lambda *s: np.random.randn(*s).astype(np.float32) * 0.05)(16, 128))
    _L1_wmod = _w((lambda *s: np.random.randn(*s).astype(np.float32) * 0.05)(128, 6 * 128) * 128 ** (-0.5))
    _d = {'L0_attn_hidden_states': _L0_attn_in['hidden_states'], 'L0_attn_Wq': _L0_attn_in['Wq'], 'L0_attn_bq': _L0_attn_in['bq'], 'L0_attn_Wk': _L0_attn_in['Wk'], 'L0_attn_bk': _L0_attn_in['bk'], 'L0_attn_Wv': _L0_attn_in['Wv'], 'L0_attn_bv': _L0_attn_in['bv'], 'L0_attn_Wo': _L0_attn_in['Wo'], 'L0_attn_bo': _L0_attn_in['bo'], 'L0_ffn_Wqkv': _L0_ffn_in['Wqkv'], 'L0_ffn_q_scale': _L0_ffn_in['q_scale'], 'L0_ffn_k_scale': _L0_ffn_in['k_scale'], 'L0_ffn_Wo': _L0_ffn_in['Wo'], 'L0_ffn_ln_g': _L0_ffn_in['ln_g'], 'L0_ffn_ln_b': _L0_ffn_in['ln_b'], 'L0_ffn_W1': _L0_ffn_in['W1'], 'L0_ffn_b1': _L0_ffn_in['b1'], 'L0_ffn_W2': _L0_ffn_in['W2'], 'L0_ffn_b2': _L0_ffn_in['b2'], 'L0_c': _L0_c, 'L0_wmod': _L0_wmod, 'L1_attn_in_proj_w': _L1_attn_in['in_proj_w'], 'L1_attn_conv_w': _L1_attn_in['conv_w'], 'L1_attn_conv_b': _L1_attn_in['conv_b'], 'L1_attn_x_proj_w': _L1_attn_in['x_proj_w'], 'L1_attn_dt_proj_w': _L1_attn_in['dt_proj_w'], 'L1_attn_dt_proj_b': _L1_attn_in['dt_proj_b'], 'L1_attn_A_log': _L1_attn_in['A_log'], 'L1_attn_D_param': _L1_attn_in['D_param'], 'L1_attn_out_proj_w': _L1_attn_in['out_proj_w'], 'L1_ffn_W': _L1_ffn_in['W'], 'L1_ffn_b': _L1_ffn_in['b'], 'L1_ffn_lora_down': _L1_ffn_in['lora_down'], 'L1_ffn_lora_up': _L1_ffn_in['lora_up'], 'L1_ffn_down_aux': _L1_ffn_in['down_aux'], 'L1_ffn_up_aux': _L1_ffn_in['up_aux'], 'L1_c': _L1_c, 'L1_wmod': _L1_wmod}
    _x0 = _d['L0_attn_hidden_states']
    _d['L0_attn_hidden_states'] = jax.random.normal(jax.random.fold_in(jax.random.key(seed), 1), (16, 256, 128), dtype=_x0.dtype)
    del _x0
    return _d

def reference(L0_attn_hidden_states, L0_attn_Wq, L0_attn_bq, L0_attn_Wk, L0_attn_bk, L0_attn_Wv, L0_attn_bv, L0_attn_Wo, L0_attn_bo, L0_ffn_Wqkv, L0_ffn_q_scale, L0_ffn_k_scale, L0_ffn_Wo, L0_ffn_ln_g, L0_ffn_ln_b, L0_ffn_W1, L0_ffn_b1, L0_ffn_W2, L0_ffn_b2, L0_c, L0_wmod, L1_attn_in_proj_w, L1_attn_conv_w, L1_attn_conv_b, L1_attn_x_proj_w, L1_attn_dt_proj_w, L1_attn_dt_proj_b, L1_attn_A_log, L1_attn_D_param, L1_attn_out_proj_w, L1_ffn_W, L1_ffn_b, L1_ffn_lora_down, L1_ffn_lora_up, L1_ffn_down_aux, L1_ffn_up_aux, L1_c, L1_wmod):

    def _L0_attn_ref(hidden_states, Wq, bq, Wk, bk, Wv, bv, Wo, bo):
        import jax, jax.numpy as jnp
        import numpy as np
        HIDDEN = 128
        HEADS = 16
        HEAD_DIM = HIDDEN // HEADS
        SCALE = HEAD_DIM ** (-0.5)
        b, s, d = hidden_states.shape
        q = (hidden_states @ Wq.T + bq).reshape(b, s, HEADS, HEAD_DIM)
        k = (hidden_states @ Wk.T + bk).reshape(b, s, HEADS, HEAD_DIM)
        v = (hidden_states @ Wv.T + bv).reshape(b, s, HEADS, HEAD_DIM)
        q = q * SCALE
        scores = jnp.einsum('bqhd,bkhd->bhqk', q, k)
        probs = jax.nn.softmax(scores.astype(jnp.float32), axis=-1).astype(scores.dtype)
        out = jnp.einsum('bhqk,bkhd->bqhd', probs, v).reshape(b, s, d)
        return out @ Wo.T + bo

    def _L0_ffn_ref(x, Wqkv, q_scale, k_scale, Wo, ln_g, ln_b, W1, b1, W2, b2):
        import jax, jax.numpy as jnp
        import numpy as np
        DIM = 128
        DEPTH = 6
        HEADS = 16
        DIM_HEAD = 64
        WINDOW = 32
        INNER = HEADS * DIM_HEAD
        DIM_INNER = int(DIM * 4 * 2 / 3)
        QK_SCALE = 8.0

        def shift_tokens(t):
            a, s = jnp.split(t, 2, -1)
            s = jnp.pad(s, ((0, 0), (1, 0), (0, 0)))[:, :-1]
            return jnp.concatenate([a, s], -1)

        def l2norm(t):
            return t / jnp.maximum(jnp.linalg.norm(t, axis=-1, keepdims=True), 1e-12)

        def rotate_half(x):
            x1, x2 = jnp.split(x, 2, -1)
            return jnp.concatenate([-x2, x1], -1)

        def rotary_tables(n):
            half = jnp.arange(0, DIM_HEAD, 2, dtype=jnp.float32)
            inv_freq = 1.0 / 10000.0 ** (half / DIM_HEAD)
            t = jnp.arange(n, dtype=jnp.float32)
            freqs = t[:, None] * inv_freq[None, :]
            freqs = jnp.concatenate([freqs, freqs], -1)
            base_scale = (half + 0.4 * DIM_HEAD) / (1.4 * DIM_HEAD)
            power = (t - n // 2) / (WINDOW // 2)
            scale = base_scale[None, :] ** power[:, None]
            scale = jnp.concatenate([scale, scale], -1)
            return (freqs, scale)

        def local_attention(q, k, v):
            b, h, n, d = q.shape
            w = WINDOW
            nw = n // w
            bq = q.reshape(b, h, nw, w, d)
            bk = k.reshape(b, h, nw, w, d)
            bv = v.reshape(b, h, nw, w, d)

            def look(t):
                p = jnp.pad(t, ((0, 0), (0, 0), (1, 0), (0, 0), (0, 0)))
                return jnp.concatenate([p[:, :, :nw], p[:, :, 1:]], axis=3)
            bk2, bv2 = (look(bk), look(bv))
            seq = jnp.arange(n).reshape(nw, w)
            seq_p = jnp.pad(seq, ((1, 0), (0, 0)), constant_values=-1)
            jt = jnp.concatenate([seq_p[:nw], seq_p[1:]], axis=1)
            it = seq[:, :, None]
            jb = jt[:, None, :]
            mask = (it < jb) | (it > jb + w) | (jb == -1)
            sim = jnp.einsum('bhwie,bhwje->bhwij', bq, bk2) * QK_SCALE
            sim = jnp.where(mask, -jnp.finfo(sim.dtype).max, sim)
            attn = jax.nn.softmax(sim, -1)
            out = jnp.einsum('bhwij,bhwje->bhwie', attn, bv2)
            return out.reshape(b, h, n, d)

        def attn_layer(x, Wqkv, qs, ksc, Wo):
            b, n, _ = x.shape
            qkv = x @ Wqkv
            q, k, v = jnp.split(qkv, 3, -1)
            sh = lambda t: t.reshape(b, n, HEADS, DIM_HEAD).transpose(0, 2, 1, 3)
            q, k, v = (sh(q), sh(k), sh(v))
            q = l2norm(q) * qs
            k = l2norm(k) * ksc
            freqs, scale = rotary_tables(n)
            cos, sin = (jnp.cos(freqs), jnp.sin(freqs))
            q = q * cos * scale + rotate_half(q) * sin * scale
            inv = 1.0 / scale
            k = k * cos * inv + rotate_half(k) * sin * inv
            out = local_attention(q, k, v)
            out = out.transpose(0, 2, 1, 3).reshape(b, n, INNER)
            return out @ Wo

        def ffn_layer(x, g, bln, W1, b1, W2, b2):
            mu = x.mean(-1, keepdims=True)
            var = ((x - mu) ** 2).mean(-1, keepdims=True)
            xn = (x - mu) / jnp.sqrt(var + 1e-05) * g + bln
            hg = xn @ W1 + b1
            a, gate = jnp.split(hg, 2, -1)
            return a * jax.nn.gelu(gate, approximate=False) @ W2 + b2
        for i in range(DEPTH):
            x = attn_layer(shift_tokens(x), Wqkv[i], q_scale[i], k_scale[i], Wo[i]) + x
            x = ffn_layer(shift_tokens(x), ln_g[i], ln_b[i], W1[i], b1[i], W2[i], b2[i]) + x
        return x

    def _L1_attn_ref(x, in_proj_w, conv_w, conv_b, x_proj_w, dt_proj_w, dt_proj_b, A_log, D_param, out_proj_w):
        import jax, jax.numpy as jnp
        import numpy as np
        DIM, D_INNER, D_STATE, DT_RANK, D_CONV = (128, 256, 16, 64, 4)
        BATCH, SEQ = (2, 128)

        def _silu(v):
            return v * jax.nn.sigmoid(v)

        def _ssm_forward(x, in_proj_w, conv_w, conv_b, x_proj_w, dt_proj_w, dt_proj_b, A_log, D_param, out_proj_w):
            b, l, _ = x.shape
            d_inner, d_conv = (conv_w.shape[0], conv_w.shape[2])
            dt_rank, n = (dt_proj_w.shape[0], A_log.shape[1])
            x_and_res = x @ in_proj_w
            xp, res = (x_and_res[..., :d_inner], x_and_res[..., d_inner:])
            h = jax.lax.conv_general_dilated(xp.transpose(0, 2, 1), conv_w, window_strides=(1,), padding=[(d_conv - 1, 0)], dimension_numbers=('NCH', 'OIH', 'NCH'), feature_group_count=d_inner) + conv_b[None, :, None]
            h = _silu(h.transpose(0, 2, 1))
            A = -jnp.exp(A_log)
            x_dbl = h @ x_proj_w
            dlt, Bm, Cm = (x_dbl[..., :dt_rank], x_dbl[..., dt_rank:dt_rank + n], x_dbl[..., dt_rank + n:])
            delta = jax.nn.softplus(dlt @ dt_proj_w + dt_proj_b)
            deltaA = jnp.exp(jnp.einsum('bld,dn->bldn', delta, A))
            deltaB_u = (delta * h)[..., None] * Bm[:, :, None, :]

            def step(state, t):
                dA_t, dBu_t, c_t = t
                state = dA_t * state + dBu_t
                y_t = jnp.einsum('bdn,bn->bd', state, c_t)
                return (state, y_t)
            init = jnp.zeros((b, d_inner, n), h.dtype)
            _, ys = jax.lax.scan(step, init, (deltaA.transpose(1, 0, 2, 3), deltaB_u.transpose(1, 0, 2, 3), Cm.transpose(1, 0, 2)))
            y = ys.transpose(1, 0, 2) + h * D_param
            y = y * _silu(res)
            return y @ out_proj_w
        return _ssm_forward(x, in_proj_w, conv_w, conv_b, x_proj_w, dt_proj_w, dt_proj_b, A_log, D_param, out_proj_w)

    def _L1_ffn_ref(hidden_states, W, b, lora_down, lora_up, down_aux, up_aux):
        import jax, jax.numpy as jnp
        import numpy as np
        ALPHA = 1.0
        lilora_weight = up_aux @ (lora_up @ (lora_down @ down_aux))
        base = jnp.einsum('bsi,oi->bso', hidden_states, W) + b
        delta = jnp.einsum('bsi,oi->bso', hidden_states, lilora_weight)
        return base + ALPHA * delta
    x = L0_attn_hidden_states
    mod = (_silu(L0_c) @ L0_wmod).reshape(L0_c.shape[0], 6, 1, -1)
    sa, ca, ga, sb, cb, gb = (mod[:, 0], mod[:, 1], mod[:, 2], mod[:, 3], mod[:, 4], mod[:, 5])
    ga = (2 * (ga >= 0) - 1) * jnp.maximum(jnp.abs(ga), 0.25)
    gb = (2 * (gb >= 0) - 1) * jnp.maximum(jnp.abs(gb), 0.25)
    h = _layernorm(x, axis=-1) * (1 + ca) + sa
    x = x + ga * _L0_attn_ref(h, L0_attn_Wq, L0_attn_bq, L0_attn_Wk, L0_attn_bk, L0_attn_Wv, L0_attn_bv, L0_attn_Wo, L0_attn_bo)
    h = _layernorm(x, axis=-1) * (1 + cb) + sb
    x = x + gb * _L0_ffn_ref(h, L0_ffn_Wqkv, L0_ffn_q_scale, L0_ffn_k_scale, L0_ffn_Wo, L0_ffn_ln_g, L0_ffn_ln_b, L0_ffn_W1, L0_ffn_b1, L0_ffn_W2, L0_ffn_b2)
    mod = (_silu(L1_c) @ L1_wmod).reshape(L1_c.shape[0], 6, 1, -1)
    sa, ca, ga, sb, cb, gb = (mod[:, 0], mod[:, 1], mod[:, 2], mod[:, 3], mod[:, 4], mod[:, 5])
    ga = (2 * (ga >= 0) - 1) * jnp.maximum(jnp.abs(ga), 0.25)
    gb = (2 * (gb >= 0) - 1) * jnp.maximum(jnp.abs(gb), 0.25)
    h = _layernorm(x, axis=-1) * (1 + ca) + sa
    x = x + ga * _L1_attn_ref(h, L1_attn_in_proj_w, L1_attn_conv_w, L1_attn_conv_b, L1_attn_x_proj_w, L1_attn_dt_proj_w, L1_attn_dt_proj_b, L1_attn_A_log, L1_attn_D_param, L1_attn_out_proj_w)
    h = _layernorm(x, axis=-1) * (1 + cb) + sb
    x = x + gb * _L1_ffn_ref(h, L1_ffn_W, L1_ffn_b, L1_ffn_lora_down, L1_ffn_lora_up, L1_ffn_down_aux, L1_ffn_up_aux)
    return x

_drawn_inputs = setup_inputs


def setup_inputs(seed=0):
    import zlib

    import numpy as np

    out = dict(_drawn_inputs(seed))
    spreads = {'L0_ffn_q_scale': (1.0, 0.2),
     'L0_ffn_k_scale': (1.0, 0.2),
     'L0_ffn_ln_g': (1.0, 0.2),
     'L0_ffn_ln_b': (0.0, 0.1),
     'L0_ffn_b1': (0.0, 0.1),
     'L0_ffn_b2': (0.0, 0.1),
     'L1_attn_D_param': (1.0, 0.2)}
    factors = {}
    for name, (base, spread) in spreads.items():
        noise = np.random.default_rng([zlib.crc32(name.encode()), seed]).standard_normal(out[name].shape)
        drawn = base * np.exp(spread * noise) if base else spread * noise
        out[name] = jnp.asarray(drawn.astype(out[name].dtype))
    for name, factor in factors.items():
        out[name] = (out[name] * factor).astype(out[name].dtype)
    return out
```

```python
from contextlib import ExitStack

import numpy as np

import concourse.bass as bass
from concourse import mybir

F32 = mybir.dt.float32
BF16 = mybir.dt.bfloat16
ALU = mybir.AluOpType
ACT = mybir.ActivationFunctionType
AX = mybir.AxisListType

P = 128
NB, NT = 16, 256
TT = NT // P
H0, D0 = 16, 8
HB, DB = 16, 64
INNER = HB * DB
WIN = 32
DEPTH = 6
FF = 341
FF_CHUNKS = [(0, 128), (128, 128), (256, FF - 256)]
NS, CH, RANK, TAPS = 16, 256, 64, 4
CC = CH // P
XD = RANK + 2 * NS
LN_EPS = 1e-5
KEYS = P + WIN
MASKED = -1e30


def wait(engine, semaphore, value):
    if isinstance(value, int) and value <= 0:
        return
    engine.wait_ge(semaphore, value)


class Store:

    def __init__(self, nc, stack, stage):
        self.nc, self.stack, self.stage = nc, stack, stage

    def sb(self, name, shape, dtype=F32):
        return self.stack.enter_context(self.nc.sbuf_tensor(f"{self.stage}_{name}", shape, dtype))

    def sems(self, names):
        return [self.stack.enter_context(self.nc.semaphore(f"{self.stage}_{name}")) for name in names.split()]


def flat(ap):
    return ap.rearrange("(c p) -> p c", p=P)




def setup(nc, g, d, ps):
    with ExitStack() as stack:
        s = Store(nc, stack, "setup")
        s.crow = s.sb("crow", [NB, 2, P]); s.sig = s.sb("sig", [NB, 2, P]); s.scT = s.sb("scT", [P, 2, NB])
        s.wmod = s.sb("wmod", [P, 2, 6 * P]); s.raw_w = s.sb("raw_w", [P, 4, P]); s.Wlin = s.sb("Wlin", [P, P])
        s.ga = s.sb("ga", [P, 2, NB, 2]); s.gb = s.sb("gb", [P, 2, NB, 2])
        s.qkscale = s.sb("qkscale", [P, 2, DEPTH, DB]); s.rot = s.sb("rot", [P, 4, TT, DB])
        s.lora_dn = s.sb("lora_dn", [4, 100]); s.dn_aux = s.sb("dn_aux", [100, P]); s.lora_up = s.sb("lora_up", [50, 4]); s.up_aux = s.sb("up_aux", [P, 50])
        s.dnT = s.sb("dnT", [100, 4]); s.upT = s.sb("upT", [4, 50]); s.uaT = s.sb("uaT", [50, P]); s.t1 = s.sb("t1", [4, P]); s.t2 = s.sb("t2", [50, P])
        s.alog = s.sb("alog", [P, CC, NS])
        s.loaded_a, s.loaded_b, s.consts, s.sig_exp, s.sig_done, s.scT_full, s.scT_done, s.mod_full = s.sems("loaded_a loaded_b consts sig_exp sig_done scT_full scT_done mod_full")
        s.mod_done, s.wt_full, s.wt_done, s.lora_full, s.lora_done, s.gstep, s.a_exp, s.chain = s.sems("mod_done wt_full wt_done lora_full lora_done gstep a_exp chain")
        block = stack.enter_context(nc.Block())
        n_a = 0

        @block.sync
        def _(sp):
            loads = [(g.ident[:], d["ident"]), (g.mask_f[:], d["mask"]), (s.crow[:, 0], d["L0_c"]), (s.crow[:, 1], d["L1_c"]),
                     (s.wmod[:, 0], d["L0_wmod"]), (s.wmod[:, 1], d["L1_wmod"])]
            loads += [(s.raw_w[:, i], w) for i, w in enumerate((d["L0_attn_Wq"], d["L0_attn_Wk"], d["L0_attn_Wv"], d["L0_attn_Wo"]))]
            loads += [(s.Wlin[:], d["L1_ffn_W"]), (s.rot[:], d["rot"]),
                      (s.lora_dn[:], d["L1_ffn_lora_down"]), (s.dn_aux[:], d["L1_ffn_down_aux"]),
                      (s.lora_up[:], d["L1_ffn_lora_up"]), (s.up_aux[:], d["L1_ffn_up_aux"])]
            for dst, src in loads:
                sp.dma_start(dst, src).then_inc(s.loaded_a, 16)
            sp.wait_ge(s.loaded_a, 16 * len(loads))

        small = [(s.alog[:], d["L1_attn_A_log"].rearrange("(c p) n -> p c n", p=P)),
                 (g.bv_row[:], d["L0_attn_bv"].rearrange("(a n) -> a n", a=1)),
                 (g.bo[:], flat(d["L0_attn_bo"])),
                 (g.lparam[:, :, 0], d["L0_ffn_ln_g"].rearrange("l p -> p l")), (g.lparam[:, :, 1], d["L0_ffn_ln_b"].rearrange("l p -> p l")),
                 (g.lparam[:, :, 2], d["L0_ffn_b2"].rearrange("l p -> p l")),
                 (g.conv_w[:], d["L1_attn_conv_w"].rearrange("(c p) o k -> p c (o k)", p=P)),
                 (g.conv_b[:], flat(d["L1_attn_conv_b"])), (g.dt_b[:], flat(d["L1_attn_dt_proj_b"])),
                 (g.D[:], flat(d["L1_attn_D_param"])), (g.blin[:], flat(d["L1_ffn_b"])),
                 (s.qkscale[:, 0], d["L0_ffn_q_scale"].rearrange("(a l) e -> a l e", a=1).broadcast_to((P, DEPTH, DB))),
                 (s.qkscale[:, 1], d["L0_ffn_k_scale"].rearrange("(a l) e -> a l e", a=1).broadcast_to((P, DEPTH, DB)))]
        for half in range(2):
            for c, (c0, w) in enumerate(FF_CHUNKS):
                small.append((g.lparam[0:w, :, 3 + 3 * half + c], d["L0_ffn_b1"][:, half * FF + c0:half * FF + c0 + w].rearrange("l p -> p l")))
        for j in range(4):
            for i, bvec in enumerate((d["L0_attn_bq"], d["L0_attn_bk"])):
                small.append((g.bqk[32 * j:32 * j + D0, i, :],
                              bvec.rearrange("(grp j e) -> j e grp", j=4, e=D0)[j]))

        @block.scalar
        def _(act):
            act.wait_ge(s.consts, 1)
            with nc.allow_non_contiguous_dma(reason="vectors laid along partitions, once"):
                for dst, src in small:
                    act.dma_start(dst, src).then_inc(s.loaded_b, 16)
            act.wait_ge(s.loaded_a, 16 * 16)
            nc.scalar.activation(s.sig[:], s.crow[:], ACT.Exp, scale=-1.0).then_inc(s.sig_exp, 1)
            act.wait_ge(s.loaded_b, 16 * len(small))
            nc.scalar.activation(g.A[:], s.alog[:], ACT.Exp).then_inc(s.a_exp, 1)
            act.wait_ge(s.mod_done, 1)
            nc.scalar.activation(s.ga[:], g.mod[:, :, :, 2:6:3], ACT.Abs).then_inc(s.gstep, 1)

        @block.gpsimd
        def _(pool):
            nc.gpsimd.memset(g.lparam[:], 0.0)
            nc.gpsimd.memset(g.bqk[:], 0.0).then_inc(s.consts, 1)

        @block.vector
        def _(dve):
            count = [0]

            def link(ins):
                count[0] += 1
                ins.then_inc(s.chain, 1)
                dve.wait_ge(s.chain, count[0])

            nc.vector.memset(g.ones_row[:], 1.0)
            nc.vector.memset(g.neg_half[:], -0.5)
            link(nc.vector.memset(g.wqk_pad[:], 0.0))
            dve.wait_ge(s.loaded_a, 16 * 16)
            nc.vector.tensor_copy(g.ident_bf[:], g.ident[:])
            nc.vector.tensor_copy(g.mask_bf[:], g.mask_f[:])
            dve.wait_ge(s.sig_exp, 1)
            link(nc.vector.tensor_scalar_add(s.sig[:], s.sig[:], 1.0))
            link(nc.vector.reciprocal(s.sig[:], s.sig[:]))
            nc.vector.tensor_tensor(s.sig[:], s.sig[:], s.crow[:], ALU.mult).then_inc(s.sig_done, 1)
            dve.wait_ge(s.wt_full, 1)
            for i in range(2):
                nc.vector.tensor_copy(g.wqk_pad[:, i].rearrange("p (h e) -> p h e", e=32)[:, :, 0:D0],
                                      ps[:, 1, i * P:(i + 1) * P].rearrange("p (h e) -> p h e", e=D0))
            nc.vector.tensor_copy(g.wvT[:], ps[:, 1, 2 * P:3 * P])
            nc.vector.tensor_copy(g.woT[:], ps[:, 1, 3 * P:4 * P])
            nc.vector.tensor_copy(s.dnT[:], ps[0:100, 2, 0:4])
            nc.vector.tensor_copy(s.upT[:], ps[0:4, 2, 128:178])
            nc.vector.tensor_copy(s.uaT[:], ps[0:50, 2, 256:384])
            nc.vector.tensor_copy(g.wlinT[:], ps[:, 2, 384:512]).then_inc(s.wt_done, 1)
            dve.wait_ge(s.lora_full, 1)
            nc.vector.tensor_copy(s.t1[:], ps[0:4, 3, 0:P]).then_inc(s.lora_done, 1)
            dve.wait_ge(s.lora_full, 2)
            nc.vector.tensor_copy(s.t2[:], ps[0:50, 4, 0:P]).then_inc(s.lora_done, 1)
            dve.wait_ge(s.lora_full, 3)
            nc.vector.tensor_tensor(g.wlinT[:], g.wlinT[:], ps[:, 5, 0:P], ALU.add)
            dve.wait_ge(s.scT_full, 1)
            nc.vector.tensor_copy(s.scT[:], ps[:, 0, 0:2 * NB].rearrange("p (l b) -> p l b", l=2)).then_inc(s.scT_done, 1)
            dve.wait_ge(s.mod_full, 1)
            nc.vector.tensor_copy(g.mod[:], ps[:, 6, 0:12 * NB].rearrange("p (l j b) -> p l b j", l=2, j=6)).then_inc(s.mod_done, 1)
            dve.wait_ge(s.gstep, 1)
            gates = g.mod[:, :, :, 2:6:3]
            nc.vector.tensor_scalar(s.gb[:], gates, 0.0, 2.0, ALU.is_ge, ALU.mult)
            link(nc.vector.tensor_scalar_max(s.ga[:], s.ga[:], 0.25))
            link(nc.vector.tensor_scalar_add(s.gb[:], s.gb[:], -1.0))
            link(nc.vector.tensor_tensor(gates, s.ga[:], s.gb[:], ALU.mult))
            scales = g.mod[:, :, :, 1:6:3]
            nc.vector.tensor_scalar_add(scales, scales, 1.0)
            dve.wait_ge(s.loaded_b, 16 * len(small))
            nc.vector.tensor_scalar_mul(g.bqk[:, 0], g.bqk[:, 0], float(D0) ** -0.5)
            for i in range(2):
                for tt in range(TT):
                    cos = s.rot[:, 2 * i:2 * i + 1, tt].broadcast_to((P, DEPTH, DB))
                    nc.vector.tensor_tensor(g.rotab[:, :, 2 * i, tt], s.qkscale[:, i], cos, ALU.mult)
                    for half in range(2):
                        a, b = half * (DB // 2), (1 - half) * (DB // 2)
                        sin = s.rot[:, 2 * i + 1:2 * i + 2, tt, a:a + DB // 2].broadcast_to((P, DEPTH, DB // 2))
                        nc.vector.tensor_tensor(g.rotab[:, :, 2 * i + 1, tt, a:a + DB // 2],
                                                s.qkscale[:, i, :, b:b + DB // 2], sin, ALU.mult)
            dve.wait_ge(s.a_exp, 1)
            nc.vector.tensor_scalar_mul(g.A[:], g.A[:], -1.0)

        @block.tensor
        def _(pe):
            pe.wait_ge(s.loaded_a, 16 * 16)
            for i in range(4):
                nc.tensor.transpose(ps[:, 1, i * P:(i + 1) * P], s.raw_w[:, i], g.ident[:])
            nc.tensor.transpose(ps[0:100, 2, 0:4], s.lora_dn[:], g.ident[0:4, 0:4])
            nc.tensor.transpose(ps[0:4, 2, 128:178], s.lora_up[:], g.ident[0:50, 0:50])
            nc.tensor.transpose(ps[0:50, 2, 256:384], s.up_aux[:], g.ident[:])
            nc.tensor.transpose(ps[:, 2, 384:512], s.Wlin[:], g.ident[:]).then_inc(s.wt_full, 1)
            pe.wait_ge(s.wt_done, 1)
            nc.tensor.matmul(ps[0:4, 3, 0:P], s.dnT[:], s.dn_aux[:], start=True, stop=True).then_inc(s.lora_full, 1)
            pe.wait_ge(s.lora_done, 1)
            nc.tensor.matmul(ps[0:50, 4, 0:P], s.upT[:], s.t1[:], start=True, stop=True).then_inc(s.lora_full, 1)
            pe.wait_ge(s.lora_done, 2)
            nc.tensor.matmul(ps[:, 5, 0:P], s.t2[:], s.uaT[:], start=True, stop=True).then_inc(s.lora_full, 1)
            pe.wait_ge(s.sig_done, 1)
            for l in range(2):
                last = nc.tensor.transpose(ps[:, 0, l * NB:(l + 1) * NB], s.sig[:, l], g.ident[0:NB, 0:NB])
            last.then_inc(s.scT_full, 1)
            pe.wait_ge(s.scT_done, 1)
            for l in range(2):
                for j in range(6):
                    k = (l * 6 + j) * NB
                    last = nc.tensor.matmul(ps[:, 6, k:k + NB], s.wmod[:, l, j * P:(j + 1) * P], s.scT[:, l],
                                            start=True, stop=True)
            last.then_inc(s.mod_full, 1)




class LayerNorm:

    def __init__(self, s, name):
        self.st = s.sb(name + "_st", [P, TT, 6])
        self.mv = s.sb(name + "_mv", [P, TT, 2])
        self.var = s.sb(name + "_var", [P, TT])
        self.rstd = s.sb(name + "_rstd", [P, TT])
        self.xn = s.sb(name + "_xn", [P, TT, P])
        self.stats, self.aggr, self.var_ready, self.rstd_ready, self.normed = s.sems(
            " ".join(f"{name}_{x}" for x in ("stats", "aggr", "var_ready", "rstd_ready", "normed")))


def layernorm_stats(nc, dve, ln, src, n):
    for tt in range(TT):
        last = nc.vector.bn_stats(ln.st[:, tt], src[:, tt])
    last.then_inc(ln.stats, 1)
    dve.wait_ge(ln.stats, n + 1)
    nc.vector.memset(ln.var[:], LN_EPS)
    for tt in range(TT):
        last = nc.vector.bn_aggr(ln.mv[:, tt], ln.st[:, tt])
    last.then_inc(ln.aggr, 1)
    dve.wait_ge(ln.aggr, n + 1)
    nc.vector.tensor_tensor(ln.var[:], ln.mv[:, :, 1], ln.var[:], ALU.add).then_inc(ln.var_ready, 1)


def layernorm_pool(nc, pool, ln, g, n):
    pool.wait_ge(ln.var_ready, n + 1)
    nc.gpsimd.tensor_tensor(ln.rstd[:], ln.var[:], g.neg_half[:, 0:TT], ALU.pow).then_inc(ln.rstd_ready, 1)


def layernorm_apply(nc, dve, ln, src, n):
    dve.wait_ge(ln.rstd_ready, n + 1)
    for tt in range(TT):
        last = nc.vector.tensor_scalar(ln.xn[:, tt], src[:, tt], ln.mv[:, tt, 0:1], ln.rstd[:, tt:tt + 1], ALU.subtract, ALU.mult)
    last.then_inc(ln.normed, 1)




def phase_a(nc, g, d, ps):
    with ExitStack() as stack:
        s = Store(nc, stack, "a")
        s.xtok = s.sb("xtok", [P, TT, P]); s.xTs = s.sb("xTs", [P, NT]); s.hT = s.sb("hT", [P, NT]); s.md = s.sb("md", [P, 6])
        s.qT = s.sb("qT", [P, 4, NT]); s.kT = s.sb("kT", [P, 4, NT]); s.V = s.sb("V", [P, TT, P])
        s.nm = s.sb("nm", [P, H0, TT]); s.ssum = s.sb("ssum", [P, H0, TT]); s.rinv = s.sb("rinv", [P, H0, TT])
        s.Pr = s.sb("Pr", [P, 3, TT, NT]); s.PT = s.sb("PT", [P, 2, TT, NT])
        s.o = s.sb("o", [P, TT, H0, D0]); s.oT = s.sb("oT", [P, NT]); s.tmp = s.sb("tmp", [P, NT]); s.x2s = s.sb("x2s", [P, NT]); s.x2tok = s.sb("x2tok", [P, TT, P])
        s.l1 = LayerNorm(s, "l1"); s.l2 = LayerNorm(s, "l2")
        s.x_in, s.md_ready, s.hx_full, s.xT_done, s.hT_ready, s.qk_full, s.qk_ready, s.v_full = s.sems("x_in md_ready hx_full xT_done hT_ready qk_full qk_ready v_full")
        s.v_ready, s.s_done, s.max_done, s.exp_done, s.t_done, s.pt_ready, s.pv_done, s.rinv_ready = s.sems("v_ready s_done max_done exp_done t_done pt_ready pv_done rinv_ready")
        s.o_ready, s.oT_full, s.oT_ready, s.proj_full, s.tmp_ready, s.x2s_ready, s.x2_full, s.x2tok_ready = s.sems("o_ready oT_full oT_ready proj_full tmp_ready x2s_ready x2_full x2tok_ready")
        s.h2_full, s.seq_done, s.x2_kept = s.sems("h2_full seq_done x2_kept")
        block = stack.enter_context(nc.Block())
        S_BANK, PT_BANK, QK_BANK = (1, 2, 3), (4, 5), (7, 4)

        @block.sync
        def _(sp):
            sp.dma_start(s.xtok[:], d["L0_attn_hidden_states"][0].rearrange("(t p) e -> p t e", p=P)).then_inc(s.x_in, 16)
            with sp.Fori(1, NB) as n:
                sp.wait_ge(s.xT_done, n)
                sp.wait_ge(s.l1.normed, n)
                sp.dma_start(s.xtok[:], d["L0_attn_hidden_states"][bass.ds(n, 1)].rearrange("b (t p) e -> p (b t) e", p=P)).then_inc(s.x_in, 16)

        @block.vector
        def _(dve):
            with dve.Fori(0, NB) as n:
                dve.wait_ge(s.seq_done, n + 1)
                nc.vector.tensor_scalar_mul(s.md[:], g.mod[:, 0, bass.ds(n, 1), :].rearrange("p a k -> p (a k)"), 1.0).then_inc(s.md_ready, 1)
                dve.wait_ge(s.x_in, 16 * n + 16)
                layernorm_stats(nc, dve, s.l1, s.xtok, n)
                layernorm_apply(nc, dve, s.l1, s.xtok, n)
                dve.wait_ge(s.hx_full, n + 1)
                nc.vector.tensor_copy(s.xTs[:], ps[:, 0, NT:2 * NT]).then_inc(s.xT_done, 1)
                dve.wait_ge(s.v_full, n + 1)
                nc.vector.tensor_copy(s.V[:], ps[:, 5, 0:NT].rearrange("p (t e) -> p t e", t=TT)).then_inc(s.v_ready, 1)
                for h in range(H0 + 1):
                    if h < H0:
                        dve.wait_ge(s.s_done, H0 * n + h + 1)
                        nc.vector.tensor_reduce(s.nm[:, h], ps[:, S_BANK[h % 3]].rearrange("p (t k) -> p t k", t=TT),
                                                AX.X, ALU.max, negate=True).then_inc(s.max_done, 1)
                    if h >= 1:
                        k = h - 1
                        dve.wait_ge(s.t_done, H0 * n + k + 1)
                        if k >= 2:
                            dve.wait_ge(s.pv_done, H0 * n + k - 1)
                        nc.vector.tensor_copy(s.PT[:, k % 2], ps[:, PT_BANK[k % 2]].rearrange("p (t k) -> p t k", t=TT)).then_inc(s.pt_ready, 1)
                nc.vector.reciprocal(s.rinv[:], s.ssum[:]).then_inc(s.rinv_ready, 1)
                dve.wait_ge(s.rinv_ready, n + 1)
                dve.wait_ge(s.pv_done, H0 * n + H0)
                for tt in range(TT):
                    last = nc.vector.tensor_tensor(s.o[:, tt], ps[:, 6, tt * P:(tt + 1) * P].rearrange("p (h e) -> p h e", e=D0),
                                                   s.rinv[:, :, tt:tt + 1].broadcast_to((P, H0, D0)), ALU.mult)
                last.then_inc(s.o_ready, 1)
                dve.wait_ge(s.proj_full, n + 1)
                nc.vector.tensor_scalar(s.tmp[:], ps[:, 7, 0:NT], g.bo[:], s.md[:, 2:3], ALU.add, ALU.mult).then_inc(s.tmp_ready, 1)
                dve.wait_ge(s.tmp_ready, n + 1)
                nc.vector.tensor_tensor(s.x2s[:], s.tmp[:], s.xTs[:], ALU.add).then_inc(s.x2s_ready, 1)
                dve.wait_ge(s.x2_full, n + 1)
                nc.vector.tensor_copy(s.x2tok[:], ps[:, 0, 0:NT].rearrange("p (t e) -> p t e", t=TT)).then_inc(s.x2tok_ready, 1)
                dve.wait_ge(s.x2tok_ready, n + 1)
                layernorm_stats(nc, dve, s.l2, s.x2tok, n)
                layernorm_apply(nc, dve, s.l2, s.x2tok, n)

        @block.gpsimd
        def _(pool):
            with pool.Fori(0, NB) as n:
                layernorm_pool(nc, pool, s.l1, g, n)
                pool.wait_ge(s.x2s_ready, n + 1)
                nc.gpsimd.tensor_copy(g.x2T[:, bass.ds(n * NT, NT)], s.x2s[:]).then_inc(s.x2_kept, 1)
                layernorm_pool(nc, pool, s.l2, g, n)

        @block.scalar
        def _(act):
            act.sem_inc(s.seq_done, 1)
            with act.Fori(0, NB) as n:
                act.wait_ge(s.xT_done, n + 1)
                act.wait_ge(s.md_ready, n + 1)
                nc.scalar.activation(s.hT[:], ps[:, 0, 0:NT], ACT.Identity, bias=s.md[:, 0:1], scale=s.md[:, 1:2]).then_inc(s.hT_ready, 1)
                for grp in range(4):
                    act.wait_ge(s.qk_full, 4 * n + grp + 1)
                    bank = QK_BANK[grp % 2]
                    nc.scalar.activation(s.qT[:, grp], ps[:, bank, 0:NT], ACT.Identity, bias=g.bqk[:, 0, grp:grp + 1], scale=float(D0) ** -0.5)
                    nc.scalar.activation(s.kT[:, grp], ps[:, bank, NT:2 * NT], ACT.Identity, bias=g.bqk[:, 1, grp:grp + 1]).then_inc(s.qk_ready, 1)
                for h in range(H0):
                    act.wait_ge(s.max_done, H0 * n + h + 1)
                    if h >= 3:
                        act.wait_ge(s.t_done, H0 * n + h - 2)
                    for tt in range(TT):
                        last = nc.scalar.activation(s.Pr[:, h % 3, tt], ps[:, S_BANK[h % 3], tt * NT:(tt + 1) * NT], ACT.Exp,
                                                    bias=s.nm[:, h, tt:tt + 1], accum_out=s.ssum[:, h, tt:tt + 1])
                    last.then_inc(s.exp_done, 1)
                act.wait_ge(s.oT_full, n + 1)
                nc.scalar.activation(s.oT[:], ps[:, 0, 0:NT], ACT.Copy).then_inc(s.oT_ready, 1)
                act.wait_ge(s.h2_full, n + 1)
                nc.scalar.activation(g.xT[:, bass.ds(n * NT, NT)], ps[:, 0, NT:2 * NT], ACT.Identity,
                                     bias=s.md[:, 3:4], scale=s.md[:, 4:5]).then_inc(s.seq_done, 1)

        @block.tensor
        def _(pe):
            with pe.Fori(0, NB) as n:
                pe.wait_ge(s.l1.normed, n + 1)
                for tt in range(TT):
                    nc.tensor.transpose(ps[:, 0, tt * P:(tt + 1) * P], s.l1.xn[:, tt], g.ident[:])
                    last = nc.tensor.transpose(ps[:, 0, NT + tt * P:NT + (tt + 1) * P], s.xtok[:, tt], g.ident[:])
                last.then_inc(s.hx_full, 1)
                pe.wait_ge(s.hT_ready, n + 1)
                for grp in range(4):
                    if grp >= 2:
                        pe.wait_ge(s.qk_ready, 4 * n + grp - 1)
                    for i in range(2):
                        last = nc.tensor.matmul(ps[:, QK_BANK[grp % 2], i * NT:(i + 1) * NT], g.wqk_pad[:, i, grp * P:(grp + 1) * P],
                                                s.hT[:], start=True, stop=True)
                    last.then_inc(s.qk_full, 1)
                for tt in range(TT):
                    nc.tensor.matmul(ps[:, 5, tt * P:(tt + 1) * P], g.ones_row[:], g.bv_row[:], start=True, stop=False)
                    last = nc.tensor.matmul(ps[:, 5, tt * P:(tt + 1) * P], s.hT[:, tt * P:(tt + 1) * P], g.wvT[:], start=False, stop=True)
                last.then_inc(s.v_full, 1)
                for h in range(H0 + 2):
                    if h < H0:
                        grp, r = h // 4, 32 * (h % 4)
                        pe.wait_ge(s.qk_ready, 4 * n + grp + 1)
                        if h >= 3:
                            pe.wait_ge(s.exp_done, H0 * n + h - 2)
                        for tt in range(TT):
                            last = nc.tensor.matmul(ps[:, S_BANK[h % 3], tt * NT:(tt + 1) * NT], s.qT[r:r + 32, grp, tt * P:(tt + 1) * P],
                                                    s.kT[r:r + 32, grp], start=True, stop=True)
                        last.then_inc(s.s_done, 1)
                    if 1 <= h <= H0:
                        k = h - 1
                        pe.wait_ge(s.exp_done, H0 * n + k + 1)
                        if k < 2:
                            pe.wait_ge(s.v_ready, n + 1)
                            pe.wait_ge(s.qk_ready, 4 * n + 4)
                        else:
                            pe.wait_ge(s.pt_ready, H0 * n + k - 1)
                        for kb in range(TT):
                            for tt in range(TT):
                                last = nc.tensor.transpose(ps[:, PT_BANK[k % 2], kb * NT + tt * P:kb * NT + (tt + 1) * P],
                                                           s.Pr[:, k % 3, tt, kb * P:(kb + 1) * P], g.ident[:])
                        last.then_inc(s.t_done, 1)
                    if h >= 2:
                        k = h - 2
                        pe.wait_ge(s.pt_ready, H0 * n + k + 1)
                        for tt in range(TT):
                            for kb in range(TT):
                                c = tt * P + k * D0
                                last = nc.tensor.matmul(ps[:, 6, c:c + D0], s.PT[:, k % 2, kb, tt * P:(tt + 1) * P],
                                                        s.V[:, kb, k * D0:(k + 1) * D0], start=kb == 0, stop=kb == TT - 1)
                        last.then_inc(s.pv_done, 1)
                pe.wait_ge(s.o_ready, n + 1)
                for tt in range(TT):
                    last = nc.tensor.transpose(ps[:, 0, tt * P:(tt + 1) * P], s.o[:, tt].rearrange("p h e -> p (h e)"), g.ident[:])
                last.then_inc(s.oT_full, 1)
                pe.wait_ge(s.oT_ready, n + 1)
                nc.tensor.matmul(ps[:, 7, 0:NT], g.woT[:], s.oT[:], start=True, stop=True).then_inc(s.proj_full, 1)
                pe.wait_ge(s.x2s_ready, n + 1)
                for tt in range(TT):
                    last = nc.tensor.transpose(ps[:, 0, tt * P:(tt + 1) * P], s.x2s[:, tt * P:(tt + 1) * P], g.ident[:])
                last.then_inc(s.x2_full, 1)
                pe.wait_ge(s.l2.normed, n + 1)
                for tt in range(TT):
                    last = nc.tensor.transpose(ps[:, 0, NT + tt * P:NT + (tt + 1) * P], s.l2.xn[:, tt], g.ident[:])
                last.then_inc(s.h2_full, 1)



ITEMS = DEPTH * NB
SLOTS = HB + 3
PIECES = 6 * TT
QK_PIECES = 4 * TT
NORM_SLOT = {6: 0, 13: 1}
TRANSPOSE_SLOT = {7: 0, 8: 1, 9: 2, 10: 3, 14: 4, 16: 5, 17: 6, 18: 7}
POWER_SLOT = {3: 0, 9: 1}
OUT_SLOT = {0: 0, 1: 1, 2: 2, 3: 3}
WO_SLOT, RES_SLOT, XT_SLOT, STATS_SLOT, NORMED_SLOT, XN_SLOT = 4, 5, 6, 7, 8, 9
W1_SLOT = {10: 0, 11: 1, 12: 2}
GELU_SLOT, W2_SLOT, END_SLOT = 13, 15, 16


def spare_uses(front, tail):
    uses = []
    for slot in range(SLOTS):
        if tail:
            if slot in OUT_SLOT:
                uses.append(("out", OUT_SLOT[slot]))
            for at, kind in ((WO_SLOT, "wo"), (XT_SLOT, "xt"), (XN_SLOT, "xn"), (W2_SLOT, "w2")):
                if slot == at:
                    uses.append((kind, 0))
            if slot in W1_SLOT:
                uses.append(("w1", W1_SLOT[slot]))
        if front and slot in TRANSPOSE_SLOT:
            uses.append(("tr", TRANSPOSE_SLOT[slot]))
    return uses


def spare_base(n):
    only_front, both, only_tail = (len(spare_uses(*x)) for x in ((True, False), (True, True), (False, True)))
    if isinstance(n, int) and n <= 0:
        return only_front * (n + 1)
    if isinstance(n, int) and n == ITEMS:
        return 2 * only_front + both * (ITEMS - 2) + only_tail
    return 2 * only_front + both * (n - 1)


def phase_b(nc, g, d, ps):
    with ExitStack() as stack:
        s = Store(nc, stack, "b")
        s.Wqkv = s.sb("Wqkv", [P, 3 * INNER]); s.Wo = s.sb("Wo", [P, INNER // P, P]); s.W1 = s.sb("W1", [P, 2 * FF]); s.W2 = s.sb("W2", [P, 3, P])
        s.xs = s.sb("xs", [P, 2, NT])
        s.w = s.sb("w", [P, TT, 2 * INNER])
        s.vt = s.sb("vt", [P, 2, 512]); s.sq = s.sb("sq", [P, 2, 512])
        s.ss = s.sb("ss", [P, TT, 2 * HB]); s.ssm = s.sb("ssm", [P, TT, 2 * HB]); s.rn = s.sb("rn", [P, TT, 2 * HB])
        s.qkT = s.sb("qkT", [P, 2, 2 * INNER // P, NT])
        s.V = s.sb("V", [P, 2, TT, INNER])
        s.nm = s.sb("nm", [P, HB, TT]); s.ssum = s.sb("ssum", [P, HB, TT]); s.rinv = s.sb("rinv", [P, HB, TT])
        s.Pr = s.sb("Pr", [P, 4, 3 * P])
        s.PT = s.sb("PT", [P, 3, 2 * P + WIN])
        s.o = s.sb("o", [P, TT, INNER]); s.oT = s.sb("oT", [P, INNER // P, NT])
        s.lp = s.sb("lp", [P, 9]); s.xs2 = s.sb("xs2", [P, NT]); s.xtok = s.sb("xtok", [P, TT, P]); s.xnT = s.sb("xnT", [P, NT])
        s.ha = s.sb("ha", [P, 3, NT]); s.hgate = s.sb("hgate", [P, 3, NT]); s.gl = s.sb("gl", [P, 3, NT]); s.hg = s.sb("hg", [P, 3, NT])
        s.ff = LayerNorm(s, "ff")
        s.zeroed, s.wqkv_in, s.wo_in, s.w12_in, s.xs_ready, s.proj_done, s.act_front, s.dve_uv = s.sems("zeroed wqkv_in wo_in w12_in xs_ready proj_done act_front dve_uv")
        s.dve_red, s.pool_add, s.clamp_done, s.pool_r, s.dve_norm, s.spare_full, s.spare_free, s.s_done = s.sems("dve_red pool_add clamp_done pool_r dve_norm spare_full spare_free s_done")
        s.max_done, s.exp_done, s.t_done, s.pt_ready, s.pv_done, s.rinv_ready, s.onorm, s.lp_ready = s.sems("max_done exp_done t_done pt_ready pv_done rinv_ready onorm lp_ready")
        s.res_done, s.shifted, s.xtok_ready, s.gelu_done, s.hg_ready, s.x_ready = s.sems("res_done shifted xtok_ready gelu_done hg_ready x_ready")
        block = stack.enter_context(nc.Block())
        S_BANK, F_BANK, T_BANK, PV_BANK, SPARE = (0, 1, 2), (3, 4), 5, 6, 7
        ONE = slice(3 * P - KEYS, 3 * P)

        def program(engine, body):
            body(-1, 1, True, False, False)
            body(0, 0, True, True, False)
            with engine.Fori(0, (ITEMS - 2) // 2) as pair:
                body(2 * pair + 1, 1, True, True, True)
                body(2 * pair + 2, 0, True, True, True)
            body(ITEMS - 1, 1, False, True, True)
            body(ITEMS, 0, False, False, True)

        def spare_index(n, front, tail):
            base = spare_base(n)
            return {use: base + i for i, use in enumerate(spare_uses(front, tail))}

        def qk_count(j):
            return j // 6 * 4 + min(j % 6, 4)

        @block.sync
        def _(sp):
            def load_qkv(l):
                sp.dma_start(s.Wqkv[:], d["L0_ffn_Wqkv"][l]).then_inc(s.wqkv_in, 16)

            def load_rest(l):
                sp.dma_start(s.Wo[:], d["L0_ffn_Wo"][l].rearrange("(c p) n -> p c n", p=P)).then_inc(s.wo_in, 16)
                sp.dma_start(s.W1[:], d["L0_ffn_W1"][l]).then_inc(s.w12_in, 16)
                sp.dma_start(s.W2[:, 0:2], d["L0_ffn_W2"][l, 0:2 * P].rearrange("(c p) n -> p c n", p=P)).then_inc(s.w12_in, 16)
                sp.dma_start(s.W2[0:FF - 2 * P, 2], d["L0_ffn_W2"][l, 2 * P:FF]).then_inc(s.w12_in, 16)

            load_qkv(0)
            load_rest(0)
            for l in range(1, DEPTH):
                sp.wait_ge(s.proj_done, PIECES * NB * l)
                load_qkv(l)
                sp.wait_ge(s.x_ready, NB * l + NB)
                load_rest(l)
            sp.wait_ge(s.wqkv_in, 16 * DEPTH)
            sp.wait_ge(s.wo_in, 16 * DEPTH)
            sp.wait_ge(s.w12_in, 48 * DEPTH)

        @block.tensor
        def _(pe):
            def body(n, odd, front, attn, tail):
                f, a, t = n + 1, n, n - 1
                pf, pa = 1 - odd, odd
                spare = spare_index(n, front, tail)

                def take_spare(use):
                    wait(pe, s.spare_free, spare[use])

                for slot in range(SLOTS):
                    if attn and slot < HB:
                        h = slot
                        bank, r, pair = S_BANK[h % 3], DB * (h % 2), h // 2
                        if h == 0:
                            pe.wait_ge(s.spare_free, spare_base(n))
                        wait(pe, s.exp_done, HB * a + h - 2)
                        q, k = s.qkT[r:r + DB, pa, pair], s.qkT[r:r + DB, pa, INNER // P + pair]
                        nc.tensor.matmul(ps[:, bank, 0:TT * KEYS], g.ident_bf[:], g.mask_bf[:], start=True, stop=False, skip_group_check=True)
                        nc.tensor.matmul(ps[:, bank, WIN:KEYS], q[:, 0:P], k[:, 0:P], start=False, stop=False, skip_group_check=True)
                        nc.tensor.matmul(ps[:, bank, KEYS:2 * KEYS], q[:, P:NT], k[:, P - WIN:NT], start=False, stop=True,
                                         skip_group_check=True).then_inc(s.s_done, 1)
                    if front and slot < PIECES:
                        j, tt, c = slot, slot // 6, slot % 6
                        if j == 0:
                            pe.wait_ge(s.xs_ready, f + 1)
                            pe.wait_ge(s.wqkv_in, 16 * (f // NB) + 16)
                        wait(pe, s.act_front, PIECES * f + j - 1)
                        if j >= 2:
                            wait(pe, s.dve_uv, QK_PIECES * f + qk_count(j - 1))
                        nc.tensor.matmul(ps[:, F_BANK[j % 2]], s.xs[:, pf, tt * P:(tt + 1) * P], s.Wqkv[:, c * 512:(c + 1) * 512],
                                         start=True, stop=True).then_inc(s.proj_done, 1)
                    if attn and 2 <= slot < HB + 2:
                        k = slot - 2
                        pe.wait_ge(s.exp_done, HB * a + k + 1)
                        wait(pe, s.pt_ready, HB * a + k)
                        for i, c in enumerate((0, 2, 1)):
                            last = nc.tensor.transpose(ps[:, T_BANK, i * P:(i + 1) * P], s.Pr[:, k % 4, c * P:(c + 1) * P], g.ident[:])
                        last.then_inc(s.t_done, 1)
                    if tail:
                        if slot in OUT_SLOT:
                            i = OUT_SLOT[slot]
                            if i == 0:
                                pe.wait_ge(s.onorm, 4 * t + 4)
                            take_spare(("out", i))
                            for k in range(4):
                                c = i % 2 * 4 + k
                                last = nc.tensor.transpose(ps[:, SPARE, k * P:(k + 1) * P], s.o[:, i // 2, c * P:(c + 1) * P], g.ident[:])
                            last.then_inc(s.spare_full, 1)
                        if slot == WO_SLOT:
                            take_spare(("wo", 0))
                            pe.wait_ge(s.wo_in, 16 * (t // NB) + 16)
                            for c in range(INNER // P):
                                last = nc.tensor.matmul(ps[:, SPARE, 0:NT], s.Wo[:, c], s.oT[:, c], start=c == 0, stop=c == INNER // P - 1)
                            last.then_inc(s.spare_full, 1)
                        if slot == XT_SLOT:
                            take_spare(("xt", 0))
                            pe.wait_ge(s.shifted, t + 1)
                            for tt in range(TT):
                                last = nc.tensor.transpose(ps[:, SPARE, tt * P:(tt + 1) * P], s.xs2[:, tt * P:(tt + 1) * P], g.ident[:])
                            last.then_inc(s.spare_full, 1)
                        if slot == XN_SLOT:
                            take_spare(("xn", 0))
                            pe.wait_ge(s.ff.normed, t + 1)
                            for tt in range(TT):
                                last = nc.tensor.transpose(ps[:, SPARE, tt * P:(tt + 1) * P], s.ff.xn[:, tt], g.ident[:])
                            last.then_inc(s.spare_full, 1)
                        if slot in W1_SLOT:
                            c = W1_SLOT[slot]
                            c0, width = FF_CHUNKS[c]
                            take_spare(("w1", c))
                            if c == 0:
                                pe.wait_ge(s.w12_in, 48 * (t // NB) + 48)
                            for half in range(2):
                                last = nc.tensor.matmul(ps[0:width, SPARE, half * NT:(half + 1) * NT],
                                                        s.W1[:, half * FF + c0:half * FF + c0 + width], s.xnT[:], start=True, stop=True)
                            last.then_inc(s.spare_full, 1)
                        if slot == W2_SLOT:
                            take_spare(("w2", 0))
                            pe.wait_ge(s.hg_ready, t + 1)
                            for c, (_, width) in enumerate(FF_CHUNKS):
                                last = nc.tensor.matmul(ps[:, SPARE, 0:NT], s.W2[0:width, c], s.hg[0:width, c], start=c == 0, stop=c == 2)
                            last.then_inc(s.spare_full, 1)
                    if attn and slot >= 3:
                        k = slot - 3
                        pe.wait_ge(s.pt_ready, HB * a + k + 1)
                        if k == 0:
                            pe.wait_ge(s.act_front, PIECES * a + PIECES)
                        if k % 4 == 0:
                            wait(pe, s.onorm, 4 * a + k // 4)
                        pt, v, col = s.PT[:, k % 3], s.V[:, pa], k * DB
                        out = ps[:, PV_BANK].rearrange("p (h t e) -> p h t e", h=4, t=TT)[:, k % 4]
                        nc.tensor.matmul(out[:, 0], pt[:, 0:P], v[:, 0, col:col + DB], start=True, stop=True)
                        nc.tensor.matmul(out[:, 1], pt[:, P:2 * P], v[:, 1, col:col + DB], start=True, stop=False, skip_group_check=True)
                        nc.tensor.matmul(out[0:WIN, 1], pt[:, 2 * P:2 * P + WIN], v[:, 0, col:col + DB], start=False, stop=True,
                                         skip_group_check=True).then_inc(s.pv_done, 1)
                    if front and slot in TRANSPOSE_SLOT:
                        i = TRANSPOSE_SLOT[slot]
                        tt, grp = i // 4, i % 4
                        take_spare(("tr", i))
                        pe.wait_ge(s.dve_norm, TT * f + tt + 1)
                        for k in range(4):
                            c = grp * 4 + k
                            last = nc.tensor.transpose(ps[:, SPARE, k * P:(k + 1) * P], s.w[:, tt, c * P:(c + 1) * P], g.ident[:])
                        last.then_inc(s.spare_full, 1)

            program(pe, body)

        @block.scalar
        def _(act):
            act.wait_ge(s.zeroed, 1)

            def body(n, odd, front, attn, tail):
                f, a, t = n + 1, n, n - 1
                pf = 1 - odd
                spare = spare_index(n, front, tail)
                for slot in range(SLOTS):
                    if front and slot < PIECES:
                        j, tt, c = slot, slot // 6, slot % 6
                        act.wait_ge(s.proj_done, PIECES * f + j + 1)
                        if c < 4:
                            jq = 4 * tt + c
                            wait(act, s.dve_red, QK_PIECES * f + jq - 1)
                            nc.scalar.activation(s.sq[:, jq % 2], ps[:, F_BANK[j % 2]], ACT.Square).then_inc(s.act_front, 1)
                        else:
                            if j == 4:
                                wait(act, s.pv_done, HB * (f - 1))
                            nc.scalar.activation(s.V[:, pf, tt, (c - 4) * 512:(c - 3) * 512], ps[:, F_BANK[j % 2]],
                                                 ACT.Copy).then_inc(s.act_front, 1)
                    if attn and 2 <= slot < HB + 2:
                        k = slot - 2
                        act.wait_ge(s.t_done, HB * a + k + 1)
                        wait(act, s.pv_done, HB * a + k - 2)
                        nc.scalar.activation(s.PT[:, k % 3], ps[:, T_BANK, 0:2 * P + WIN], ACT.Copy).then_inc(s.pt_ready, 1)
                    if attn and slot < HB:
                        h = slot
                        bank = S_BANK[h % 3]
                        act.wait_ge(s.max_done, HB * a + h + 1)
                        wait(act, s.t_done, HB * a + h - 3)
                        nc.scalar.activation(s.Pr[:, h % 4, 0:P], ps[:, bank, WIN:KEYS], ACT.Exp,
                                             bias=s.nm[:, h, 0:1], accum_out=s.ssum[:, h, 0:1])
                        nc.scalar.activation(s.Pr[:, h % 4, ONE], ps[:, bank, KEYS:2 * KEYS], ACT.Exp,
                                             bias=s.nm[:, h, 1:2], accum_out=s.ssum[:, h, 1:2]).then_inc(s.exp_done, 1)
                    if tail:
                        if slot in OUT_SLOT:
                            i = OUT_SLOT[slot]
                            act.wait_ge(s.spare_full, spare[("out", i)] + 1)
                            nc.scalar.activation(s.oT[:, i % 2 * 4:i % 2 * 4 + 4, i // 2 * P:(i // 2 + 1) * P],
                                                 ps[:, SPARE].rearrange("p (c t) -> p c t", c=4), ACT.Copy).then_inc(s.spare_free, 1)
                        if slot == XN_SLOT:
                            act.wait_ge(s.spare_full, spare[("xn", 0)] + 1)
                            act.wait_ge(s.lp_ready, t + 1)
                            nc.scalar.activation(s.xnT[:], ps[:, SPARE, 0:NT], ACT.Identity, bias=s.lp[:, 1:2],
                                                 scale=s.lp[:, 0:1]).then_inc(s.spare_free, 1)
                        if slot == GELU_SLOT:
                            act.wait_ge(s.spare_free, spare[("w1", 2)] + 1)
                            nc.scalar.activation(s.gl[:], s.hgate[:], ACT.Gelu).then_inc(s.gelu_done, 1)
                    if front and slot in TRANSPOSE_SLOT:
                        i = TRANSPOSE_SLOT[slot]
                        tt, grp = i // 4, i % 4
                        act.wait_ge(s.spare_full, spare[("tr", i)] + 1)
                        if i == 0:
                            wait(act, s.s_done, HB * (f - 1))
                        nc.scalar.activation(s.qkT[:, pf, grp * 4:grp * 4 + 4, tt * P:(tt + 1) * P],
                                             ps[:, SPARE].rearrange("p (c t) -> p c t", c=4), ACT.Copy).then_inc(s.spare_free, 1)

            program(act, body)

        @block.vector
        def _(dve):
            for buffer in (s.Pr, s.xs, s.xs2, s.ha):
                nc.vector.memset(buffer[:], 0.0)
            nc.vector.memset(s.hgate[:], 0.0).then_inc(s.zeroed, 1)
            dve.wait_ge(s.zeroed, 1)
            dve.sem_inc(s.x_ready, NB)
            lower, upper = slice(0, P // 2), slice(P // 2, P)

            def body(n, odd, front, attn, tail):
                f, a, t = n + 1, n, n - 1
                pf = 1 - odd
                spare = spare_index(n, front, tail)
                if front:
                    src, lf = (f % NB) * NT, f // NB
                    if not isinstance(n, int):
                        src, lf = dve.snap(src), dve.snap(lf)
                    dve.wait_ge(s.x_ready, f + 1)
                    wait(dve, s.proj_done, PIECES * (f - 1))
                    nc.vector.tensor_scalar_mul(s.xs[lower, pf], g.xT[lower, bass.ds(src, NT)], 1.0)
                    nc.vector.tensor_scalar_mul(s.xs[upper, pf, 1:NT], g.xT[upper, bass.ds(src, NT - 1)], 1.0).then_inc(s.xs_ready, 1)
                if tail:
                    dst, lt = (t % NB) * NT, t // NB
                    if not isinstance(n, int):
                        dst, lt = dve.snap(dst), dve.snap(lt)
                    x_lower, x_upper, x_all = g.xT[lower, bass.ds(dst, NT)], g.xT[upper, bass.ds(dst, NT - 1)], g.xT[:, bass.ds(dst, NT)]
                    nc.vector.tensor_scalar_mul(s.lp[:], g.lparam[:, bass.ds(lt, 1), :].rearrange("p a k -> p (a k)"), 1.0).then_inc(s.lp_ready, 1)
                for slot in range(SLOTS):
                    if attn and slot < HB:
                        h = slot
                        dve.wait_ge(s.s_done, HB * a + h + 1)
                        nc.vector.tensor_reduce(s.nm[:, h], ps[:, S_BANK[h % 3], 0:TT * KEYS].rearrange("p (t k) -> p t k", t=TT),
                                                AX.X, ALU.max, negate=True).then_inc(s.max_done, 1)
                    if front and slot < PIECES and slot % 6 < 4:
                        j, tt, c = slot, slot // 6, slot % 6
                        jq, which = 4 * tt + c, c // 2
                        dve.wait_ge(s.act_front, PIECES * f + j + 1)
                        if j == 0:
                            wait(dve, s.spare_full, spare_base(n))
                        wait(dve, s.pool_add, QK_PIECES * f + jq - 1)
                        raw = ps[:, F_BANK[j % 2]].rearrange("p (h z e) -> p h z e", z=2, e=DB // 2)
                        turned = s.vt[:, jq % 2].rearrange("p (h z e) -> p h z e", z=2, e=DB // 2)
                        sin = g.rotab[:, bass.ds(lf, 1), 2 * which + 1, tt]
                        nc.vector.tensor_tensor(s.w[:, tt, c * 512:(c + 1) * 512].rearrange("p (h e) -> p h e", e=DB),
                                                ps[:, F_BANK[j % 2]].rearrange("p (h e) -> p h e", e=DB),
                                                g.rotab[:, bass.ds(lf, 1), 2 * which, tt].broadcast_to((P, 8, DB)), ALU.mult)
                        for z in range(2):
                            last = nc.vector.tensor_tensor(turned[:, :, z], raw[:, :, 1 - z],
                                                           sin[:, :, z * (DB // 2):(z + 1) * (DB // 2)].broadcast_to((P, 8, DB // 2)), ALU.mult)
                        last.then_inc(s.dve_uv, 1)
                        nc.vector.tensor_reduce(s.ss[:, tt, c * 8:(c + 1) * 8], s.sq[:, jq % 2].rearrange("p (h e) -> p h e", e=DB),
                                                AX.X, ALU.add).then_inc(s.dve_red, 1)
                        if c == 3:
                            dve.wait_ge(s.dve_red, QK_PIECES * f + 4 * tt + 4)
                            nc.vector.tensor_scalar_max(s.ssm[:, tt], s.ss[:, tt], 1e-24).then_inc(s.clamp_done, 1)
                    if tail:
                        if slot == RES_SLOT:
                            dve.wait_ge(s.spare_full, spare[("wo", 0)] + 1)
                            nc.vector.tensor_tensor(x_all, ps[:, SPARE, 0:NT], x_all, ALU.add).then_inc(s.spare_free, 1)
                            dve.wait_ge(s.spare_free, spare[("wo", 0)] + 1)
                            nc.vector.tensor_scalar_mul(s.xs2[lower], x_lower, 1.0)
                            nc.vector.tensor_scalar_mul(s.xs2[upper, 1:NT], x_upper, 1.0).then_inc(s.shifted, 1)
                        if slot == STATS_SLOT:
                            dve.wait_ge(s.spare_full, spare[("xt", 0)] + 1)
                            nc.vector.tensor_copy(s.xtok[:], ps[:, SPARE, 0:NT].rearrange("p (t e) -> p t e", t=TT)).then_inc(s.spare_free, 1)
                            dve.wait_ge(s.spare_free, spare[("xt", 0)] + 1)
                            layernorm_stats(nc, dve, s.ff, s.xtok, t)
                        if slot == NORMED_SLOT:
                            layernorm_apply(nc, dve, s.ff, s.xtok, t)
                        if slot in W1_SLOT:
                            c = W1_SLOT[slot]
                            width = FF_CHUNKS[c][1]
                            dve.wait_ge(s.spare_full, spare[("w1", c)] + 1)
                            nc.vector.tensor_scalar_add(s.hgate[0:width, c], ps[0:width, SPARE, NT:2 * NT], s.lp[0:width, 6 + c:7 + c])
                            nc.vector.tensor_scalar_add(s.ha[0:width, c], ps[0:width, SPARE, 0:NT], s.lp[0:width, 3 + c:4 + c]).then_inc(s.spare_free, 1)
                        if slot == END_SLOT:
                            dve.wait_ge(s.spare_full, spare[("w2", 0)] + 1)
                            nc.vector.scalar_tensor_tensor(out=x_all, in0=ps[:, SPARE, 0:NT], scalar=s.lp[:, 2:3], in1=x_all,
                                                           op0=ALU.add, op1=ALU.add).then_inc(s.spare_free, 1)
                            dve.wait_ge(s.spare_free, spare[("w2", 0)] + 1)
                            dve.sem_inc(s.x_ready, 1)
                    if attn and slot % 4 == 2 and slot >= 6:
                        i = slot // 4 - 1
                        dve.wait_ge(s.pv_done, HB * a + 4 * i + 4)
                        if i == 0:
                            wait(dve, s.spare_free, spare_base(n) + (4 if tail else 0))
                        heads = slice(4 * i, 4 * i + 4)
                        nc.vector.reciprocal(s.rinv[:, heads], s.ssum[:, heads]).then_inc(s.rinv_ready, 1)
                        dve.wait_ge(s.rinv_ready, 4 * a + i + 1)
                        pv = ps[:, PV_BANK].rearrange("p (h t e) -> p h t e", h=4, t=TT)
                        for tt in range(TT):
                            last = nc.vector.tensor_tensor(s.o[:, tt, i * 4 * DB:(i + 1) * 4 * DB].rearrange("p (h e) -> p h e", e=DB),
                                                           pv[:, :, tt], s.rinv[:, heads, tt:tt + 1].broadcast_to((P, 4, DB)), ALU.mult)
                        last.then_inc(s.onorm, 1)
                    if front and slot in NORM_SLOT:
                        tt = NORM_SLOT[slot]
                        dve.wait_ge(s.pool_r, TT * f + tt + 1)
                        dve.wait_ge(s.pool_add, QK_PIECES * f + 4 * tt + 4)
                        rows = s.w[:, tt].rearrange("p (h e) -> p h e", e=DB)
                        nc.vector.tensor_tensor(rows, rows, s.rn[:, tt].rearrange("p (h o) -> p h o", o=1).broadcast_to((P, 2 * HB, DB)),
                                                ALU.mult).then_inc(s.dve_norm, 1)

            program(dve, body)

        @block.gpsimd
        def _(pool):
            def body(n, odd, front, attn, tail):
                f, t = n + 1, n - 1
                for slot in range(SLOTS):
                    if front and slot < PIECES and slot % 6 < 4:
                        tt, c = slot // 6, slot % 6
                        jq = 4 * tt + c
                        pool.wait_ge(s.dve_uv, QK_PIECES * f + jq + 1)
                        rows = s.w[:, tt, c * 512:(c + 1) * 512]
                        nc.gpsimd.tensor_tensor(rows, rows, s.vt[:, jq % 2], ALU.add).then_inc(s.pool_add, 1)
                    if front and slot in POWER_SLOT:
                        tt = POWER_SLOT[slot]
                        pool.wait_ge(s.clamp_done, TT * f + tt + 1)
                        nc.gpsimd.tensor_tensor(s.rn[:, tt], s.ssm[:, tt], g.neg_half[:], ALU.pow).then_inc(s.pool_r, 1)
                    if tail and slot == STATS_SLOT:
                        layernorm_pool(nc, pool, s.ff, g, t)
                    if tail and slot == GELU_SLOT:
                        pool.wait_ge(s.gelu_done, t + 1)
                        nc.gpsimd.tensor_tensor(s.hg[:], s.ha[:], s.gl[:], ALU.mult).then_inc(s.hg_ready, 1)

            program(pool, body)


def phase_c(nc, g, d, ps, out):
    with ExitStack() as stack:
        s = Store(nc, stack, "c")
        s.Win = s.sb("Win", [P, 2 * CH]); s.Wx = s.sb("Wx", [P, CC, XD]); s.Wdt = s.sb("Wdt", [RANK, CH]); s.Wout = s.sb("Wout", [P, CC, P])
        s.sel = s.sb("sel", [XD, 2 * NS, P])
        s.md0 = s.sb("md0", [P, 6]); s.md = s.sb("md", [P, 6])
        s.x3T = s.sb("x3T", [P, NT]); s.x3tok = s.sb("x3tok", [P, TT, P]); s.hT = s.sb("hT", [P, NT]); s.hT2 = s.sb("hT2", [P, NT])
        s.xp = s.sb("xp", [P, CC, TAPS - 1 + NT]); s.cv = s.sb("cv", [P, CC, NT]); s.h = s.sb("h", [P, CC, NT]); s.sr = s.sb("sr", [P, CC, NT])
        s.xd = s.sb("xd", [XD, NT]); s.zb = s.sb("zb", [P, CC, NT]); s.za = s.sb("za", [P, CC, NT]); s.delta = s.sb("delta", [P, CC, NT]); s.du = s.sb("du", [P, CC, NT])
        s.dA = s.sb("dA", [P, CC, NS, NT]); s.bu = s.sb("bu", [P, CC, NS, NT])
        s.y = s.sb("y", [P, CC, NT]); s.x4T = s.sb("x4T", [P, NT]); s.x4tok = s.sb("x4tok", [P, TT, P]); s.tmp = s.sb("tmp", [P, NT]); s.x5T = s.sb("x5T", [P, NT]); s.xout = s.sb("xout", [P, TT, P])
        s.l1 = LayerNorm(s, "l1"); s.l2 = LayerNorm(s, "l2")
        s.w_in, s.zeroed, s.md_ready, s.x3_ready, s.x3_full, s.x3tok_ready, s.h_full, s.hT_ready = s.sems("w_in zeroed md_ready x3_ready x3_full x3tok_ready h_full hT_ready")
        s.in_full, s.res_ready, s.xp_ready, s.conv_step, s.h_ready, s.xd_full, s.xd_ready, s.dl_full = s.sems("in_full res_ready xp_ready conv_step h_ready xd_full xd_ready dl_full")
        s.zb_ready, s.abs_done, s.exp_done, s.sp_done, s.delta_ready, s.du_ready, s.dA_ready, s.b_full = s.sems("zb_ready abs_done exp_done sp_done delta_ready du_ready dA_ready b_full")
        s.bu_ready, s.scan_done, s.c_full, s.yc_ready, s.y_full, s.y1_ready, s.y_ready, s.op_full = s.sems("bu_ready scan_done c_full yc_ready y_full y1_ready y_ready op_full")
        s.x4_ready, s.x4_full, s.x4tok_ready, s.h2_full, s.hT2_ready, s.lin_full, s.tmp_ready, s.x5_ready = s.sems("x4_ready x4_full x4tok_ready h2_full hT2_ready lin_full tmp_ready x5_ready")
        s.out_full, s.xout_ready, s.stored = s.sems("out_full xout_ready stored")
        block = stack.enter_context(nc.Block())
        PAIRS = NS // 2
        B_BANK, C_BANK, Y_BANK = (4, 5), (6, 7), 2

        @block.sync
        def _(sp):
            for dst, src in ((s.Win[:], d["L1_attn_in_proj_w"]), (s.Wx[:], d["L1_attn_x_proj_w"].rearrange("(c p) n -> p c n", p=P)),
                             (s.Wdt[:], d["L1_attn_dt_proj_w"]), (s.Wout[:], d["L1_attn_out_proj_w"].rearrange("(c p) n -> p c n", p=P)),
                             (s.sel[:], d["sel"])):
                sp.dma_start(dst, src).then_inc(s.w_in, 16)
            with sp.Fori(0, NB) as n:
                sp.wait_ge(s.xout_ready, n + 2)
                sp.dma_start(out[bass.ds(n, 1)].rearrange("b (t p) e -> p (b t) e", p=P), s.xout[:]).then_inc(s.stored, 16)
            sp.wait_ge(s.stored, 16 * NB + 16)

        @block.vector
        def _(dve):
            nc.vector.memset(s.dA[:], 0.0)
            nc.vector.memset(s.xp[:], 0.0).then_inc(s.zeroed, 1)
            dve.wait_ge(s.zeroed, 1)
            with dve.Fori(0, NB) as n:
                at = dve.snap(n * NT)
                dve.wait_ge(s.xout_ready, n + 1)
                nc.vector.tensor_scalar_mul(s.md0[:], g.mod[:, 0, bass.ds(n, 1), :].rearrange("p a k -> p (a k)"), 1.0)
                nc.vector.tensor_scalar_mul(s.md[:], g.mod[:, 1, bass.ds(n, 1), :].rearrange("p a k -> p (a k)"), 1.0).then_inc(s.md_ready, 1)
                dve.wait_ge(s.md_ready, n + 1)
                nc.vector.scalar_tensor_tensor(out=s.x3T[:], in0=g.xT[:, bass.ds(at, NT)], scalar=s.md0[:, 5:6], in1=g.x2T[:, bass.ds(at, NT)],
                                               op0=ALU.mult, op1=ALU.add).then_inc(s.x3_ready, 1)
                dve.wait_ge(s.x3_full, n + 1)
                nc.vector.tensor_copy(s.x3tok[:], ps[:, 0, 0:NT].rearrange("p (t e) -> p t e", t=TT)).then_inc(s.x3tok_ready, 1)
                dve.wait_ge(s.x3tok_ready, n + 1)
                layernorm_stats(nc, dve, s.l1, s.x3tok, n)
                layernorm_apply(nc, dve, s.l1, s.x3tok, n)
                dve.wait_ge(s.in_full, n + 1)
                nc.vector.tensor_copy(s.xp[:, :, TAPS - 1:], ps[:, 1].rearrange("p (c t) -> p c t", c=CC)).then_inc(s.xp_ready, 1)
                dve.wait_ge(s.xp_ready, n + 1)
                for k in range(TAPS):
                    for c in range(CC):
                        tap, w = s.xp[:, c, k:k + NT], g.conv_w[:, c, k:k + 1]
                        if k == 0:
                            last = nc.vector.tensor_scalar(s.cv[:, c], tap, w, g.conv_b[:, c:c + 1], ALU.mult, ALU.add)
                        else:
                            last = nc.vector.scalar_tensor_tensor(out=s.cv[:, c], in0=tap, scalar=w, in1=s.cv[:, c], op0=ALU.mult, op1=ALU.add)
                    last.then_inc(s.conv_step, 1)
                    dve.wait_ge(s.conv_step, TAPS * n + k + 1)
                dve.wait_ge(s.xd_full, n + 1)
                nc.vector.tensor_copy(s.xd[:], ps[0:XD, 2, 0:NT]).then_inc(s.xd_ready, 1)
                dve.wait_ge(s.dl_full, n + 1)
                for c in range(CC):
                    last = nc.vector.tensor_scalar_add(s.zb[:, c], ps[:, 3, c * NT:(c + 1) * NT], g.dt_b[:, c:c + 1])
                last.then_inc(s.zb_ready, 1)
                dve.wait_ge(s.sp_done, n + 1)
                nc.vector.scalar_tensor_tensor(out=s.delta[:], in0=s.zb[:], scalar=0.0, in1=s.za[:], op0=ALU.max, op1=ALU.add).then_inc(s.delta_ready, 1)
                dve.wait_ge(s.delta_ready, n + 1)
                nc.vector.tensor_tensor(s.du[:], s.delta[:], s.h[:], ALU.mult).then_inc(s.du_ready, 1)
                dve.wait_ge(s.du_ready, n + 1)
                for i in range(PAIRS):
                    dve.wait_ge(s.b_full, PAIRS * n + i + 1)
                    for c in range(CC):
                        last = nc.vector.tensor_tensor(s.bu[:, c, 2 * i:2 * i + 2], s.du[:, c:c + 1].broadcast_to((P, 2, NT)),
                                                       ps[:, B_BANK[i % 2]].rearrange("p (n t) -> p n t", n=2), ALU.mult)
                    last.then_inc(s.bu_ready, 1)
                dve.wait_ge(s.dA_ready, CC * (n + 1))
                dve.wait_ge(s.bu_ready, PAIRS * n + PAIRS)
                for c in range(CC):
                    for k in range(2):
                        half = slice(k * NS // 2, (k + 1) * NS // 2)
                        run = s.bu[:, c, half].rearrange("p n t -> p (n t)")
                        last = nc.vector.tensor_tensor_scan(run, s.dA[:, c, half].rearrange("p n t -> p (n t)"), run, 0.0, ALU.mult, ALU.add)
                last.then_inc(s.scan_done, 1)
                dve.wait_ge(s.scan_done, n + 1)
                for i in range(PAIRS):
                    dve.wait_ge(s.c_full, PAIRS * n + i + 1)
                    for c in range(CC):
                        both = s.bu[:, c, 2 * i:2 * i + 2]
                        last = nc.vector.tensor_tensor(both, both, ps[:, C_BANK[i % 2]].rearrange("p (n t) -> p n t", n=2), ALU.mult)
                    last.then_inc(s.yc_ready, 1)
                dve.wait_ge(s.y_full, n + 1)
                for c in range(CC):
                    last = nc.vector.scalar_tensor_tensor(out=s.y[:, c], in0=s.h[:, c], scalar=g.D[:, c:c + 1], in1=ps[:, Y_BANK, c * NT:(c + 1) * NT],
                                                          op0=ALU.mult, op1=ALU.add)
                last.then_inc(s.y1_ready, 1)
                dve.wait_ge(s.y1_ready, n + 1)
                nc.vector.tensor_tensor(s.y[:], s.y[:], s.sr[:], ALU.mult).then_inc(s.y_ready, 1)
                dve.wait_ge(s.op_full, n + 1)
                nc.vector.scalar_tensor_tensor(out=s.x4T[:], in0=ps[:, 0, 0:NT], scalar=s.md[:, 2:3], in1=s.x3T[:],
                                               op0=ALU.mult, op1=ALU.add).then_inc(s.x4_ready, 1)
                dve.wait_ge(s.x4_full, n + 1)
                nc.vector.tensor_copy(s.x4tok[:], ps[:, 1, 0:NT].rearrange("p (t e) -> p t e", t=TT)).then_inc(s.x4tok_ready, 1)
                dve.wait_ge(s.x4tok_ready, n + 1)
                layernorm_stats(nc, dve, s.l2, s.x4tok, n)
                layernorm_apply(nc, dve, s.l2, s.x4tok, n)
                dve.wait_ge(s.lin_full, n + 1)
                nc.vector.tensor_scalar(s.tmp[:], ps[:, 0, 0:NT], g.blin[:], s.md[:, 5:6], ALU.add, ALU.mult).then_inc(s.tmp_ready, 1)
                dve.wait_ge(s.tmp_ready, n + 1)
                nc.vector.tensor_tensor(s.x5T[:], s.tmp[:], s.x4T[:], ALU.add).then_inc(s.x5_ready, 1)

        @block.gpsimd
        def _(pool):
            with pool.Fori(0, NB) as n:
                layernorm_pool(nc, pool, s.l1, g, n)
                layernorm_pool(nc, pool, s.l2, g, n)

        @block.scalar
        def _(act):
            act.wait_ge(s.zeroed, 1)
            act.sem_inc(s.xout_ready, 1)
            act.sem_inc(s.stored, 16)
            with act.Fori(0, NB) as n:
                act.wait_ge(s.h_full, n + 1)
                act.wait_ge(s.md_ready, n + 1)
                nc.scalar.activation(s.hT[:], ps[:, 0, NT:2 * NT], ACT.Identity, bias=s.md[:, 0:1], scale=s.md[:, 1:2]).then_inc(s.hT_ready, 1)
                act.wait_ge(s.in_full, n + 1)
                nc.scalar.activation(s.sr[:], ps[:, 3].rearrange("p (c t) -> p c t", c=CC), ACT.Silu).then_inc(s.res_ready, 1)
                act.wait_ge(s.conv_step, TAPS * n + TAPS)
                nc.scalar.activation(s.h[:], s.cv[:], ACT.Silu).then_inc(s.h_ready, 1)
                act.wait_ge(s.zb_ready, n + 1)
                nc.scalar.activation(s.za[:], s.zb[:], ACT.Abs).then_inc(s.abs_done, 1)
                act.wait_ge(s.abs_done, n + 1)
                nc.scalar.activation(s.za[:], s.za[:], ACT.Exp, scale=-1.0).then_inc(s.exp_done, 1)
                act.wait_ge(s.exp_done, n + 1)
                nc.scalar.activation(s.za[:], s.za[:], ACT.Ln, bias=1.0).then_inc(s.sp_done, 1)
                act.wait_ge(s.delta_ready, n + 1)
                for c in range(CC):
                    for i in range(NS):
                        last = nc.scalar.activation(s.dA[:, c, i, 1:NT], s.delta[:, c, 1:NT], ACT.Exp, scale=g.A[:, c, i:i + 1])
                    last.then_inc(s.dA_ready, 1)
                act.wait_ge(s.h2_full, n + 1)
                nc.scalar.activation(s.hT2[:], ps[:, 1, NT:2 * NT], ACT.Identity, bias=s.md[:, 3:4], scale=s.md[:, 4:5]).then_inc(s.hT2_ready, 1)
                act.wait_ge(s.out_full, n + 1)
                act.wait_ge(s.stored, 16 * n + 16)
                nc.scalar.activation(s.xout[:], ps[:, 0, NT:2 * NT].rearrange("p (t e) -> p t e", t=TT), ACT.Copy).then_inc(s.xout_ready, 1)

        @block.tensor
        def _(pe):
            pe.wait_ge(s.w_in, 16 * 5)
            with pe.Fori(0, NB) as n:
                pe.wait_ge(s.x3_ready, n + 1)
                for tt in range(TT):
                    last = nc.tensor.transpose(ps[:, 0, tt * P:(tt + 1) * P], s.x3T[:, tt * P:(tt + 1) * P], g.ident[:])
                last.then_inc(s.x3_full, 1)
                pe.wait_ge(s.l1.normed, n + 1)
                for tt in range(TT):
                    last = nc.tensor.transpose(ps[:, 0, NT + tt * P:NT + (tt + 1) * P], s.l1.xn[:, tt], g.ident[:])
                last.then_inc(s.h_full, 1)
                pe.wait_ge(s.hT_ready, n + 1)
                for c in range(2 * CC):
                    bank = 1 if c < CC else 3
                    last = nc.tensor.matmul(ps[:, bank, c % CC * NT:(c % CC + 1) * NT], s.Win[:, c * P:(c + 1) * P], s.hT[:], start=True, stop=True)
                last.then_inc(s.in_full, 1)
                pe.wait_ge(s.h_ready, n + 1)
                for c in range(CC):
                    last = nc.tensor.matmul(ps[0:XD, 2, 0:NT], s.Wx[:, c], s.h[:, c], start=c == 0, stop=c == CC - 1)
                last.then_inc(s.xd_full, 1)
                pe.wait_ge(s.xd_ready, n + 1)
                pe.wait_ge(s.res_ready, n + 1)
                for c in range(CC):
                    last = nc.tensor.matmul(ps[:, 3, c * NT:(c + 1) * NT], s.Wdt[:, c * P:(c + 1) * P], s.xd[0:RANK], start=True, stop=True)
                last.then_inc(s.dl_full, 1)
                for which, banks, used, full in ((0, B_BANK, s.bu_ready, s.b_full), (1, C_BANK, s.yc_ready, s.c_full)):
                    for i in range(PAIRS):
                        if i >= 2:
                            pe.wait_ge(used, PAIRS * n + i - 1)
                        for k in range(2):
                            last = nc.tensor.matmul(ps[:, banks[i % 2], k * NT:(k + 1) * NT], s.sel[:, which * NS + 2 * i + k], s.xd[:], start=True, stop=True)
                        last.then_inc(full, 1)
                for i in range(NS):
                    pe.wait_ge(s.yc_ready, PAIRS * n + i // 2 + 1)
                    last = nc.tensor.matmul(ps[:, Y_BANK], g.ident[:], s.bu[:, :, i], start=i == 0, stop=i == NS - 1)
                last.then_inc(s.y_full, 1)
                pe.wait_ge(s.y_ready, n + 1)
                for c in range(CC):
                    last = nc.tensor.matmul(ps[:, 0, 0:NT], s.Wout[:, c], s.y[:, c], start=c == 0, stop=c == CC - 1)
                last.then_inc(s.op_full, 1)
                pe.wait_ge(s.x4_ready, n + 1)
                for tt in range(TT):
                    last = nc.tensor.transpose(ps[:, 1, tt * P:(tt + 1) * P], s.x4T[:, tt * P:(tt + 1) * P], g.ident[:])
                last.then_inc(s.x4_full, 1)
                pe.wait_ge(s.l2.normed, n + 1)
                for tt in range(TT):
                    last = nc.tensor.transpose(ps[:, 1, NT + tt * P:NT + (tt + 1) * P], s.l2.xn[:, tt], g.ident[:])
                last.then_inc(s.h2_full, 1)
                pe.wait_ge(s.hT2_ready, n + 1)
                nc.tensor.matmul(ps[:, 0, 0:NT], g.wlinT[:], s.hT2[:], start=True, stop=True).then_inc(s.lin_full, 1)
                pe.wait_ge(s.x5_ready, n + 1)
                for tt in range(TT):
                    last = nc.tensor.transpose(ps[:, 0, NT + tt * P:NT + (tt + 1) * P], s.x5T[:, tt * P:(tt + 1) * P], g.ident[:])
                last.then_inc(s.out_full, 1)



INPUTS = ["L0_attn_hidden_states", "L0_attn_Wq", "L0_attn_bq", "L0_attn_Wk", "L0_attn_bk", "L0_attn_Wv", "L0_attn_bv",
          "L0_attn_Wo", "L0_attn_bo", "L0_ffn_Wqkv", "L0_ffn_q_scale", "L0_ffn_k_scale", "L0_ffn_Wo", "L0_ffn_ln_g",
          "L0_ffn_ln_b", "L0_ffn_W1", "L0_ffn_b1", "L0_ffn_W2", "L0_ffn_b2", "L0_c", "L0_wmod", "L1_attn_in_proj_w",
          "L1_attn_conv_w", "L1_attn_conv_b", "L1_attn_x_proj_w", "L1_attn_dt_proj_w", "L1_attn_dt_proj_b", "L1_attn_A_log",
          "L1_attn_D_param", "L1_attn_out_proj_w", "L1_ffn_W", "L1_ffn_b", "L1_ffn_lora_down", "L1_ffn_lora_up",
          "L1_ffn_down_aux", "L1_ffn_up_aux", "L1_c", "L1_wmod"]


def build(nc, d, out):
    with ExitStack() as stack:
        g = Store(nc, stack, "all")
        g.ident = g.sb("ident", [P, P]); g.ident_bf = g.sb("ident_bf", [P, P], BF16); g.mask_f = g.sb("mask_f", [P, TT * KEYS]); g.mask_bf = g.sb("mask_bf", [P, TT * KEYS], BF16)
        g.ones_row = g.sb("ones_row", [1, P]); g.neg_half = g.sb("neg_half", [P, 2 * HB])
        g.xT = g.sb("xT", [P, NB * NT]); g.x2T = g.sb("x2T", [P, NB * NT])
        g.mod = g.sb("mod", [P, 2, NB, 6])
        g.wqk_pad = g.sb("wqk_pad", [P, 2, 4 * P]); g.wvT = g.sb("wvT", [P, P]); g.woT = g.sb("woT", [P, P]); g.wlinT = g.sb("wlinT", [P, P])
        g.bqk = g.sb("bqk", [P, 2, 4]); g.bv_row = g.sb("bv_row", [1, P]); g.bo = g.sb("bo", [P, 1])
        g.rotab = g.sb("rotab", [P, DEPTH, 4, TT, DB]); g.lparam = g.sb("lparam", [P, DEPTH, 9])
        g.conv_w = g.sb("conv_w", [P, CC, TAPS]); g.conv_b = g.sb("conv_b", [P, CC]); g.dt_b = g.sb("dt_b", [P, CC]); g.A = g.sb("A", [P, CC, NS]); g.D = g.sb("D", [P, CC])
        g.blin = g.sb("blin", [P, 1])
        ps = stack.enter_context(nc.psum_tensor("ps", [P, 8, 512], F32))
        setup(nc, g, d, ps)
        phase_a(nc, g, d, ps)
        phase_b(nc, g, d, ps)
        phase_c(nc, g, d, ps, out)


def shape_constants():
    i, c = np.arange(P)[:, None], np.arange(KEYS)[None, :]
    band = (c >= i) & (c <= i + WIN)
    mask = np.where(np.stack([band & (c >= WIN), band], 1), 0.0, MASKED).astype(np.float32).reshape(P, TT * KEYS)
    half = np.arange(0, DB, 2, dtype=np.float32)
    inv_freq = (np.float32(1.0) / np.float32(10000.0) ** (half / np.float32(DB))).astype(np.float32)
    t = np.arange(NT, dtype=np.float32)
    freqs = t[:, None] * inv_freq[None, :]
    base = ((half + np.float32(0.4 * DB)) / np.float32(1.4 * DB)).astype(np.float32)
    power = (t - NT // 2) / (WIN // 2)
    scale = base[None, :].astype(np.float64) ** power[:, None]
    cos, sin = np.cos(freqs.astype(np.float64)), np.sin(freqs.astype(np.float64))
    tables = []
    for factor in (8.0 * scale, 1.0 / scale):
        tables.append(np.concatenate([cos * factor, cos * factor], 1))
        tables.append(np.concatenate([-sin * factor, sin * factor], 1))
    rot = np.stack(tables, 0).astype(np.float32).reshape(4, TT, P, DB).transpose(2, 0, 1, 3)
    sel = np.zeros((XD, 2 * NS, P), np.float32)
    for k in range(2 * NS):
        sel[RANK + k, k] = 1.0
    return {"ident": np.eye(P, dtype=np.float32), "mask": mask, "rot": np.ascontiguousarray(rot), "sel": sel}


def kernel(**inputs):
    import concourse.bacc as bacc
    from concourse.bass_utils import run_bass_kernel_spmd

    nc = bacc.Bacc("TRN2", target_bir_lowering=False, num_devices=1)
    arrays, d = {}, {}
    given = {name: np.ascontiguousarray(inputs[name]) for name in INPUTS}
    given.update(shape_constants())
    for name, a in given.items():
        arrays["in_" + name] = a
        d[name] = nc.dram_tensor("in_" + name, a.shape, mybir.dt.from_np(a.dtype), kind="ExternalInput").ap()
    out = nc.dram_tensor("out", (NB, NT, P), F32, kind="ExternalOutput").ap()
    build(nc, d, out)
    result = run_bass_kernel_spmd(nc, [arrays], core_ids=[0])
    return result.results[0]["out"]
```

```python
from contextlib import ExitStack

import numpy as np

import concourse.bass as bass
from concourse import mybir

F32 = mybir.dt.float32
BF16 = mybir.dt.bfloat16
F32R = mybir.dt.float32r
ALU = mybir.AluOpType
ACT = mybir.ActivationFunctionType
AX = mybir.AxisListType

P = 128
NB, NT = 16, 256
TT = NT // P
H0, D0 = 16, 8
HB, DB = 16, 64
INNER = HB * DB
WIN = 32
DEPTH = 6
FF = 341
FF_CHUNKS = [(0, 128), (128, 128), (256, FF - 256)]
NS, CH, RANK, TAPS = 16, 256, 64, 4
CC = CH // P
XD = RANK + 2 * NS
LN_EPS = 1e-5
KEYS = P + WIN
MASKED = -1e30


def wait(engine, semaphore, value):
    if isinstance(value, int) and value <= 0:
        return
    engine.wait_ge(semaphore, value)


class Store:

    def __init__(self, nc, stack, stage):
        self.nc, self.stack, self.stage = nc, stack, stage

    def sb(self, name, shape, dtype=F32):
        return self.stack.enter_context(self.nc.sbuf_tensor(f"{self.stage}_{name}", shape, dtype))

    def sems(self, names):
        return [self.stack.enter_context(self.nc.semaphore(f"{self.stage}_{name}")) for name in names.split()]


def flat(ap):
    return ap.rearrange("(c p) -> p c", p=P)




def setup(nc, g, d, ps):
    with ExitStack() as stack:
        s = Store(nc, stack, "setup")
        s.crow = s.sb("crow", [NB, 2, P]); s.sig = s.sb("sig", [NB, 2, P]); s.scT = s.sb("scT", [P, 2, NB])
        s.wmod = s.sb("wmod", [P, 2, 6 * P]); s.raw_w = s.sb("raw_w", [P, 4, P]); s.Wlin = s.sb("Wlin", [P, P])
        s.ga = s.sb("ga", [P, 2, NB, 2]); s.gb = s.sb("gb", [P, 2, NB, 2])
        s.qkscale = s.sb("qkscale", [P, 2, DEPTH, DB]); s.rot = s.sb("rot", [P, 4, TT, DB])
        s.lora_dn = s.sb("lora_dn", [4, 100]); s.dn_aux = s.sb("dn_aux", [100, P]); s.lora_up = s.sb("lora_up", [50, 4]); s.up_aux = s.sb("up_aux", [P, 50])
        s.dnT = s.sb("dnT", [100, 4]); s.upT = s.sb("upT", [4, 50]); s.uaT = s.sb("uaT", [50, P]); s.t1 = s.sb("t1", [4, P]); s.t2 = s.sb("t2", [50, P])
        s.alog = s.sb("alog", [P, CC, NS])
        s.loaded_a, s.loaded_b, s.consts, s.sig_exp, s.sig_done, s.scT_full, s.scT_done, s.mod_full = s.sems("loaded_a loaded_b consts sig_exp sig_done scT_full scT_done mod_full")
        s.mod_done, s.wt_full, s.wt_done, s.lora_full, s.lora_done, s.gstep, s.a_exp, s.chain = s.sems("mod_done wt_full wt_done lora_full lora_done gstep a_exp chain")
        block = stack.enter_context(nc.Block())
        n_a = 0

        @block.sync
        def _(sp):
            loads = [(g.ident[:], d["ident"]), (g.mask_f[:], d["mask"]), (s.crow[:, 0], d["L0_c"]), (s.crow[:, 1], d["L1_c"]),
                     (s.wmod[:, 0], d["L0_wmod"]), (s.wmod[:, 1], d["L1_wmod"])]
            loads += [(s.raw_w[:, i], w) for i, w in enumerate((d["L0_attn_Wq"], d["L0_attn_Wk"], d["L0_attn_Wv"], d["L0_attn_Wo"]))]
            loads += [(s.Wlin[:], d["L1_ffn_W"]), (s.rot[:], d["rot"]),
                      (s.lora_dn[:], d["L1_ffn_lora_down"]), (s.dn_aux[:], d["L1_ffn_down_aux"]),
                      (s.lora_up[:], d["L1_ffn_lora_up"]), (s.up_aux[:], d["L1_ffn_up_aux"])]
            for dst, src in loads:
                sp.dma_start(dst, src).then_inc(s.loaded_a, 16)
            sp.wait_ge(s.loaded_a, 16 * len(loads))

        small = [(s.alog[:], d["L1_attn_A_log"].rearrange("(c p) n -> p c n", p=P)),
                 (g.bv_row[:], d["L0_attn_bv"].rearrange("(a n) -> a n", a=1)),
                 (g.bo[:], flat(d["L0_attn_bo"])),
                 (g.lparam[:, :, 0], d["L0_ffn_ln_g"].rearrange("l p -> p l")), (g.lparam[:, :, 1], d["L0_ffn_ln_b"].rearrange("l p -> p l")),
                 (g.lparam[:, :, 2], d["L0_ffn_b2"].rearrange("l p -> p l")),
                 (g.conv_w[:], d["L1_attn_conv_w"].rearrange("(c p) o k -> p c (o k)", p=P)),
                 (g.conv_b[:], flat(d["L1_attn_conv_b"])), (g.dt_b[:], flat(d["L1_attn_dt_proj_b"])),
                 (g.D[:], flat(d["L1_attn_D_param"])), (g.blin[:], flat(d["L1_ffn_b"])),
                 (s.qkscale[:, 0], d["L0_ffn_q_scale"].rearrange("(a l) e -> a l e", a=1).broadcast_to((P, DEPTH, DB))),
                 (s.qkscale[:, 1], d["L0_ffn_k_scale"].rearrange("(a l) e -> a l e", a=1).broadcast_to((P, DEPTH, DB)))]
        for half in range(2):
            for c, (c0, w) in enumerate(FF_CHUNKS):
                small.append((g.lparam[0:w, :, 3 + 3 * half + c], d["L0_ffn_b1"][:, half * FF + c0:half * FF + c0 + w].rearrange("l p -> p l")))
        for j in range(4):
            for i, bvec in enumerate((d["L0_attn_bq"], d["L0_attn_bk"])):
                small.append((g.bqk[32 * j:32 * j + D0, i, :],
                              bvec.rearrange("(grp j e) -> j e grp", j=4, e=D0)[j]))

        @block.scalar
        def _(act):
            act.wait_ge(s.consts, 1)
            with nc.allow_non_contiguous_dma(reason="vectors laid along partitions, once"):
                for dst, src in small:
                    act.dma_start(dst, src).then_inc(s.loaded_b, 16)
            act.wait_ge(s.loaded_a, 16 * 16)
            nc.scalar.activation(s.sig[:], s.crow[:], ACT.Exp, scale=-1.0).then_inc(s.sig_exp, 1)
            act.wait_ge(s.loaded_b, 16 * len(small))
            nc.scalar.activation(g.A[:], s.alog[:], ACT.Exp).then_inc(s.a_exp, 1)
            act.wait_ge(s.mod_done, 1)
            nc.scalar.activation(s.ga[:], g.mod[:, :, :, 2:6:3], ACT.Abs).then_inc(s.gstep, 1)

        @block.gpsimd
        def _(pool):
            nc.gpsimd.memset(g.lparam[:], 0.0)
            nc.gpsimd.memset(g.bqk[:], 0.0).then_inc(s.consts, 1)

        @block.vector
        def _(dve):
            count = [0]

            def link(ins):
                count[0] += 1
                ins.then_inc(s.chain, 1)
                dve.wait_ge(s.chain, count[0])

            nc.vector.memset(g.ones_row[:], 1.0)
            nc.vector.memset(g.neg_half[:], -0.5)
            link(nc.vector.memset(g.wqk_pad[:], 0.0))
            dve.wait_ge(s.loaded_a, 16 * 16)
            nc.vector.tensor_copy(g.ident_bf[:], g.ident[:])
            nc.vector.tensor_copy(g.mask_bf[:], g.mask_f[:])
            dve.wait_ge(s.sig_exp, 1)
            link(nc.vector.tensor_scalar_add(s.sig[:], s.sig[:], 1.0))
            link(nc.vector.reciprocal(s.sig[:], s.sig[:]))
            nc.vector.tensor_tensor(s.sig[:], s.sig[:], s.crow[:], ALU.mult).then_inc(s.sig_done, 1)
            dve.wait_ge(s.wt_full, 1)
            for i in range(2):
                nc.vector.tensor_copy(g.wqk_pad[:, i].rearrange("p (h e) -> p h e", e=32)[:, :, 0:D0],
                                      ps[:, 1, i * P:(i + 1) * P].rearrange("p (h e) -> p h e", e=D0))
            nc.vector.tensor_copy(g.wvT[:], ps[:, 1, 2 * P:3 * P])
            nc.vector.tensor_copy(g.woT[:], ps[:, 1, 3 * P:4 * P])
            nc.vector.tensor_copy(s.dnT[:], ps[0:100, 2, 0:4])
            nc.vector.tensor_copy(s.upT[:], ps[0:4, 2, 128:178])
            nc.vector.tensor_copy(s.uaT[:], ps[0:50, 2, 256:384])
            nc.vector.tensor_copy(g.wlinT[:], ps[:, 2, 384:512]).then_inc(s.wt_done, 1)
            dve.wait_ge(s.lora_full, 1)
            nc.vector.tensor_copy(s.t1[:], ps[0:4, 3, 0:P]).then_inc(s.lora_done, 1)
            dve.wait_ge(s.lora_full, 2)
            nc.vector.tensor_copy(s.t2[:], ps[0:50, 4, 0:P]).then_inc(s.lora_done, 1)
            dve.wait_ge(s.lora_full, 3)
            nc.vector.tensor_tensor(g.wlinT[:], g.wlinT[:], ps[:, 5, 0:P], ALU.add)
            dve.wait_ge(s.scT_full, 1)
            nc.vector.tensor_copy(s.scT[:], ps[:, 0, 0:2 * NB].rearrange("p (l b) -> p l b", l=2)).then_inc(s.scT_done, 1)
            dve.wait_ge(s.mod_full, 1)
            nc.vector.tensor_copy(g.mod[:], ps[:, 6, 0:12 * NB].rearrange("p (l j b) -> p l b j", l=2, j=6)).then_inc(s.mod_done, 1)
            dve.wait_ge(s.gstep, 1)
            gates = g.mod[:, :, :, 2:6:3]
            nc.vector.tensor_scalar(s.gb[:], gates, 0.0, 2.0, ALU.is_ge, ALU.mult)
            link(nc.vector.tensor_scalar_max(s.ga[:], s.ga[:], 0.25))
            link(nc.vector.tensor_scalar_add(s.gb[:], s.gb[:], -1.0))
            link(nc.vector.tensor_tensor(gates, s.ga[:], s.gb[:], ALU.mult))
            scales = g.mod[:, :, :, 1:6:3]
            nc.vector.tensor_scalar_add(scales, scales, 1.0)
            dve.wait_ge(s.loaded_b, 16 * len(small))
            nc.vector.tensor_scalar_mul(g.bqk[:, 0], g.bqk[:, 0], float(D0) ** -0.5)
            for i in range(2):
                for tt in range(TT):
                    cos = s.rot[:, 2 * i:2 * i + 1, tt].broadcast_to((P, DEPTH, DB))
                    nc.vector.tensor_tensor(g.rotab[:, :, 2 * i, tt], s.qkscale[:, i], cos, ALU.mult)
                    for half in range(2):
                        a, b = half * (DB // 2), (1 - half) * (DB // 2)
                        sin = s.rot[:, 2 * i + 1:2 * i + 2, tt, a:a + DB // 2].broadcast_to((P, DEPTH, DB // 2))
                        nc.vector.tensor_tensor(g.rotab[:, :, 2 * i + 1, tt, a:a + DB // 2],
                                                s.qkscale[:, i, :, b:b + DB // 2], sin, ALU.mult)
            dve.wait_ge(s.a_exp, 1)
            nc.vector.tensor_scalar_mul(g.A[:], g.A[:], -1.0)

        @block.tensor
        def _(pe):
            pe.wait_ge(s.loaded_a, 16 * 16)
            for i in range(4):
                nc.tensor.transpose(ps[:, 1, i * P:(i + 1) * P], s.raw_w[:, i], g.ident[:])
            nc.tensor.transpose(ps[0:100, 2, 0:4], s.lora_dn[:], g.ident[0:4, 0:4])
            nc.tensor.transpose(ps[0:4, 2, 128:178], s.lora_up[:], g.ident[0:50, 0:50])
            nc.tensor.transpose(ps[0:50, 2, 256:384], s.up_aux[:], g.ident[:])
            nc.tensor.transpose(ps[:, 2, 384:512], s.Wlin[:], g.ident[:]).then_inc(s.wt_full, 1)
            pe.wait_ge(s.wt_done, 1)
            nc.tensor.matmul(ps[0:4, 3, 0:P], s.dnT[:], s.dn_aux[:], start=True, stop=True).then_inc(s.lora_full, 1)
            pe.wait_ge(s.lora_done, 1)
            nc.tensor.matmul(ps[0:50, 4, 0:P], s.upT[:], s.t1[:], start=True, stop=True).then_inc(s.lora_full, 1)
            pe.wait_ge(s.lora_done, 2)
            nc.tensor.matmul(ps[:, 5, 0:P], s.t2[:], s.uaT[:], start=True, stop=True).then_inc(s.lora_full, 1)
            pe.wait_ge(s.sig_done, 1)
            for l in range(2):
                last = nc.tensor.transpose(ps[:, 0, l * NB:(l + 1) * NB], s.sig[:, l], g.ident[0:NB, 0:NB])
            last.then_inc(s.scT_full, 1)
            pe.wait_ge(s.scT_done, 1)
            for l in range(2):
                for j in range(6):
                    k = (l * 6 + j) * NB
                    last = nc.tensor.matmul(ps[:, 6, k:k + NB], s.wmod[:, l, j * P:(j + 1) * P], s.scT[:, l],
                                            start=True, stop=True)
            last.then_inc(s.mod_full, 1)




class LayerNorm:

    def __init__(self, s, name):
        self.st = s.sb(name + "_st", [P, TT, 6])
        self.mv = s.sb(name + "_mv", [P, TT, 2])
        self.var = s.sb(name + "_var", [P, TT])
        self.rstd = s.sb(name + "_rstd", [P, TT])
        self.xn = s.sb(name + "_xn", [P, TT, P])
        self.stats, self.aggr, self.var_ready, self.rstd_ready, self.normed = s.sems(
            " ".join(f"{name}_{x}" for x in ("stats", "aggr", "var_ready", "rstd_ready", "normed")))


def layernorm_stats(nc, dve, ln, src, n):
    for tt in range(TT):
        last = nc.vector.bn_stats(ln.st[:, tt], src[:, tt])
    last.then_inc(ln.stats, 1)
    dve.wait_ge(ln.stats, n + 1)
    nc.vector.memset(ln.var[:], LN_EPS)
    for tt in range(TT):
        last = nc.vector.bn_aggr(ln.mv[:, tt], ln.st[:, tt])
    last.then_inc(ln.aggr, 1)
    dve.wait_ge(ln.aggr, n + 1)
    nc.vector.tensor_tensor(ln.var[:], ln.mv[:, :, 1], ln.var[:], ALU.add).then_inc(ln.var_ready, 1)


def layernorm_pool(nc, pool, ln, g, n):
    pool.wait_ge(ln.var_ready, n + 1)
    nc.gpsimd.tensor_tensor(ln.rstd[:], ln.var[:], g.neg_half[:, 0:TT], ALU.pow).then_inc(ln.rstd_ready, 1)


def layernorm_apply(nc, dve, ln, src, n):
    dve.wait_ge(ln.rstd_ready, n + 1)
    for tt in range(TT):
        last = nc.vector.tensor_scalar(ln.xn[:, tt], src[:, tt], ln.mv[:, tt, 0:1], ln.rstd[:, tt:tt + 1], ALU.subtract, ALU.mult)
    last.then_inc(ln.normed, 1)




def phase_a(nc, g, d, ps):
    with ExitStack() as stack:
        s = Store(nc, stack, "a")
        s.xtok = s.sb("xtok", [P, TT, P]); s.xTs = s.sb("xTs", [P, NT]); s.hT = s.sb("hT", [P, NT]); s.md = s.sb("md", [P, 6])
        s.qT = s.sb("qT", [P, 4, NT]); s.kT = s.sb("kT", [P, 4, NT]); s.V = s.sb("V", [P, TT, P])
        s.nm = s.sb("nm", [P, H0, TT]); s.ssum = s.sb("ssum", [P, H0, TT]); s.rinv = s.sb("rinv", [P, H0, TT])
        s.Pr = s.sb("Pr", [P, 3, TT, NT]); s.PT = s.sb("PT", [P, 2, TT, NT])
        s.o = s.sb("o", [P, TT, H0, D0]); s.oT = s.sb("oT", [P, NT]); s.tmp = s.sb("tmp", [P, NT]); s.x2s = s.sb("x2s", [P, NT]); s.x2tok = s.sb("x2tok", [P, TT, P])
        s.l1 = LayerNorm(s, "l1"); s.l2 = LayerNorm(s, "l2")
        s.x_in, s.md_ready, s.hx_full, s.xT_done, s.hT_ready, s.qk_full, s.qk_ready, s.v_full = s.sems("x_in md_ready hx_full xT_done hT_ready qk_full qk_ready v_full")
        s.v_ready, s.s_done, s.max_done, s.exp_done, s.t_done, s.pt_ready, s.pv_done, s.rinv_ready = s.sems("v_ready s_done max_done exp_done t_done pt_ready pv_done rinv_ready")
        s.o_ready, s.oT_full, s.oT_ready, s.proj_full, s.tmp_ready, s.x2s_ready, s.x2_full, s.x2tok_ready = s.sems("o_ready oT_full oT_ready proj_full tmp_ready x2s_ready x2_full x2tok_ready")
        s.h2_full, s.seq_done, s.x2_kept = s.sems("h2_full seq_done x2_kept")
        block = stack.enter_context(nc.Block())
        S_BANK, PT_BANK, QK_BANK = (1, 2, 3), (4, 5), (7, 4)

        @block.sync
        def _(sp):
            sp.dma_start(s.xtok[:], d["L0_attn_hidden_states"][0].rearrange("(t p) e -> p t e", p=P)).then_inc(s.x_in, 16)
            with sp.Fori(1, NB) as n:
                sp.wait_ge(s.xT_done, n)
                sp.wait_ge(s.l1.normed, n)
                sp.dma_start(s.xtok[:], d["L0_attn_hidden_states"][bass.ds(n, 1)].rearrange("b (t p) e -> p (b t) e", p=P)).then_inc(s.x_in, 16)

        @block.vector
        def _(dve):
            with dve.Fori(0, NB) as n:
                dve.wait_ge(s.seq_done, n + 1)
                nc.vector.tensor_scalar_mul(s.md[:], g.mod[:, 0, bass.ds(n, 1), :].rearrange("p a k -> p (a k)"), 1.0).then_inc(s.md_ready, 1)
                dve.wait_ge(s.x_in, 16 * n + 16)
                layernorm_stats(nc, dve, s.l1, s.xtok, n)
                layernorm_apply(nc, dve, s.l1, s.xtok, n)
                dve.wait_ge(s.hx_full, n + 1)
                nc.vector.tensor_copy(s.xTs[:], ps[:, 0, NT:2 * NT]).then_inc(s.xT_done, 1)
                dve.wait_ge(s.v_full, n + 1)
                nc.vector.tensor_copy(s.V[:], ps[:, 5, 0:NT].rearrange("p (t e) -> p t e", t=TT)).then_inc(s.v_ready, 1)
                for h in range(H0 + 1):
                    if h < H0:
                        dve.wait_ge(s.s_done, H0 * n + h + 1)
                        nc.vector.tensor_reduce(s.nm[:, h], ps[:, S_BANK[h % 3]].rearrange("p (t k) -> p t k", t=TT),
                                                AX.X, ALU.max, negate=True).then_inc(s.max_done, 1)
                    if h >= 1:
                        k = h - 1
                        dve.wait_ge(s.t_done, H0 * n + k + 1)
                        if k >= 2:
                            dve.wait_ge(s.pv_done, H0 * n + k - 1)
                        nc.vector.tensor_copy(s.PT[:, k % 2], ps[:, PT_BANK[k % 2]].rearrange("p (t k) -> p t k", t=TT)).then_inc(s.pt_ready, 1)
                nc.vector.reciprocal(s.rinv[:], s.ssum[:]).then_inc(s.rinv_ready, 1)
                dve.wait_ge(s.rinv_ready, n + 1)
                dve.wait_ge(s.pv_done, H0 * n + H0)
                for tt in range(TT):
                    last = nc.vector.tensor_tensor(s.o[:, tt], ps[:, 6, tt * P:(tt + 1) * P].rearrange("p (h e) -> p h e", e=D0),
                                                   s.rinv[:, :, tt:tt + 1].broadcast_to((P, H0, D0)), ALU.mult)
                last.then_inc(s.o_ready, 1)
                dve.wait_ge(s.proj_full, n + 1)
                nc.vector.tensor_scalar(s.tmp[:], ps[:, 7, 0:NT], g.bo[:], s.md[:, 2:3], ALU.add, ALU.mult).then_inc(s.tmp_ready, 1)
                dve.wait_ge(s.tmp_ready, n + 1)
                nc.vector.tensor_tensor(s.x2s[:], s.tmp[:], s.xTs[:], ALU.add).then_inc(s.x2s_ready, 1)
                dve.wait_ge(s.x2_full, n + 1)
                nc.vector.tensor_copy(s.x2tok[:], ps[:, 0, 0:NT].rearrange("p (t e) -> p t e", t=TT)).then_inc(s.x2tok_ready, 1)
                dve.wait_ge(s.x2tok_ready, n + 1)
                layernorm_stats(nc, dve, s.l2, s.x2tok, n)
                layernorm_apply(nc, dve, s.l2, s.x2tok, n)

        @block.gpsimd
        def _(pool):
            with pool.Fori(0, NB) as n:
                layernorm_pool(nc, pool, s.l1, g, n)
                pool.wait_ge(s.x2s_ready, n + 1)
                nc.gpsimd.tensor_copy(g.x2T[:, bass.ds(n * NT, NT)], s.x2s[:]).then_inc(s.x2_kept, 1)
                layernorm_pool(nc, pool, s.l2, g, n)

        @block.scalar
        def _(act):
            act.sem_inc(s.seq_done, 1)
            with act.Fori(0, NB) as n:
                act.wait_ge(s.xT_done, n + 1)
                act.wait_ge(s.md_ready, n + 1)
                nc.scalar.activation(s.hT[:], ps[:, 0, 0:NT], ACT.Identity, bias=s.md[:, 0:1], scale=s.md[:, 1:2]).then_inc(s.hT_ready, 1)
                for grp in range(4):
                    act.wait_ge(s.qk_full, 4 * n + grp + 1)
                    bank = QK_BANK[grp % 2]
                    nc.scalar.activation(s.qT[:, grp], ps[:, bank, 0:NT], ACT.Identity, bias=g.bqk[:, 0, grp:grp + 1], scale=float(D0) ** -0.5)
                    nc.scalar.activation(s.kT[:, grp], ps[:, bank, NT:2 * NT], ACT.Identity, bias=g.bqk[:, 1, grp:grp + 1]).then_inc(s.qk_ready, 1)
                for h in range(H0):
                    act.wait_ge(s.max_done, H0 * n + h + 1)
                    if h >= 3:
                        act.wait_ge(s.t_done, H0 * n + h - 2)
                    for tt in range(TT):
                        last = nc.scalar.activation(s.Pr[:, h % 3, tt], ps[:, S_BANK[h % 3], tt * NT:(tt + 1) * NT], ACT.Exp,
                                                    bias=s.nm[:, h, tt:tt + 1], accum_out=s.ssum[:, h, tt:tt + 1])
                    last.then_inc(s.exp_done, 1)
                act.wait_ge(s.oT_full, n + 1)
                nc.scalar.activation(s.oT[:], ps[:, 0, 0:NT], ACT.Copy).then_inc(s.oT_ready, 1)
                act.wait_ge(s.h2_full, n + 1)
                nc.scalar.activation(g.xT[:, bass.ds(n * NT, NT)], ps[:, 0, NT:2 * NT], ACT.Identity,
                                     bias=s.md[:, 3:4], scale=s.md[:, 4:5]).then_inc(s.seq_done, 1)

        @block.tensor
        def _(pe):
            with pe.Fori(0, NB) as n:
                pe.wait_ge(s.l1.normed, n + 1)
                for tt in range(TT):
                    nc.tensor.transpose(ps[:, 0, tt * P:(tt + 1) * P], s.l1.xn[:, tt], g.ident[:])
                    last = nc.tensor.transpose(ps[:, 0, NT + tt * P:NT + (tt + 1) * P], s.xtok[:, tt], g.ident[:])
                last.then_inc(s.hx_full, 1)
                pe.wait_ge(s.hT_ready, n + 1)
                for grp in range(4):
                    if grp >= 2:
                        pe.wait_ge(s.qk_ready, 4 * n + grp - 1)
                    for i in range(2):
                        last = nc.tensor.matmul(ps[:, QK_BANK[grp % 2], i * NT:(i + 1) * NT], g.wqk_pad[:, i, grp * P:(grp + 1) * P],
                                                s.hT[:], start=True, stop=True)
                    last.then_inc(s.qk_full, 1)
                for tt in range(TT):
                    nc.tensor.matmul(ps[:, 5, tt * P:(tt + 1) * P], g.ones_row[:], g.bv_row[:], start=True, stop=False)
                    last = nc.tensor.matmul(ps[:, 5, tt * P:(tt + 1) * P], s.hT[:, tt * P:(tt + 1) * P], g.wvT[:], start=False, stop=True)
                last.then_inc(s.v_full, 1)
                for h in range(H0 + 2):
                    if h < H0:
                        grp, r = h // 4, 32 * (h % 4)
                        pe.wait_ge(s.qk_ready, 4 * n + grp + 1)
                        if h >= 3:
                            pe.wait_ge(s.exp_done, H0 * n + h - 2)
                        for tt in range(TT):
                            last = nc.tensor.matmul(ps[:, S_BANK[h % 3], tt * NT:(tt + 1) * NT], s.qT[r:r + 32, grp, tt * P:(tt + 1) * P],
                                                    s.kT[r:r + 32, grp], start=True, stop=True)
                        last.then_inc(s.s_done, 1)
                    if 1 <= h <= H0:
                        k = h - 1
                        pe.wait_ge(s.exp_done, H0 * n + k + 1)
                        if k < 2:
                            pe.wait_ge(s.v_ready, n + 1)
                            pe.wait_ge(s.qk_ready, 4 * n + 4)
                        else:
                            pe.wait_ge(s.pt_ready, H0 * n + k - 1)
                        for kb in range(TT):
                            for tt in range(TT):
                                last = nc.tensor.transpose(ps[:, PT_BANK[k % 2], kb * NT + tt * P:kb * NT + (tt + 1) * P],
                                                           s.Pr[:, k % 3, tt, kb * P:(kb + 1) * P], g.ident[:])
                        last.then_inc(s.t_done, 1)
                    if h >= 2:
                        k = h - 2
                        pe.wait_ge(s.pt_ready, H0 * n + k + 1)
                        for tt in range(TT):
                            for kb in range(TT):
                                c = tt * P + k * D0
                                last = nc.tensor.matmul(ps[:, 6, c:c + D0], s.PT[:, k % 2, kb, tt * P:(tt + 1) * P],
                                                        s.V[:, kb, k * D0:(k + 1) * D0], start=kb == 0, stop=kb == TT - 1)
                        last.then_inc(s.pv_done, 1)
                pe.wait_ge(s.o_ready, n + 1)
                for tt in range(TT):
                    last = nc.tensor.transpose(ps[:, 0, tt * P:(tt + 1) * P], s.o[:, tt].rearrange("p h e -> p (h e)"), g.ident[:])
                last.then_inc(s.oT_full, 1)
                pe.wait_ge(s.oT_ready, n + 1)
                nc.tensor.matmul(ps[:, 7, 0:NT], g.woT[:], s.oT[:], start=True, stop=True).then_inc(s.proj_full, 1)
                pe.wait_ge(s.x2s_ready, n + 1)
                for tt in range(TT):
                    last = nc.tensor.transpose(ps[:, 0, tt * P:(tt + 1) * P], s.x2s[:, tt * P:(tt + 1) * P], g.ident[:])
                last.then_inc(s.x2_full, 1)
                pe.wait_ge(s.l2.normed, n + 1)
                for tt in range(TT):
                    last = nc.tensor.transpose(ps[:, 0, NT + tt * P:NT + (tt + 1) * P], s.l2.xn[:, tt], g.ident[:])
                last.then_inc(s.h2_full, 1)



ITEMS = DEPTH * NB
SLOTS = HB
T_LAG, PV_LAG = 2, 3
WCHUNKS = 6
RAW = 3
PIECES = [(tt, c) for tt in range(TT) for c in range(4)] + [(tt, c) for tt in range(TT) for c in (4, 5)]
N_QK = 4 * TT
POWER_SLOT = {3: 0, 7: 1}
NORM_SLOT = {7: 0, 11: 1}
TRANSPOSE_SLOT = {9: (0, 0), 10: (0, 2), 11: (0, 1), 12: (0, 3), 13: (1, 0), 14: (1, 2)}
LATE_SLOT = {1: (1, 1), 2: (1, 3)}
OUT_SLOT = {0: ((0, 0), (1, 0)), 5: ((0, 1),), 6: ((1, 1),)}
WO_SLOT, RES_SLOT, XT_SLOT, STATS_SLOT, NORMED_SLOT, XN_SLOT = 8, 9, 11, 11, 13, 15
W1_SLOT = {3: 0, 4: 1, 7: 2}
GELU_SLOT, W2_SLOT, END_SLOT, SPLIT_SLOT = 9, 15, 15, 14


def spare_uses(front, attn, tail, ffn):
    uses = []
    for slot in range(SLOTS):
        if tail:
            uses += [("out", which) for which in OUT_SLOT.get(slot, ())]
            uses += [(kind, 0) for at, kind in ((WO_SLOT, "wo"), (XT_SLOT, "xt"), (XN_SLOT, "xn")) if slot == at]
        if ffn:
            uses += [("w1", W1_SLOT[slot])] if slot in W1_SLOT else []
            uses += [("w2", 0)] if slot == W2_SLOT else []
        if attn and slot in LATE_SLOT:
            uses.append(("tr", LATE_SLOT[slot]))
        if front and slot in TRANSPOSE_SLOT:
            uses.append(("tr", TRANSPOSE_SLOT[slot]))
    return uses


def stages_of(n):
    return n + 1 < ITEMS, 0 <= n < ITEMS, 0 <= n - 1 < ITEMS, 0 <= n - 2 < ITEMS


class Step:

    def __init__(self, n, odd, front, tail, ffn, half=None, convert=False):
        self.n, self.odd, self.front, self.tail, self.ffn, self.convert = n, odd, front, tail, ffn, convert
        every = len(spare_uses(True, True, True, True))
        if half is None:
            self.attn = stages_of(n)[1]
            self.uses, self.uses_before = spare_uses(*stages_of(n)), spare_uses(*stages_of(n - 1))
            self.halves, self.first = 0, sum(len(spare_uses(*stages_of(i))) for i in range(-1, n))
        else:
            self.attn = True
            self.uses = self.uses_before = spare_uses(True, True, True, True)
            start = sum(len(spare_uses(*stages_of(i))) for i in range(-1, 2))
            self.halves, self.first = every * half, start + (every if odd else 0) - 2 * every

    def spare(self, use):
        i = self.first + self.uses.index(use)
        return i % 2, self.halves + i // 2

    def spare_of_before(self, use):
        i = self.first - len(self.uses_before) + self.uses_before.index(use)
        return i % 2, self.halves + i // 2


def phase_b_steps(engine, body):
    def whole(n):
        stages = stages_of(n)
        items = [divmod(n + d, NB) if there else None for d, there in zip((1, 0, -1, -2), stages)]
        body(Step(n, n % 2, items[0], items[2], items[3], convert=n == -1))

    def inner(l):
        with engine.Fori(1, NB // 2 - 1) as pair:
            n, half = NB * l + 2 * pair + 1, NB // 2 * l + pair
            body(Step(n, 1, (l, 2 * pair + 2), (l, 2 * pair), (l, 2 * pair - 1), half))
            body(Step(n + 1, 0, (l, 2 * pair + 3), (l, 2 * pair + 1), (l, 2 * pair), half + 1))

    for n in range(-1, 3):
        whole(n)
    with engine.Fori(0, DEPTH - 1) as l:
        inner(l)
        n, half = NB * l + NB - 1, NB // 2 * l + NB // 2 - 1
        body(Step(n, 1, (l + 1, 0), (l, NB - 2), (l, NB - 3), half, convert=True))
        body(Step(n + 1, 0, (l + 1, 1), (l, NB - 1), (l, NB - 2), half + 1))
        body(Step(n + 2, 1, (l + 1, 2), (l + 1, 0), (l, NB - 1), half + 1))
        body(Step(n + 3, 0, (l + 1, 3), (l + 1, 1), (l + 1, 0), half + 2))
    inner(DEPTH - 1)
    for n in range(ITEMS - 1, ITEMS + 2):
        whole(n)


def phase_b(nc, g, d, ps):
    with ExitStack() as stack:
        s = Store(nc, stack, "b")
        s.Wraw = s.sb("Wraw", [P, RAW, 512])
        s.Whi = s.sb("Whi", [P, 3 * INNER], F32R); s.Wlo = s.sb("Wlo", [P, 3 * INNER], F32R)
        s.Wo = s.sb("Wo", [P, INNER // P, P]); s.W1 = s.sb("W1", [P, 2 * FF]); s.W2 = s.sb("W2", [P, 3, P])
        s.xhi = s.sb("xhi", [P, 2, NT], F32R); s.xlo = s.sb("xlo", [P, 2, NT], F32R)
        s.w = s.sb("w", [P, TT, 2 * INNER])
        s.vt = s.sb("vt", [P, 4, 512]); s.sq = s.sb("sq", [P, 2, 512])
        s.ss = s.sb("ss", [P, TT, 2 * HB]); s.ssm = s.sb("ssm", [P, TT, 2 * HB]); s.rn = s.sb("rn", [P, TT, 2 * HB])
        s.qkT = s.sb("qkT", [P, 2, 2 * INNER // P, NT])
        s.V = s.sb("V", [P, 2, TT, INNER])
        s.nm = s.sb("nm", [P, HB, TT]); s.ssum = s.sb("ssum", [P, HB, TT]); s.rinv = s.sb("rinv", [P, HB, TT])
        s.Pr = s.sb("Pr", [P, 4, P + KEYS])
        s.PT = s.sb("PT", [P, 4, 2 * P + WIN])
        s.o = s.sb("o", [P, TT, INNER]); s.oT = s.sb("oT", [P, INNER // P, NT])
        s.lp = s.sb("lp", [P, 7]); s.lnp = s.sb("lnp", [P, 2])
        s.xs2 = s.sb("xs2", [P, NT]); s.xtok = s.sb("xtok", [P, TT, P]); s.xnT = s.sb("xnT", [P, NT])
        s.ha = s.sb("ha", [P, 3, NT]); s.hgate = s.sb("hgate", [P, 3, NT])
        s.ff = LayerNorm(s, "ff")
        s.zeroed, s.wo_in, s.w1_in, s.w2_in, s.whi_done, s.w_ready = s.sems("zeroed wo_in w1_in w2_in whi_done w_ready")
        s.xhi_done, s.xs_ready, s.proj_done, s.act_front, s.dve_uv, s.dve_red, s.pool_add = s.sems(
            "xhi_done xs_ready proj_done act_front dve_uv dve_red pool_add")
        s.clamp_done, s.pool_r, s.dve_norm, s.s_done, s.max_done, s.exp_done, s.t_done, s.pt_ready, s.before_ready = s.sems(
            "clamp_done pool_r dve_norm s_done max_done exp_done t_done pt_ready before_ready")
        s.pv_done, s.rinv_ready, s.onorm, s.lp_ready, s.lnp_ready, s.shifted, s.gelu_done, s.hg_ready, s.x_ready = s.sems(
            "pv_done rinv_ready onorm lp_ready lnp_ready shifted gelu_done hg_ready x_ready")
        s.wqkv_in = s.sems(" ".join(f"wqkv_in_{i}" for i in range(RAW)))
        s.spare_full = s.sems("spare_full_0 spare_full_1")
        s.spare_free = s.sems("spare_free_0 spare_free_1")
        block = stack.enter_context(nc.Block())
        S_BANK, F_BANK, T_BANK, PV_BANK, SPARE = (0, 1), (2, 3), 4, 5, (6, 7)
        OWN, BEFORE = slice(P + WIN, P + KEYS), slice(P, P + WIN)

        def started(step, slot, lag):
            if slot >= lag:
                return (step.n, slot - lag) if step.attn else (None, None)
            return (step.n - 1, slot - lag + SLOTS) if step.tail is not None else (None, None)

        @block.sync
        def _(sp):
            def load_chunks(l, pieces):
                for c in pieces:
                    wait(sp, s.w_ready, WCHUNKS * l + c + 1 - RAW)
                    sp.dma_start(s.Wraw[:, c % RAW], d["L0_ffn_Wqkv"][l, :, c * 512:(c + 1) * 512]).then_inc(s.wqkv_in[c % RAW], 16)

            for l in range(DEPTH):
                load_chunks(l, range(RAW if l == 0 else WCHUNKS))
                if l:
                    sp.wait_ge(s.shifted, NB * l)
                sp.dma_start(s.Wo[:], d["L0_ffn_Wo"][l].rearrange("(c p) n -> p c n", p=P)).then_inc(s.wo_in, 16)
                if l:
                    sp.wait_ge(s.gelu_done, NB * l)
                sp.dma_start(s.W1[:], d["L0_ffn_W1"][l]).then_inc(s.w1_in, 16)
                if l:
                    sp.wait_ge(s.x_ready, NB * l + NB)
                sp.dma_start(s.W2[:, 0:2], d["L0_ffn_W2"][l, 0:2 * P].rearrange("(c p) n -> p c n", p=P)).then_inc(s.w2_in, 16)
                sp.dma_start(s.W2[0:FF - 2 * P, 2], d["L0_ffn_W2"][l, 2 * P:FF]).then_inc(s.w2_in, 16)
                if l == 0:
                    load_chunks(0, range(RAW, WCHUNKS))
            for loaded in s.wqkv_in:
                sp.wait_ge(loaded, 16 * WCHUNKS // RAW * DEPTH)
            sp.wait_ge(s.wo_in, 16 * DEPTH)
            sp.wait_ge(s.w1_in, 16 * DEPTH)
            sp.wait_ge(s.w2_in, 32 * DEPTH)

        @block.tensor
        def _(pe):
            def body(step):
                n, f, t, u = step.n, step.n + 1, step.n - 1, step.n - 2
                pf, pa = 1 - step.odd, step.odd

                def take_spare(use):
                    bank, uses = step.spare(use)
                    wait(pe, s.spare_free[bank], uses)
                    return ps[:, SPARE[bank]]

                def give_spare(use, last):
                    last.then_inc(s.spare_full[step.spare(use)[0]], 1)

                def read_out(bank_uses):
                    bank, uses = bank_uses
                    pe.wait_ge(s.spare_free[bank], uses + 1)

                def transpose_qk(item, which):
                    tt, four = which
                    bank = take_spare(("tr", which))
                    pe.wait_ge(s.dve_norm, TT * item + tt + 1)
                    for i in range(4):
                        c = four * 4 + i
                        last = nc.tensor.transpose(bank[:, i * P:(i + 1) * P], s.w[:, tt, c * P:(c + 1) * P], g.ident[:])
                    give_spare(("tr", which), last)

                for slot in range(SLOTS):
                    if step.attn:
                        h = slot
                        bank, r, pair = S_BANK[h % 2], DB * (h % 2), h // 2
                        if h == 0:
                            read_out(step.spare_of_before(("tr", (1, 0))))
                            read_out(step.spare_of_before(("tr", (1, 2))))
                        if h == HB // 2:
                            read_out(step.spare(("tr", (1, 1))))
                            read_out(step.spare(("tr", (1, 3))))
                        wait(pe, s.exp_done, HB * n + h - 1)
                        q, k = s.qkT[r:r + DB, pa, pair], s.qkT[r:r + DB, pa, INNER // P + pair]
                        nc.tensor.matmul(ps[:, bank, 0:TT * KEYS], g.ident_bf[:], g.mask_bf[:], start=True, stop=False, skip_group_check=True)
                        nc.tensor.matmul(ps[:, bank, WIN:KEYS], q[:, 0:P], k[:, 0:P], start=False, stop=False, skip_group_check=True)
                        nc.tensor.matmul(ps[:, bank, KEYS:2 * KEYS], q[:, P:NT], k[:, P - WIN:NT], start=False, stop=True,
                                         skip_group_check=True).then_inc(s.s_done, 1)
                    if step.front is not None and slot < len(PIECES):
                        tt, c = PIECES[slot]
                        N = len(PIECES)
                        if slot == 0:
                            pe.wait_ge(s.xs_ready, f + 1)
                        if tt == 0:
                            pe.wait_ge(s.w_ready, WCHUNKS * step.front[0] + c + 1)
                        wait(pe, s.act_front, N * f + slot - 1)
                        if slot >= 2:
                            wait(pe, s.dve_uv, N_QK * f + min(slot - 1, N_QK))
                        rows, cols = slice(tt * P, (tt + 1) * P), slice(c * 512, (c + 1) * 512)
                        nc.tensor.matmul(ps[:, F_BANK[slot % 2]], s.xlo[:, pf, rows], s.Whi[:, cols], start=True, stop=False)
                        nc.tensor.matmul(ps[:, F_BANK[slot % 2]], s.xhi[:, pf, rows], s.Wlo[:, cols], start=False, stop=False)
                        nc.tensor.matmul(ps[:, F_BANK[slot % 2]], s.xhi[:, pf, rows], s.Whi[:, cols], start=False, stop=True).then_inc(s.proj_done, 1)
                    item, k = started(step, slot, T_LAG)
                    if k is not None:
                        pe.wait_ge(s.exp_done, HB * item + k + 1)
                        wait(pe, s.pt_ready, HB * item + k)
                        nc.tensor.transpose(ps[:, T_BANK, 0:P], s.Pr[:, k % 4, 0:P], g.ident[:])
                        nc.tensor.transpose(ps[:, T_BANK, P:2 * P], s.Pr[:, k % 4, OWN], g.ident[:]).then_inc(s.t_done, 1)
                    if step.tail is not None:
                        lt = step.tail[0]
                        for tt, half in OUT_SLOT.get(slot, ()):
                            use = ("out", (tt, half))
                            bank = take_spare(use)
                            pe.wait_ge(s.onorm, 4 * t + 2 * half + 2)
                            for i in range(4):
                                c = half * 4 + i
                                last = nc.tensor.transpose(bank[:, i * P:(i + 1) * P], s.o[:, tt, c * P:(c + 1) * P], g.ident[:])
                            give_spare(use, last)
                        if slot == WO_SLOT:
                            bank = take_spare(("wo", 0))
                            for tt in range(TT):
                                read_out(step.spare(("out", (tt, 1))))
                            pe.wait_ge(s.wo_in, 16 * lt + 16)
                            for c in range(INNER // P):
                                last = nc.tensor.matmul(bank[:, 0:NT], s.Wo[:, c], s.oT[:, c], start=c == 0, stop=c == INNER // P - 1)
                            give_spare(("wo", 0), last)
                        if slot == XT_SLOT:
                            bank = take_spare(("xt", 0))
                            pe.wait_ge(s.shifted, t + 1)
                            for tt in range(TT):
                                last = nc.tensor.transpose(bank[:, tt * P:(tt + 1) * P], s.xs2[:, tt * P:(tt + 1) * P], g.ident[:])
                            give_spare(("xt", 0), last)
                        if slot == XN_SLOT:
                            bank = take_spare(("xn", 0))
                            pe.wait_ge(s.ff.normed, t + 1)
                            for tt in range(TT):
                                last = nc.tensor.transpose(bank[:, tt * P:(tt + 1) * P], s.ff.xn[:, tt], g.ident[:])
                            give_spare(("xn", 0), last)
                    if step.ffn is not None:
                        lu = step.ffn[0]
                        if slot in W1_SLOT:
                            c = W1_SLOT[slot]
                            c0, width = FF_CHUNKS[c]
                            bank = take_spare(("w1", c))
                            if c == 0:
                                pe.wait_ge(s.w1_in, 16 * lu + 16)
                                read_out(step.spare_of_before(("xn", 0)))
                            for half in range(2):
                                last = nc.tensor.matmul(bank[0:width, half * NT:(half + 1) * NT],
                                                        s.W1[:, half * FF + c0:half * FF + c0 + width], s.xnT[:], start=True, stop=True)
                            give_spare(("w1", c), last)
                        if slot == W2_SLOT:
                            bank = take_spare(("w2", 0))
                            pe.wait_ge(s.w2_in, 32 * lu + 32)
                            pe.wait_ge(s.hg_ready, u + 1)
                            for c, (_, width) in enumerate(FF_CHUNKS):
                                last = nc.tensor.matmul(bank[:, 0:NT], s.W2[0:width, c], s.ha[0:width, c], start=c == 0, stop=c == 2)
                            give_spare(("w2", 0), last)
                    item, k = started(step, slot, PV_LAG)
                    if k is not None:
                        pe.wait_ge(s.pt_ready, HB * item + k + 1)
                        pe.wait_ge(s.before_ready, HB * item + k + 1)
                        if k == 0:
                            pe.wait_ge(s.act_front, len(PIECES) * (item + 1))
                        if k % 4 == 0:
                            wait(pe, s.onorm, 4 * item + k // 4)
                        pt, v, col = s.PT[:, k % 4], s.V[:, pa if slot >= PV_LAG else 1 - pa], k * DB
                        out = ps[:, PV_BANK].rearrange("p (h t e) -> p h t e", h=4, t=TT)[:, k % 4]
                        nc.tensor.matmul(out[:, 0], pt[:, 0:P], v[:, 0, col:col + DB], start=True, stop=True)
                        nc.tensor.matmul(out[:, 1], pt[:, P:2 * P], v[:, 1, col:col + DB], start=True, stop=False, skip_group_check=True)
                        nc.tensor.matmul(out[0:WIN, 1], pt[P - WIN:P, 2 * P:], v[P - WIN:P, 0, col:col + DB], start=False, stop=True,
                                         skip_group_check=True).then_inc(s.pv_done, 1)
                    if step.attn and slot in LATE_SLOT:
                        transpose_qk(n, LATE_SLOT[slot])
                    if step.front is not None and slot in TRANSPOSE_SLOT:
                        transpose_qk(f, TRANSPOSE_SLOT[slot])

            phase_b_steps(pe, body)

        @block.scalar
        def _(act):
            act.wait_ge(s.zeroed, 1)

            def body(step):
                n, f, t, u = step.n, step.n + 1, step.n - 1, step.n - 2
                pf, pa = 1 - step.odd, step.odd

                def full_spare(use):
                    bank, uses = step.spare(use)
                    act.wait_ge(s.spare_full[bank], uses + 1)
                    return bank

                def store_qk(parity, which):
                    tt, four = which
                    bank = full_spare(("tr", which))
                    nc.scalar.activation(s.qkT[:, parity, four * 4:four * 4 + 4, tt * P:(tt + 1) * P],
                                         ps[:, SPARE[bank]].rearrange("p (c t) -> p c t", c=4), ACT.Copy).then_inc(s.spare_free[bank], 1)

                for slot in range(SLOTS):
                    if step.convert:
                        for c in ((0, 1) if slot == 0 else (slot + 1,) if slot < WCHUNKS - 1 else ()):
                            act.wait_ge(s.wqkv_in[c % RAW], 16 * (WCHUNKS // RAW) * step.front[0] + 16 * (c // RAW) + 16)
                            if c == 0:
                                wait(act, s.proj_done, len(PIECES) * f)
                            nc.scalar.activation(s.Whi[:, c * 512:(c + 1) * 512], s.Wraw[:, c % RAW], ACT.Copy).then_inc(s.whi_done, 1)
                    if step.front is not None and slot < len(PIECES):
                        tt, c = PIECES[slot]
                        act.wait_ge(s.proj_done, len(PIECES) * f + slot + 1)
                        if c < 4:
                            wait(act, s.dve_red, N_QK * f + slot - 1)
                            nc.scalar.activation(s.sq[:, slot % 2], ps[:, F_BANK[slot % 2]], ACT.Square).then_inc(s.act_front, 1)
                        else:
                            if slot == N_QK:
                                wait(act, s.pv_done, HB * (f - 1))
                            nc.scalar.activation(s.V[:, pf, tt, (c - 4) * 512:(c - 3) * 512], ps[:, F_BANK[slot % 2]],
                                                 ACT.Copy).then_inc(s.act_front, 1)
                    item, k = started(step, slot, T_LAG)
                    if k is not None:
                        act.wait_ge(s.t_done, HB * item + k + 1)
                        wait(act, s.pv_done, HB * item + k - 3)
                        nc.scalar.activation(s.PT[:, k % 4, 0:2 * P], ps[:, T_BANK, 0:2 * P], ACT.Copy).then_inc(s.pt_ready, 1)
                    if step.attn:
                        h = slot
                        bank = S_BANK[h % 2]
                        act.wait_ge(s.max_done, HB * n + h + 1)
                        wait(act, s.t_done, HB * n + h - 3)
                        wait(act, s.before_ready, HB * n + h - 3)
                        nc.scalar.activation(s.Pr[:, h % 4, 0:P], ps[:, bank, WIN:KEYS], ACT.Exp,
                                             bias=s.nm[:, h, 0:1], accum_out=s.ssum[:, h, 0:1])
                        nc.scalar.activation(s.Pr[:, h % 4, P:], ps[:, bank, KEYS:2 * KEYS], ACT.Exp,
                                             bias=s.nm[:, h, 1:2], accum_out=s.ssum[:, h, 1:2]).then_inc(s.exp_done, 1)
                    if step.tail is not None:
                        for tt, half in OUT_SLOT.get(slot, ()):
                            bank = full_spare(("out", (tt, half)))
                            nc.scalar.activation(s.oT[:, half * 4:half * 4 + 4, tt * P:(tt + 1) * P],
                                                 ps[:, SPARE[bank]].rearrange("p (c t) -> p c t", c=4), ACT.Copy).then_inc(s.spare_free[bank], 1)
                        if slot == XN_SLOT:
                            bank = full_spare(("xn", 0))
                            act.wait_ge(s.lnp_ready, t + 1)
                            nc.scalar.activation(s.xnT[:], ps[:, SPARE[bank], 0:NT], ACT.Identity, bias=s.lnp[:, 1:2],
                                                 scale=s.lnp[:, 0:1]).then_inc(s.spare_free[bank], 1)
                    if step.ffn is not None:
                        if slot in W1_SLOT:
                            c = W1_SLOT[slot]
                            width = FF_CHUNKS[c][1]
                            act.wait_ge(s.lp_ready, u + 1)
                            bank = full_spare(("w1", c))
                            nc.scalar.activation(s.hgate[0:width, c], ps[0:width, SPARE[bank], NT:2 * NT], ACT.Identity, bias=s.lp[0:width, 4 + c:5 + c])
                            nc.scalar.activation(s.ha[0:width, c], ps[0:width, SPARE[bank], 0:NT], ACT.Identity,
                                                 bias=s.lp[0:width, 1 + c:2 + c]).then_inc(s.spare_free[bank], 1)
                        if slot == GELU_SLOT:
                            for c in range(3):
                                b, uses = step.spare(("w1", c))
                                act.wait_ge(s.spare_free[b], uses + 1)
                            nc.scalar.activation(s.hgate[:], s.hgate[:], ACT.Gelu).then_inc(s.gelu_done, 1)
                    if step.attn and slot in LATE_SLOT:
                        store_qk(pa, LATE_SLOT[slot])
                    if step.front is not None and slot in TRANSPOSE_SLOT:
                        if slot == min(TRANSPOSE_SLOT):
                            wait(act, s.s_done, HB * (f - 1))
                        store_qk(pf, TRANSPOSE_SLOT[slot])

            phase_b_steps(act, body)

        @block.vector
        def _(dve):
            for buffer in (s.xhi, s.xlo):
                nc.vector.memset(buffer[:].bitcast(F32), 0.0)
            for buffer in (s.xs2, s.ha):
                nc.vector.memset(buffer[:], 0.0)
            nc.vector.memset(s.hgate[:], 0.0).then_inc(s.zeroed, 1)
            dve.wait_ge(s.zeroed, 1)
            dve.sem_inc(s.x_ready, NB)
            lower, upper = slice(0, P // 2), slice(P // 2, P)

            def split_input(item, parity, src):
                dve.wait_ge(s.x_ready, item + 1)
                wait(dve, s.proj_done, len(PIECES) * (item - 1))
                own, shifted = g.xT[lower, bass.ds(src, NT)], g.xT[upper, bass.ds(src, NT - 1)]
                nc.vector.tensor_scalar_mul(s.xhi[lower, parity], own, 1.0)
                nc.vector.tensor_scalar_mul(s.xhi[upper, parity, 1:NT], shifted, 1.0).then_inc(s.xhi_done, 1)
                dve.wait_ge(s.xhi_done, item + 1)
                nc.vector.tensor_tensor(s.xlo[lower, parity], own, s.xhi[lower, parity].bitcast(F32), ALU.subtract)
                nc.vector.tensor_tensor(s.xlo[upper, parity, 1:NT], shifted, s.xhi[upper, parity, 1:NT].bitcast(F32), ALU.subtract).then_inc(s.xs_ready, 1)

            def body(step):
                n, f, t, u = step.n, step.n + 1, step.n - 1, step.n - 2

                def full_spare(use):
                    bank, uses = step.spare(use)
                    dve.wait_ge(s.spare_full[bank], uses + 1)
                    return bank

                def known(value):
                    return value if isinstance(value, int) else dve.snap(value)

                if step.front is not None:
                    lf = known(step.front[0])
                    next_src = known((step.front[1] + 1) % NB * NT)
                if step.tail is not None:
                    lt, dst = known(step.tail[0]), known(step.tail[1] * NT)
                    x_lower, x_upper, x_all = g.xT[lower, bass.ds(dst, NT)], g.xT[upper, bass.ds(dst, NT - 1)], g.xT[:, bass.ds(dst, NT)]
                if step.ffn is not None:
                    lu, end = known(step.ffn[0]), known(step.ffn[1] * NT)
                    x_end = g.xT[:, bass.ds(end, NT)]
                    nc.vector.tensor_scalar_mul(s.lp[:], g.lparam[:, bass.ds(lu, 1), 2:9].rearrange("p a k -> p (a k)"), 1.0).then_inc(s.lp_ready, 1)
                for slot in range(SLOTS):
                    if step.convert:
                        for c in ((0, 1) if slot == 0 else (slot + 1,) if slot < WCHUNKS - 1 else ()):
                            cols = slice(c * 512, (c + 1) * 512)
                            dve.wait_ge(s.whi_done, WCHUNKS * lf + c + 1)
                            nc.vector.tensor_tensor(s.Wlo[:, cols], s.Wraw[:, c % RAW], s.Whi[:, cols].bitcast(F32), ALU.subtract).then_inc(s.w_ready, 1)
                    item, k = started(step, slot, PV_LAG + 1)
                    if k is not None and k % 4 == 3:
                        i = k // 4
                        heads = slice(4 * i, 4 * i + 4)
                        dve.wait_ge(s.pv_done, HB * item + k + 1)
                        nc.vector.reciprocal(s.rinv[:, heads], s.ssum[:, heads]).then_inc(s.rinv_ready, 1)
                        if i == 0 and step.tail is not None:
                            full_spare(("out", (0, 1)))
                            full_spare(("out", (1, 1)))
                        dve.wait_ge(s.rinv_ready, 4 * item + i + 1)
                        pv = ps[:, PV_BANK].rearrange("p (h t e) -> p h t e", h=4, t=TT)
                        for tt in range(TT):
                            last = nc.vector.tensor_tensor(s.o[:, tt, i * 4 * DB:(i + 1) * 4 * DB].rearrange("p (h e) -> p h e", e=DB),
                                                           pv[:, :, tt], s.rinv[:, heads, tt:tt + 1].broadcast_to((P, 4, DB)), ALU.mult)
                        last.then_inc(s.onorm, 1)
                    if step.attn:
                        h = slot
                        dve.wait_ge(s.s_done, HB * n + h + 1)
                        nc.vector.tensor_reduce(s.nm[:, h], ps[:, S_BANK[h % 2], 0:TT * KEYS].rearrange("p (t k) -> p t k", t=TT),
                                                AX.X, ALU.max, negate=True).then_inc(s.max_done, 1)
                    item, k = started(step, slot, T_LAG)
                    if k is not None:
                        dve.wait_ge(s.exp_done, HB * item + k + 1)
                        wait(dve, s.pv_done, HB * item + k - 3)
                        nc.vector.transpose(s.PT[P - WIN:P, k % 4, 2 * P:], s.Pr[0:WIN, k % 4, BEFORE]).then_inc(s.before_ready, 1)
                    if step.front is not None and slot < N_QK:
                        tt, c = PIECES[slot]
                        which = c // 2
                        dve.wait_ge(s.act_front, len(PIECES) * f + slot + 1)
                        if step.attn and c == 0:
                            for use in ((0, 1), (0, 3)) if tt == 0 else ((1, 1), (1, 3)):
                                b, uses = step.spare_of_before(("tr", use)) if tt == 0 else step.spare(("tr", use))
                                dve.wait_ge(s.spare_full[b], uses + 1)
                        wait(dve, s.pool_add, N_QK * f + slot - 3)
                        raw = ps[:, F_BANK[slot % 2]].rearrange("p (h z e) -> p h z e", z=2, e=DB // 2)
                        turned = s.vt[:, slot % 4].rearrange("p (h z e) -> p h z e", z=2, e=DB // 2)
                        sin = g.rotab[:, bass.ds(lf, 1), 2 * which + 1, tt]
                        nc.vector.tensor_tensor(s.w[:, tt, c * 512:(c + 1) * 512].rearrange("p (h e) -> p h e", e=DB),
                                                ps[:, F_BANK[slot % 2]].rearrange("p (h e) -> p h e", e=DB),
                                                g.rotab[:, bass.ds(lf, 1), 2 * which, tt].broadcast_to((P, 8, DB)), ALU.mult)
                        for z in range(2):
                            last = nc.vector.tensor_tensor(turned[:, :, z], raw[:, :, 1 - z],
                                                           sin[:, :, z * (DB // 2):(z + 1) * (DB // 2)].broadcast_to((P, 8, DB // 2)), ALU.mult)
                        last.then_inc(s.dve_uv, 1)
                        nc.vector.tensor_reduce(s.ss[:, tt, c * 8:(c + 1) * 8], s.sq[:, slot % 2].rearrange("p (h e) -> p h e", e=DB),
                                                AX.X, ALU.add).then_inc(s.dve_red, 1)
                        if c == 3:
                            dve.wait_ge(s.dve_red, N_QK * f + slot + 1)
                            nc.vector.tensor_scalar_max(s.ssm[:, tt], s.ss[:, tt], 1e-24).then_inc(s.clamp_done, 1)
                    if step.tail is not None:
                        if slot == RES_SLOT:
                            bank = full_spare(("wo", 0))
                            nc.vector.tensor_tensor(x_all, ps[:, SPARE[bank], 0:NT], x_all, ALU.add).then_inc(s.spare_free[bank], 1)
                            dve.wait_ge(s.spare_free[bank], step.spare(("wo", 0))[1] + 1)
                            nc.vector.tensor_scalar_mul(s.xs2[lower], x_lower, 1.0)
                            nc.vector.tensor_scalar_mul(s.xs2[upper, 1:NT], x_upper, 1.0).then_inc(s.shifted, 1)
                        if slot == STATS_SLOT:
                            bank = full_spare(("xt", 0))
                            nc.vector.tensor_copy(s.xtok[:], ps[:, SPARE[bank], 0:NT].rearrange("p (t e) -> p t e", t=TT)).then_inc(s.spare_free[bank], 1)
                            dve.wait_ge(s.spare_free[bank], step.spare(("xt", 0))[1] + 1)
                            layernorm_stats(nc, dve, s.ff, s.xtok, t)
                        if slot == NORMED_SLOT:
                            layernorm_apply(nc, dve, s.ff, s.xtok, t)
                            nc.vector.tensor_scalar_mul(s.lnp[:], g.lparam[:, bass.ds(lt, 1), 0:2].rearrange("p a k -> p (a k)"), 1.0).then_inc(s.lnp_ready, 1)
                    if step.front is not None and slot in NORM_SLOT:
                        tt = NORM_SLOT[slot]
                        dve.wait_ge(s.pool_r, TT * f + tt + 1)
                        dve.wait_ge(s.pool_add, N_QK * f + 4 * tt + 4)
                        rows = s.w[:, tt].rearrange("p (h e) -> p h e", e=DB)
                        nc.vector.tensor_tensor(rows, rows, s.rn[:, tt].rearrange("p (h o) -> p h o", o=1).broadcast_to((P, 2 * HB, DB)),
                                                ALU.mult).then_inc(s.dve_norm, 1)
                    if step.front is not None and slot == SPLIT_SLOT:
                        split_input(f + 1, step.odd, next_src)
                    if step.ffn is not None and slot == END_SLOT:
                        bank = full_spare(("w2", 0))
                        nc.vector.scalar_tensor_tensor(out=x_end, in0=ps[:, SPARE[bank], 0:NT], scalar=s.lp[:, 0:1], in1=x_end,
                                                       op0=ALU.add, op1=ALU.add).then_inc(s.spare_free[bank], 1)
                        dve.wait_ge(s.spare_free[bank], step.spare(("w2", 0))[1] + 1)
                        dve.sem_inc(s.x_ready, 1)

            split_input(0, 0, 0)
            phase_b_steps(dve, body)

        @block.gpsimd
        def _(pool):
            def body(step):
                f, t, u = step.n + 1, step.n - 1, step.n - 2
                for slot in range(SLOTS):
                    if step.front is not None and slot < N_QK:
                        tt, c = PIECES[slot]
                        pool.wait_ge(s.dve_uv, N_QK * f + slot + 1)
                        rows = s.w[:, tt, c * 512:(c + 1) * 512]
                        nc.gpsimd.tensor_tensor(rows, rows, s.vt[:, slot % 4], ALU.add).then_inc(s.pool_add, 1)
                    if step.front is not None and slot in POWER_SLOT:
                        tt = POWER_SLOT[slot]
                        pool.wait_ge(s.clamp_done, TT * f + tt + 1)
                        nc.gpsimd.tensor_tensor(s.rn[:, tt], s.ssm[:, tt], g.neg_half[:], ALU.pow).then_inc(s.pool_r, 1)
                    if step.ffn is not None and slot == GELU_SLOT:
                        pool.wait_ge(s.gelu_done, u + 1)
                        nc.gpsimd.tensor_tensor(s.ha[:], s.ha[:], s.hgate[:], ALU.mult).then_inc(s.hg_ready, 1)
                    if step.tail is not None and slot == STATS_SLOT:
                        layernorm_pool(nc, pool, s.ff, g, t)

            phase_b_steps(pool, body)




def phase_c(nc, g, d, ps, out):
    with ExitStack() as stack:
        s = Store(nc, stack, "c")
        s.Win = s.sb("Win", [P, 2 * CH]); s.Wx = s.sb("Wx", [P, CC, XD]); s.Wdt = s.sb("Wdt", [RANK, CH]); s.Wout = s.sb("Wout", [P, CC, P])
        s.sel = s.sb("sel", [XD, 2 * NS, P])
        s.md0 = s.sb("md0", [P, 6]); s.md = s.sb("md", [P, 6])
        s.x3T = s.sb("x3T", [P, NT]); s.x3tok = s.sb("x3tok", [P, TT, P]); s.hT = s.sb("hT", [P, NT]); s.hT2 = s.sb("hT2", [P, NT])
        s.xp = s.sb("xp", [P, CC, TAPS - 1 + NT]); s.cv = s.sb("cv", [P, CC, NT]); s.h = s.sb("h", [P, CC, NT]); s.sr = s.sb("sr", [P, CC, NT])
        s.xd = s.sb("xd", [XD, NT]); s.zb = s.sb("zb", [P, CC, NT]); s.za = s.sb("za", [P, CC, NT]); s.delta = s.sb("delta", [P, CC, NT]); s.du = s.sb("du", [P, CC, NT])
        s.dA = s.sb("dA", [P, CC, NS, NT]); s.bu = s.sb("bu", [P, CC, NS, NT])
        s.y = s.sb("y", [P, CC, NT]); s.x4T = s.sb("x4T", [P, NT]); s.x4tok = s.sb("x4tok", [P, TT, P]); s.tmp = s.sb("tmp", [P, NT]); s.x5T = s.sb("x5T", [P, NT]); s.xout = s.sb("xout", [P, TT, P])
        s.l1 = LayerNorm(s, "l1"); s.l2 = LayerNorm(s, "l2")
        s.w_in, s.zeroed, s.md_ready, s.x3_ready, s.x3_full, s.x3tok_ready, s.h_full, s.hT_ready = s.sems("w_in zeroed md_ready x3_ready x3_full x3tok_ready h_full hT_ready")
        s.in_full, s.res_ready, s.xp_ready, s.conv_step, s.h_ready, s.xd_full, s.xd_ready, s.dl_full = s.sems("in_full res_ready xp_ready conv_step h_ready xd_full xd_ready dl_full")
        s.zb_ready, s.abs_done, s.exp_done, s.sp_done, s.delta_ready, s.du_ready, s.dA_ready, s.b_full = s.sems("zb_ready abs_done exp_done sp_done delta_ready du_ready dA_ready b_full")
        s.bu_ready, s.scan_done, s.c_full, s.yc_ready, s.y_full, s.y1_ready, s.y_ready, s.op_full = s.sems("bu_ready scan_done c_full yc_ready y_full y1_ready y_ready op_full")
        s.x4_ready, s.x4_full, s.x4tok_ready, s.h2_full, s.hT2_ready, s.lin_full, s.tmp_ready, s.x5_ready = s.sems("x4_ready x4_full x4tok_ready h2_full hT2_ready lin_full tmp_ready x5_ready")
        s.out_full, s.xout_ready, s.stored = s.sems("out_full xout_ready stored")
        block = stack.enter_context(nc.Block())
        PAIRS = NS // 2
        B_BANK, C_BANK, Y_BANK = (4, 5), (6, 7), 2

        @block.sync
        def _(sp):
            for dst, src in ((s.Win[:], d["L1_attn_in_proj_w"]), (s.Wx[:], d["L1_attn_x_proj_w"].rearrange("(c p) n -> p c n", p=P)),
                             (s.Wdt[:], d["L1_attn_dt_proj_w"]), (s.Wout[:], d["L1_attn_out_proj_w"].rearrange("(c p) n -> p c n", p=P)),
                             (s.sel[:], d["sel"])):
                sp.dma_start(dst, src).then_inc(s.w_in, 16)
            with sp.Fori(0, NB) as n:
                sp.wait_ge(s.xout_ready, n + 2)
                sp.dma_start(out[bass.ds(n, 1)].rearrange("b (t p) e -> p (b t) e", p=P), s.xout[:]).then_inc(s.stored, 16)
            sp.wait_ge(s.stored, 16 * NB + 16)

        @block.vector
        def _(dve):
            nc.vector.memset(s.dA[:], 0.0)
            nc.vector.memset(s.xp[:], 0.0).then_inc(s.zeroed, 1)
            dve.wait_ge(s.zeroed, 1)
            with dve.Fori(0, NB) as n:
                at = dve.snap(n * NT)
                dve.wait_ge(s.xout_ready, n + 1)
                nc.vector.tensor_scalar_mul(s.md0[:], g.mod[:, 0, bass.ds(n, 1), :].rearrange("p a k -> p (a k)"), 1.0)
                nc.vector.tensor_scalar_mul(s.md[:], g.mod[:, 1, bass.ds(n, 1), :].rearrange("p a k -> p (a k)"), 1.0).then_inc(s.md_ready, 1)
                dve.wait_ge(s.md_ready, n + 1)
                nc.vector.scalar_tensor_tensor(out=s.x3T[:], in0=g.xT[:, bass.ds(at, NT)], scalar=s.md0[:, 5:6], in1=g.x2T[:, bass.ds(at, NT)],
                                               op0=ALU.mult, op1=ALU.add).then_inc(s.x3_ready, 1)
                dve.wait_ge(s.x3_full, n + 1)
                nc.vector.tensor_copy(s.x3tok[:], ps[:, 0, 0:NT].rearrange("p (t e) -> p t e", t=TT)).then_inc(s.x3tok_ready, 1)
                dve.wait_ge(s.x3tok_ready, n + 1)
                layernorm_stats(nc, dve, s.l1, s.x3tok, n)
                layernorm_apply(nc, dve, s.l1, s.x3tok, n)
                dve.wait_ge(s.in_full, n + 1)
                nc.vector.tensor_copy(s.xp[:, :, TAPS - 1:], ps[:, 1].rearrange("p (c t) -> p c t", c=CC)).then_inc(s.xp_ready, 1)
                dve.wait_ge(s.xp_ready, n + 1)
                for k in range(TAPS):
                    for c in range(CC):
                        tap, w = s.xp[:, c, k:k + NT], g.conv_w[:, c, k:k + 1]
                        if k == 0:
                            last = nc.vector.tensor_scalar(s.cv[:, c], tap, w, g.conv_b[:, c:c + 1], ALU.mult, ALU.add)
                        else:
                            last = nc.vector.scalar_tensor_tensor(out=s.cv[:, c], in0=tap, scalar=w, in1=s.cv[:, c], op0=ALU.mult, op1=ALU.add)
                    last.then_inc(s.conv_step, 1)
                    dve.wait_ge(s.conv_step, TAPS * n + k + 1)
                dve.wait_ge(s.xd_full, n + 1)
                nc.vector.tensor_copy(s.xd[:], ps[0:XD, 2, 0:NT]).then_inc(s.xd_ready, 1)
                dve.wait_ge(s.dl_full, n + 1)
                for c in range(CC):
                    last = nc.vector.tensor_scalar_add(s.zb[:, c], ps[:, 3, c * NT:(c + 1) * NT], g.dt_b[:, c:c + 1])
                last.then_inc(s.zb_ready, 1)
                dve.wait_ge(s.sp_done, n + 1)
                nc.vector.scalar_tensor_tensor(out=s.delta[:], in0=s.zb[:], scalar=0.0, in1=s.za[:], op0=ALU.max, op1=ALU.add).then_inc(s.delta_ready, 1)
                dve.wait_ge(s.delta_ready, n + 1)
                nc.vector.tensor_tensor(s.du[:], s.delta[:], s.h[:], ALU.mult).then_inc(s.du_ready, 1)
                dve.wait_ge(s.du_ready, n + 1)
                for i in range(PAIRS):
                    dve.wait_ge(s.b_full, PAIRS * n + i + 1)
                    for c in range(CC):
                        last = nc.vector.tensor_tensor(s.bu[:, c, 2 * i:2 * i + 2], s.du[:, c:c + 1].broadcast_to((P, 2, NT)),
                                                       ps[:, B_BANK[i % 2]].rearrange("p (n t) -> p n t", n=2), ALU.mult)
                    last.then_inc(s.bu_ready, 1)
                dve.wait_ge(s.dA_ready, CC * (n + 1))
                dve.wait_ge(s.bu_ready, PAIRS * n + PAIRS)
                for c in range(CC):
                    for k in range(2):
                        half = slice(k * NS // 2, (k + 1) * NS // 2)
                        run = s.bu[:, c, half].rearrange("p n t -> p (n t)")
                        last = nc.vector.tensor_tensor_scan(run, s.dA[:, c, half].rearrange("p n t -> p (n t)"), run, 0.0, ALU.mult, ALU.add)
                last.then_inc(s.scan_done, 1)
                dve.wait_ge(s.scan_done, n + 1)
                for i in range(PAIRS):
                    dve.wait_ge(s.c_full, PAIRS * n + i + 1)
                    for c in range(CC):
                        both = s.bu[:, c, 2 * i:2 * i + 2]
                        last = nc.vector.tensor_tensor(both, both, ps[:, C_BANK[i % 2]].rearrange("p (n t) -> p n t", n=2), ALU.mult)
                    last.then_inc(s.yc_ready, 1)
                dve.wait_ge(s.y_full, n + 1)
                for c in range(CC):
                    last = nc.vector.scalar_tensor_tensor(out=s.y[:, c], in0=s.h[:, c], scalar=g.D[:, c:c + 1], in1=ps[:, Y_BANK, c * NT:(c + 1) * NT],
                                                          op0=ALU.mult, op1=ALU.add)
                last.then_inc(s.y1_ready, 1)
                dve.wait_ge(s.y1_ready, n + 1)
                nc.vector.tensor_tensor(s.y[:], s.y[:], s.sr[:], ALU.mult).then_inc(s.y_ready, 1)
                dve.wait_ge(s.op_full, n + 1)
                nc.vector.scalar_tensor_tensor(out=s.x4T[:], in0=ps[:, 0, 0:NT], scalar=s.md[:, 2:3], in1=s.x3T[:],
                                               op0=ALU.mult, op1=ALU.add).then_inc(s.x4_ready, 1)
                dve.wait_ge(s.x4_full, n + 1)
                nc.vector.tensor_copy(s.x4tok[:], ps[:, 1, 0:NT].rearrange("p (t e) -> p t e", t=TT)).then_inc(s.x4tok_ready, 1)
                dve.wait_ge(s.x4tok_ready, n + 1)
                layernorm_stats(nc, dve, s.l2, s.x4tok, n)
                layernorm_apply(nc, dve, s.l2, s.x4tok, n)
                dve.wait_ge(s.lin_full, n + 1)
                nc.vector.tensor_scalar(s.tmp[:], ps[:, 0, 0:NT], g.blin[:], s.md[:, 5:6], ALU.add, ALU.mult).then_inc(s.tmp_ready, 1)
                dve.wait_ge(s.tmp_ready, n + 1)
                nc.vector.tensor_tensor(s.x5T[:], s.tmp[:], s.x4T[:], ALU.add).then_inc(s.x5_ready, 1)

        @block.gpsimd
        def _(pool):
            with pool.Fori(0, NB) as n:
                layernorm_pool(nc, pool, s.l1, g, n)
                layernorm_pool(nc, pool, s.l2, g, n)

        @block.scalar
        def _(act):
            act.wait_ge(s.zeroed, 1)
            act.sem_inc(s.xout_ready, 1)
            act.sem_inc(s.stored, 16)
            with act.Fori(0, NB) as n:
                act.wait_ge(s.h_full, n + 1)
                act.wait_ge(s.md_ready, n + 1)
                nc.scalar.activation(s.hT[:], ps[:, 0, NT:2 * NT], ACT.Identity, bias=s.md[:, 0:1], scale=s.md[:, 1:2]).then_inc(s.hT_ready, 1)
                act.wait_ge(s.in_full, n + 1)
                nc.scalar.activation(s.sr[:], ps[:, 3].rearrange("p (c t) -> p c t", c=CC), ACT.Silu).then_inc(s.res_ready, 1)
                act.wait_ge(s.conv_step, TAPS * n + TAPS)
                nc.scalar.activation(s.h[:], s.cv[:], ACT.Silu).then_inc(s.h_ready, 1)
                act.wait_ge(s.zb_ready, n + 1)
                nc.scalar.activation(s.za[:], s.zb[:], ACT.Abs).then_inc(s.abs_done, 1)
                act.wait_ge(s.abs_done, n + 1)
                nc.scalar.activation(s.za[:], s.za[:], ACT.Exp, scale=-1.0).then_inc(s.exp_done, 1)
                act.wait_ge(s.exp_done, n + 1)
                nc.scalar.activation(s.za[:], s.za[:], ACT.Ln, bias=1.0).then_inc(s.sp_done, 1)
                act.wait_ge(s.delta_ready, n + 1)
                for c in range(CC):
                    for i in range(NS):
                        last = nc.scalar.activation(s.dA[:, c, i, 1:NT], s.delta[:, c, 1:NT], ACT.Exp, scale=g.A[:, c, i:i + 1])
                    last.then_inc(s.dA_ready, 1)
                act.wait_ge(s.h2_full, n + 1)
                nc.scalar.activation(s.hT2[:], ps[:, 1, NT:2 * NT], ACT.Identity, bias=s.md[:, 3:4], scale=s.md[:, 4:5]).then_inc(s.hT2_ready, 1)
                act.wait_ge(s.out_full, n + 1)
                act.wait_ge(s.stored, 16 * n + 16)
                nc.scalar.activation(s.xout[:], ps[:, 0, NT:2 * NT].rearrange("p (t e) -> p t e", t=TT), ACT.Copy).then_inc(s.xout_ready, 1)

        @block.tensor
        def _(pe):
            pe.wait_ge(s.w_in, 16 * 5)
            with pe.Fori(0, NB) as n:
                pe.wait_ge(s.x3_ready, n + 1)
                for tt in range(TT):
                    last = nc.tensor.transpose(ps[:, 0, tt * P:(tt + 1) * P], s.x3T[:, tt * P:(tt + 1) * P], g.ident[:])
                last.then_inc(s.x3_full, 1)
                pe.wait_ge(s.l1.normed, n + 1)
                for tt in range(TT):
                    last = nc.tensor.transpose(ps[:, 0, NT + tt * P:NT + (tt + 1) * P], s.l1.xn[:, tt], g.ident[:])
                last.then_inc(s.h_full, 1)
                pe.wait_ge(s.hT_ready, n + 1)
                for c in range(2 * CC):
                    bank = 1 if c < CC else 3
                    last = nc.tensor.matmul(ps[:, bank, c % CC * NT:(c % CC + 1) * NT], s.Win[:, c * P:(c + 1) * P], s.hT[:], start=True, stop=True)
                last.then_inc(s.in_full, 1)
                pe.wait_ge(s.h_ready, n + 1)
                for c in range(CC):
                    last = nc.tensor.matmul(ps[0:XD, 2, 0:NT], s.Wx[:, c], s.h[:, c], start=c == 0, stop=c == CC - 1)
                last.then_inc(s.xd_full, 1)
                pe.wait_ge(s.xd_ready, n + 1)
                pe.wait_ge(s.res_ready, n + 1)
                for c in range(CC):
                    last = nc.tensor.matmul(ps[:, 3, c * NT:(c + 1) * NT], s.Wdt[:, c * P:(c + 1) * P], s.xd[0:RANK], start=True, stop=True)
                last.then_inc(s.dl_full, 1)
                for which, banks, used, full in ((0, B_BANK, s.bu_ready, s.b_full), (1, C_BANK, s.yc_ready, s.c_full)):
                    for i in range(PAIRS):
                        if i >= 2:
                            pe.wait_ge(used, PAIRS * n + i - 1)
                        for k in range(2):
                            last = nc.tensor.matmul(ps[:, banks[i % 2], k * NT:(k + 1) * NT], s.sel[:, which * NS + 2 * i + k], s.xd[:], start=True, stop=True)
                        last.then_inc(full, 1)
                for i in range(NS):
                    pe.wait_ge(s.yc_ready, PAIRS * n + i // 2 + 1)
                    last = nc.tensor.matmul(ps[:, Y_BANK], g.ident[:], s.bu[:, :, i], start=i == 0, stop=i == NS - 1)
                last.then_inc(s.y_full, 1)
                pe.wait_ge(s.y_ready, n + 1)
                for c in range(CC):
                    last = nc.tensor.matmul(ps[:, 0, 0:NT], s.Wout[:, c], s.y[:, c], start=c == 0, stop=c == CC - 1)
                last.then_inc(s.op_full, 1)
                pe.wait_ge(s.x4_ready, n + 1)
                for tt in range(TT):
                    last = nc.tensor.transpose(ps[:, 1, tt * P:(tt + 1) * P], s.x4T[:, tt * P:(tt + 1) * P], g.ident[:])
                last.then_inc(s.x4_full, 1)
                pe.wait_ge(s.l2.normed, n + 1)
                for tt in range(TT):
                    last = nc.tensor.transpose(ps[:, 1, NT + tt * P:NT + (tt + 1) * P], s.l2.xn[:, tt], g.ident[:])
                last.then_inc(s.h2_full, 1)
                pe.wait_ge(s.hT2_ready, n + 1)
                nc.tensor.matmul(ps[:, 0, 0:NT], g.wlinT[:], s.hT2[:], start=True, stop=True).then_inc(s.lin_full, 1)
                pe.wait_ge(s.x5_ready, n + 1)
                for tt in range(TT):
                    last = nc.tensor.transpose(ps[:, 0, NT + tt * P:NT + (tt + 1) * P], s.x5T[:, tt * P:(tt + 1) * P], g.ident[:])
                last.then_inc(s.out_full, 1)



INPUTS = ["L0_attn_hidden_states", "L0_attn_Wq", "L0_attn_bq", "L0_attn_Wk", "L0_attn_bk", "L0_attn_Wv", "L0_attn_bv",
          "L0_attn_Wo", "L0_attn_bo", "L0_ffn_Wqkv", "L0_ffn_q_scale", "L0_ffn_k_scale", "L0_ffn_Wo", "L0_ffn_ln_g",
          "L0_ffn_ln_b", "L0_ffn_W1", "L0_ffn_b1", "L0_ffn_W2", "L0_ffn_b2", "L0_c", "L0_wmod", "L1_attn_in_proj_w",
          "L1_attn_conv_w", "L1_attn_conv_b", "L1_attn_x_proj_w", "L1_attn_dt_proj_w", "L1_attn_dt_proj_b", "L1_attn_A_log",
          "L1_attn_D_param", "L1_attn_out_proj_w", "L1_ffn_W", "L1_ffn_b", "L1_ffn_lora_down", "L1_ffn_lora_up",
          "L1_ffn_down_aux", "L1_ffn_up_aux", "L1_c", "L1_wmod"]


def build(nc, d, out):
    with ExitStack() as stack:
        g = Store(nc, stack, "all")
        g.ident = g.sb("ident", [P, P]); g.ident_bf = g.sb("ident_bf", [P, P], BF16); g.mask_bf = g.sb("mask_bf", [P, TT * KEYS], BF16)
        g.ones_row = g.sb("ones_row", [1, P]); g.neg_half = g.sb("neg_half", [P, 2 * HB])
        g.xT = g.sb("xT", [P, NB * NT]); g.x2T = g.sb("x2T", [P, NB * NT])
        g.mod = g.sb("mod", [P, 2, NB, 6])
        g.wlinT = g.sb("wlinT", [P, P])
        g.bqk = g.sb("bqk", [P, 2, 4]); g.bv_row = g.sb("bv_row", [1, P]); g.bo = g.sb("bo", [P, 1])
        g.rotab = g.sb("rotab", [P, DEPTH, 4, TT, DB]); g.lparam = g.sb("lparam", [P, DEPTH, 9])
        g.conv_w = g.sb("conv_w", [P, CC, TAPS]); g.conv_b = g.sb("conv_b", [P, CC]); g.dt_b = g.sb("dt_b", [P, CC]); g.A = g.sb("A", [P, CC, NS]); g.D = g.sb("D", [P, CC])
        g.blin = g.sb("blin", [P, 1])
        ps = stack.enter_context(nc.psum_tensor("ps", [P, 8, 512], F32))
        with ExitStack() as first:
            f = Store(nc, first, "first")
            g.mask_f = f.sb("mask_f", [P, TT * KEYS]); g.wqk_pad = f.sb("wqk_pad", [P, 2, 4 * P]); g.wvT = f.sb("wvT", [P, P]); g.woT = f.sb("woT", [P, P])
            setup(nc, g, d, ps)
            phase_a(nc, g, d, ps)
        phase_b(nc, g, d, ps)
        phase_c(nc, g, d, ps, out)


def shape_constants():
    i, c = np.arange(P)[:, None], np.arange(KEYS)[None, :]
    band = (c >= i) & (c <= i + WIN)
    mask = np.where(np.stack([band & (c >= WIN), band], 1), 0.0, MASKED).astype(np.float32).reshape(P, TT * KEYS)
    half = np.arange(0, DB, 2, dtype=np.float32)
    inv_freq = (np.float32(1.0) / np.float32(10000.0) ** (half / np.float32(DB))).astype(np.float32)
    t = np.arange(NT, dtype=np.float32)
    freqs = t[:, None] * inv_freq[None, :]
    base = ((half + np.float32(0.4 * DB)) / np.float32(1.4 * DB)).astype(np.float32)
    power = (t - NT // 2) / (WIN // 2)
    scale = base[None, :].astype(np.float64) ** power[:, None]
    cos, sin = np.cos(freqs.astype(np.float64)), np.sin(freqs.astype(np.float64))
    tables = []
    for factor in (8.0 * scale, 1.0 / scale):
        tables.append(np.concatenate([cos * factor, cos * factor], 1))
        tables.append(np.concatenate([-sin * factor, sin * factor], 1))
    rot = np.stack(tables, 0).astype(np.float32).reshape(4, TT, P, DB).transpose(2, 0, 1, 3)
    sel = np.zeros((XD, 2 * NS, P), np.float32)
    for k in range(2 * NS):
        sel[RANK + k, k] = 1.0
    return {"ident": np.eye(P, dtype=np.float32), "mask": mask, "rot": np.ascontiguousarray(rot), "sel": sel}


def kernel(**inputs):
    import concourse.bacc as bacc
    from concourse.bass_utils import run_bass_kernel_spmd

    nc = bacc.Bacc("TRN2", target_bir_lowering=False, num_devices=1)
    arrays, d = {}, {}
    given = {name: np.ascontiguousarray(inputs[name]) for name in INPUTS}
    given.update(shape_constants())
    for name, a in given.items():
        arrays["in_" + name] = a
        d[name] = nc.dram_tensor("in_" + name, a.shape, mybir.dt.from_np(a.dtype), kind="ExternalInput").ap()
    out = nc.dram_tensor("out", (NB, NT, P), F32, kind="ExternalOutput").ap()
    build(nc, d, out)
    result = run_bass_kernel_spmd(nc, [arrays], core_ids=[0])
    return result.results[0]["out"]
```

```python
from contextlib import ExitStack

import numpy as np

import concourse.bass as bass
from concourse import mybir

F32 = mybir.dt.float32
BF16 = mybir.dt.bfloat16
F32R = mybir.dt.float32r
ALU = mybir.AluOpType
ACT = mybir.ActivationFunctionType
AX = mybir.AxisListType

P = 128
NB, NT = 16, 256
TT = NT // P
H0, D0 = 16, 8
HB, DB = 16, 64
INNER = HB * DB
WIN = 32
DEPTH = 6
FF = 341
FF_CHUNKS = [(0, 128), (128, 128), (256, FF - 256)]
NS, CH, RANK, TAPS = 16, 256, 64, 4
CC = CH // P
XBC = 2 * NS
XD = RANK + XBC
LN_EPS = 1e-5
KEYS = P + WIN
MASKED = -1e30


def wait(engine, semaphore, value):
    if isinstance(value, int) and value <= 0:
        return
    engine.wait_ge(semaphore, value)


class Store:

    def __init__(self, nc, stack, stage):
        self.nc, self.stack, self.stage = nc, stack, stage

    def sb(self, name, shape, dtype=F32):
        return self.stack.enter_context(self.nc.sbuf_tensor(f"{self.stage}_{name}", shape, dtype))

    def sems(self, names):
        return [self.stack.enter_context(self.nc.semaphore(f"{self.stage}_{name}")) for name in names.split()]


def flat(ap):
    return ap.rearrange("(c p) -> p c", p=P)




def setup(nc, g, d, ps):
    with ExitStack() as stack:
        s = Store(nc, stack, "setup")
        s.crow = s.sb("crow", [NB, 2, P]); s.sig = s.sb("sig", [NB, 2, P]); s.scT = s.sb("scT", [P, 2, NB])
        s.wmod = s.sb("wmod", [P, 2, 6 * P]); s.raw_w = s.sb("raw_w", [P, 4, P]); s.Wlin = s.sb("Wlin", [P, P])
        s.ga = s.sb("ga", [P, 2, NB, 2]); s.gb = s.sb("gb", [P, 2, NB, 2])
        s.qkscale = s.sb("qkscale", [P, 2, DEPTH, DB]); s.rot = s.sb("rot", [P, 4, TT, DB])
        s.lora_dn = s.sb("lora_dn", [4, 100]); s.dn_aux = s.sb("dn_aux", [100, P]); s.lora_up = s.sb("lora_up", [50, 4]); s.up_aux = s.sb("up_aux", [P, 50])
        s.dnT = s.sb("dnT", [100, 4]); s.upT = s.sb("upT", [4, 50]); s.uaT = s.sb("uaT", [50, P]); s.t1 = s.sb("t1", [4, P]); s.t2 = s.sb("t2", [50, P])
        s.alog = s.sb("alog", [P, CC, NS])
        s.loaded_a, s.loaded_b, s.consts, s.sig_exp, s.sig_done, s.scT_full, s.scT_done, s.mod_full = s.sems("loaded_a loaded_b consts sig_exp sig_done scT_full scT_done mod_full")
        s.mod_done, s.wt_full, s.wt_done, s.lora_full, s.lora_done, s.gstep, s.a_exp, s.chain = s.sems("mod_done wt_full wt_done lora_full lora_done gstep a_exp chain")
        block = stack.enter_context(nc.Block())
        n_a = 0

        @block.sync
        def _(sp):
            loads = [(g.ident[:], d["ident"]), (g.mask_f[:], d["mask"]), (s.crow[:, 0], d["L0_c"]), (s.crow[:, 1], d["L1_c"]),
                     (s.wmod[:, 0], d["L0_wmod"]), (s.wmod[:, 1], d["L1_wmod"])]
            loads += [(s.raw_w[:, i], w) for i, w in enumerate((d["L0_attn_Wq"], d["L0_attn_Wk"], d["L0_attn_Wv"], d["L0_attn_Wo"]))]
            loads += [(s.Wlin[:], d["L1_ffn_W"]), (s.rot[:], d["rot"]),
                      (s.lora_dn[:], d["L1_ffn_lora_down"]), (s.dn_aux[:], d["L1_ffn_down_aux"]),
                      (s.lora_up[:], d["L1_ffn_lora_up"]), (s.up_aux[:], d["L1_ffn_up_aux"])]
            for dst, src in loads:
                sp.dma_start(dst, src).then_inc(s.loaded_a, 16)
            sp.wait_ge(s.loaded_a, 16 * len(loads))

        small = [(s.alog[:], d["L1_attn_A_log"].rearrange("(c p) n -> p c n", p=P)),
                 (g.bv_row[:], d["L0_attn_bv"].rearrange("(a n) -> a n", a=1)),
                 (g.bo[:], flat(d["L0_attn_bo"])),
                 (g.lparam[:, :, 0], d["L0_ffn_ln_g"].rearrange("l p -> p l")), (g.lparam[:, :, 1], d["L0_ffn_ln_b"].rearrange("l p -> p l")),
                 (g.lparam[:, :, 2], d["L0_ffn_b2"].rearrange("l p -> p l")),
                 (g.conv_w[:], d["L1_attn_conv_w"].rearrange("(c p) o k -> p c (o k)", p=P)),
                 (g.conv_b[:], flat(d["L1_attn_conv_b"])), (g.dt_b[:], flat(d["L1_attn_dt_proj_b"])),
                 (g.D[:], flat(d["L1_attn_D_param"])), (g.blin[:], flat(d["L1_ffn_b"])),
                 (s.qkscale[:, 0], d["L0_ffn_q_scale"].rearrange("(a l) e -> a l e", a=1).broadcast_to((P, DEPTH, DB))),
                 (s.qkscale[:, 1], d["L0_ffn_k_scale"].rearrange("(a l) e -> a l e", a=1).broadcast_to((P, DEPTH, DB)))]
        for half in range(2):
            for c, (c0, w) in enumerate(FF_CHUNKS):
                small.append((g.lparam[0:w, :, 3 + 3 * half + c], d["L0_ffn_b1"][:, half * FF + c0:half * FF + c0 + w].rearrange("l p -> p l")))
        small += [(g.bqk[:, 0:1], flat(d["L0_attn_bq"])), (g.bqk[:, 1:2], flat(d["L0_attn_bk"])), (g.head_rows[:], d["head_rows"])]

        @block.scalar
        def _(act):
            act.wait_ge(s.consts, 1)
            with nc.allow_non_contiguous_dma(reason="vectors laid along partitions, once"):
                for dst, src in small:
                    act.dma_start(dst, src).then_inc(s.loaded_b, 16)
            act.wait_ge(s.loaded_a, 16 * 16)
            nc.scalar.activation(s.sig[:], s.crow[:], ACT.Exp, scale=-1.0).then_inc(s.sig_exp, 1)
            act.wait_ge(s.loaded_b, 16 * len(small))
            nc.scalar.activation(g.A[:], s.alog[:], ACT.Exp).then_inc(s.a_exp, 1)
            act.wait_ge(s.mod_done, 1)
            nc.scalar.activation(s.ga[:], g.mod[:, :, :, 2:6:3], ACT.Abs).then_inc(s.gstep, 1)

        @block.gpsimd
        def _(pool):
            nc.gpsimd.memset(g.lparam[:], 0.0).then_inc(s.consts, 1)

        @block.vector
        def _(dve):
            count = [0]

            def link(ins):
                count[0] += 1
                ins.then_inc(s.chain, 1)
                dve.wait_ge(s.chain, count[0])

            nc.vector.memset(g.ones_row[:], 1.0)
            nc.vector.memset(g.neg_half[:], -0.5)
            dve.wait_ge(s.loaded_a, 16 * 16)
            nc.vector.tensor_copy(g.ident_bf[:], g.ident[:])
            nc.vector.tensor_copy(g.mask_bf[:], g.mask_f[:])
            dve.wait_ge(s.sig_exp, 1)
            link(nc.vector.tensor_scalar_add(s.sig[:], s.sig[:], 1.0))
            link(nc.vector.reciprocal(s.sig[:], s.sig[:]))
            nc.vector.tensor_tensor(s.sig[:], s.sig[:], s.crow[:], ALU.mult).then_inc(s.sig_done, 1)
            dve.wait_ge(s.wt_full, 1)
            nc.vector.tensor_copy(g.wqT[:], ps[:, 1, 0:P])
            nc.vector.tensor_copy(g.wkT[:], ps[:, 1, P:2 * P])
            nc.vector.tensor_copy(g.wvT[:], ps[:, 1, 2 * P:3 * P])
            nc.vector.tensor_copy(g.woT[:], ps[:, 1, 3 * P:4 * P])
            nc.vector.tensor_copy(s.dnT[:], ps[0:100, 2, 0:4])
            nc.vector.tensor_copy(s.upT[:], ps[0:4, 2, 128:178])
            nc.vector.tensor_copy(s.uaT[:], ps[0:50, 2, 256:384])
            nc.vector.tensor_copy(g.wlinT[:], ps[:, 2, 384:512]).then_inc(s.wt_done, 1)
            dve.wait_ge(s.lora_full, 1)
            nc.vector.tensor_copy(s.t1[:], ps[0:4, 3, 0:P]).then_inc(s.lora_done, 1)
            dve.wait_ge(s.lora_full, 2)
            nc.vector.tensor_copy(s.t2[:], ps[0:50, 4, 0:P]).then_inc(s.lora_done, 1)
            dve.wait_ge(s.lora_full, 3)
            nc.vector.tensor_tensor(g.wlinT[:], g.wlinT[:], ps[:, 5, 0:P], ALU.add)
            dve.wait_ge(s.scT_full, 1)
            nc.vector.tensor_copy(s.scT[:], ps[:, 0, 0:2 * NB].rearrange("p (l b) -> p l b", l=2)).then_inc(s.scT_done, 1)
            dve.wait_ge(s.mod_full, 1)
            nc.vector.tensor_copy(g.mod[:], ps[:, 6, 0:12 * NB].rearrange("p (l j b) -> p l b j", l=2, j=6)).then_inc(s.mod_done, 1)
            dve.wait_ge(s.gstep, 1)
            gates = g.mod[:, :, :, 2:6:3]
            nc.vector.tensor_scalar(s.gb[:], gates, 0.0, 2.0, ALU.is_ge, ALU.mult)
            link(nc.vector.tensor_scalar_max(s.ga[:], s.ga[:], 0.25))
            link(nc.vector.tensor_scalar_add(s.gb[:], s.gb[:], -1.0))
            link(nc.vector.tensor_tensor(gates, s.ga[:], s.gb[:], ALU.mult))
            scales = g.mod[:, :, :, 1:6:3]
            nc.vector.tensor_scalar_add(scales, scales, 1.0)
            dve.wait_ge(s.loaded_b, 16 * len(small))
            nc.vector.tensor_scalar_mul(g.bqk[:, 0:1], g.bqk[:, 0:1], float(D0) ** -0.5)
            for i in range(2):
                for tt in range(TT):
                    cos = s.rot[:, 2 * i:2 * i + 1, tt].broadcast_to((P, DEPTH, DB))
                    nc.vector.tensor_tensor(g.rotab[:, :, 2 * i, tt], s.qkscale[:, i], cos, ALU.mult)
                    for half in range(2):
                        a, b = half * (DB // 2), (1 - half) * (DB // 2)
                        sin = s.rot[:, 2 * i + 1:2 * i + 2, tt, a:a + DB // 2].broadcast_to((P, DEPTH, DB // 2))
                        nc.vector.tensor_tensor(g.rotab[:, :, 2 * i + 1, tt, a:a + DB // 2],
                                                s.qkscale[:, i, :, b:b + DB // 2], sin, ALU.mult)
            dve.wait_ge(s.a_exp, 1)
            nc.vector.tensor_scalar_mul(g.A[:], g.A[:], -1.0)

        @block.tensor
        def _(pe):
            pe.wait_ge(s.loaded_a, 16 * 16)
            for i in range(4):
                nc.tensor.transpose(ps[:, 1, i * P:(i + 1) * P], s.raw_w[:, i], g.ident[:])
            nc.tensor.transpose(ps[0:100, 2, 0:4], s.lora_dn[:], g.ident[0:4, 0:4])
            nc.tensor.transpose(ps[0:4, 2, 128:178], s.lora_up[:], g.ident[0:50, 0:50])
            nc.tensor.transpose(ps[0:50, 2, 256:384], s.up_aux[:], g.ident[:])
            nc.tensor.transpose(ps[:, 2, 384:512], s.Wlin[:], g.ident[:]).then_inc(s.wt_full, 1)
            pe.wait_ge(s.wt_done, 1)
            nc.tensor.matmul(ps[0:4, 3, 0:P], s.dnT[:], s.dn_aux[:], start=True, stop=True).then_inc(s.lora_full, 1)
            pe.wait_ge(s.lora_done, 1)
            nc.tensor.matmul(ps[0:50, 4, 0:P], s.upT[:], s.t1[:], start=True, stop=True).then_inc(s.lora_full, 1)
            pe.wait_ge(s.lora_done, 2)
            nc.tensor.matmul(ps[:, 5, 0:P], s.t2[:], s.uaT[:], start=True, stop=True).then_inc(s.lora_full, 1)
            pe.wait_ge(s.sig_done, 1)
            for l in range(2):
                last = nc.tensor.transpose(ps[:, 0, l * NB:(l + 1) * NB], s.sig[:, l], g.ident[0:NB, 0:NB])
            last.then_inc(s.scT_full, 1)
            pe.wait_ge(s.scT_done, 1)
            for l in range(2):
                for j in range(6):
                    k = (l * 6 + j) * NB
                    last = nc.tensor.matmul(ps[:, 6, k:k + NB], s.wmod[:, l, j * P:(j + 1) * P], s.scT[:, l],
                                            start=True, stop=True)
            last.then_inc(s.mod_full, 1)




class LayerNorm:

    def __init__(self, s, name):
        self.st = s.sb(name + "_st", [P, TT, 6])
        self.mv = s.sb(name + "_mv", [P, TT, 2])
        self.var = s.sb(name + "_var", [P, TT])
        self.rstd = s.sb(name + "_rstd", [P, TT])
        self.xn = s.sb(name + "_xn", [P, TT, P])
        self.moment, self.var_ready, self.rstd_ready, self.normed = s.sems(
            " ".join(f"{name}_{x}" for x in ("moment", "var_ready", "rstd_ready", "normed")))


def layernorm_stats(nc, dve, ln, src, n):
    for tt in range(TT):
        last = nc.vector.bn_stats(ln.st[:, tt], src[:, tt])
    last.then_inc(ln.moment, 1)
    dve.wait_ge(ln.moment, 2 * n + 1)
    nc.vector.memset(ln.var[:], LN_EPS)
    for tt in range(TT):
        last = nc.vector.bn_aggr(ln.mv[:, tt], ln.st[:, tt])
    last.then_inc(ln.moment, 1)
    dve.wait_ge(ln.moment, 2 * n + 2)
    nc.vector.tensor_tensor(ln.var[:], ln.mv[:, :, 1], ln.var[:], ALU.add).then_inc(ln.var_ready, 1)


def layernorm_pool(nc, pool, ln, g, n):
    pool.wait_ge(ln.var_ready, n + 1)
    nc.gpsimd.tensor_tensor(ln.rstd[:], ln.var[:], g.neg_half[:, 0:TT], ALU.pow).then_inc(ln.rstd_ready, 1)


def layernorm_apply(nc, dve, ln, src, n):
    dve.wait_ge(ln.rstd_ready, n + 1)
    for tt in range(TT):
        last = nc.vector.tensor_scalar(ln.xn[:, tt], src[:, tt], ln.mv[:, tt, 0:1], ln.rstd[:, tt:tt + 1], ALU.subtract, ALU.mult)
    last.then_inc(ln.normed, 1)



SLOTS = HB
T_LAG, PV_LAG = 2, 3
BY_ACT = [k for k in range(H0) if k % 3 == 2]
BY_DVE = [k for k in range(H0) if k % 3 != 2]
QM_PIECES = 4


class StepA:

    def __init__(self, n, odd, front, heads, tail, last):
        self.n, self.odd, self.front, self.heads, self.tail, self.last = n, odd, front, heads, tail, last


def phase_a_steps(engine, body):
    def whole(n):
        body(StepA(n, n % 2, n + 1 < NB, 0 <= n < NB, 0 <= n - 1 < NB, 0 <= n - 2 < NB))

    for n in range(-1, 3):
        whole(n)
    with engine.Fori(1, NB // 2 - 1) as pair:
        body(StepA(2 * pair + 1, 1, True, True, True, True))
        body(StepA(2 * pair + 2, 0, True, True, True, True))
    for n in range(NB - 1, NB + 2):
        whole(n)


def phase_a(nc, g, d, ps):
    with ExitStack() as stack:
        s = Store(nc, stack, "a")
        s.xtok = s.sb("xtok", [P, 2, TT, P]); s.hT = s.sb("hT", [P, NT])
        s.md_front = s.sb("md_front", [P, 2]); s.md_out = s.sb("md_out", [P, 1]); s.md_last = s.sb("md_last", [P, 2])
        s.qT = s.sb("qT", [P, NT]); s.kT = s.sb("kT", [P, 2, NT]); s.V = s.sb("V", [P, 2, TT, P])
        s.qm = s.sb("qm", [P, 2, H0, NT])
        s.nm = s.sb("nm", [P, H0, TT]); s.ssum = s.sb("ssum", [P, 2, H0, TT]); s.rinv = s.sb("rinv", [P, H0, TT])
        s.Pr = s.sb("Pr", [P, 4, TT, NT]); s.PT = s.sb("PT", [P, 4, TT, NT])
        s.o = s.sb("o", [P, TT, H0, D0]); s.oT = s.sb("oT", [P, NT]); s.tmp = s.sb("tmp", [P, NT]); s.x2s = s.sb("x2s", [P, NT]); s.x2tok = s.sb("x2tok", [P, TT, P])
        s.l1 = LayerNorm(s, "l1"); s.l2 = LayerNorm(s, "l2")
        s.x_in = s.sems("x_in_0 x_in_1")
        s.md_front_ready, s.hx_full, s.x_kept, s.hT_ready, s.qk_full, s.qk_ready, s.qm_ready, s.v_full, s.v_ready = s.sems(
            "md_front_ready hx_full x_kept hT_ready qk_full qk_ready qm_ready v_full v_ready")
        s.s_done, s.max_done, s.exp_done, s.t_done, s.pt_act, s.pt_dve, s.pv_done, s.rinv_ready = s.sems(
            "s_done max_done exp_done t_done pt_act pt_dve pv_done rinv_ready")
        s.o_ready, s.oT_full, s.oT_ready, s.proj_full, s.tmp_ready, s.x2s_ready, s.x2_full, s.x2tok_ready = s.sems(
            "o_ready oT_full oT_ready proj_full tmp_ready x2s_ready x2_full x2tok_ready")
        s.h2_full, s.md_last_ready, s.seq_done, s.x2_kept = s.sems("h2_full md_last_ready seq_done x2_kept")
        block = stack.enter_context(nc.Block())
        S_BANK, T_BANK, O_BANK, FRONT_BANK, TAIL_BANK = (0, 1), (2, 3), (4, 5), 6, 7

        def started(step, slot, lag):
            if slot >= lag:
                return (step.n, slot - lag) if step.heads else (None, None)
            return (step.n - 1, slot - lag + SLOTS) if step.tail else (None, None)

        def wait_pt(engine, item, k):
            if k in BY_ACT:
                engine.wait_ge(s.pt_act, len(BY_ACT) * item + BY_ACT.index(k) + 1)
            else:
                engine.wait_ge(s.pt_dve, len(BY_DVE) * item + BY_DVE.index(k) + 1)

        @block.sync
        def _(sp):
            def load(n, parity, src):
                sp.dma_start(s.xtok[:, parity], src.rearrange("b (t p) e -> p (b t) e", p=P)).then_inc(s.x_in[parity], 16)

            load(0, 0, d["L0_attn_hidden_states"][0:1])
            load(1, 1, d["L0_attn_hidden_states"][1:2])
            with sp.Fori(1, NB // 2) as pair:
                for parity in range(2):
                    n = 2 * pair + parity
                    sp.wait_ge(s.hx_full, n - 1)
                    sp.dma_start(s.xtok[:, parity], d["L0_attn_hidden_states"][bass.ds(n, 1)].rearrange("b (t p) e -> p (b t) e", p=P)).then_inc(s.x_in[parity], 16)
            for loaded in s.x_in:
                sp.wait_ge(loaded, 16 * NB // 2)

        @block.vector
        def _(dve):
            def body(step):
                n, f, t, u = step.n, step.n + 1, step.n - 1, step.n - 2
                pf = 1 - step.odd

                def known(value):
                    return value if isinstance(value, int) else dve.snap(value)

                def copy_mod(dst, seq, a, b):
                    return nc.vector.tensor_scalar_mul(dst[:], g.mod[:, 0, bass.ds(seq, 1), a:b].rearrange("p a k -> p (a k)"), 1.0)

                if step.front:
                    f_seq, f_half = known(f), known(f >> 1)
                if step.tail:
                    t_seq = known(t)
                    copy_mod(s.md_out, t_seq, 2, 3)
                if step.last:
                    copy_mod(s.md_last, known(u), 3, 5).then_inc(s.md_last_ready, 1)
                for slot in range(SLOTS):
                    if step.tail and slot == PV_LAG:
                        dve.wait_ge(s.pv_done, H0 * t + H0)
                        nc.vector.reciprocal(s.rinv[:], s.ssum[:, 1 - step.odd]).then_inc(s.rinv_ready, 1)
                        dve.wait_ge(s.rinv_ready, t + 1)
                        for tt in range(TT):
                            last = nc.vector.tensor_tensor(s.o[:, tt], ps[:, O_BANK[1 - step.odd], tt * P:(tt + 1) * P].rearrange("p (h e) -> p h e", e=D0),
                                                           s.rinv[:, :, tt:tt + 1].broadcast_to((P, H0, D0)), ALU.mult)
                        last.then_inc(s.o_ready, 1)
                    if step.heads:
                        h = slot
                        dve.wait_ge(s.s_done, H0 * n + h + 1)
                        nc.vector.tensor_reduce(s.nm[:, h], ps[:, S_BANK[h % 2]].rearrange("p (t k) -> p t k", t=TT),
                                                AX.X, ALU.max, negate=True).then_inc(s.max_done, 1)
                    item, k = started(step, slot, T_LAG)
                    if k in BY_DVE:
                        dve.wait_ge(s.t_done, H0 * item + k + 1)
                        wait(dve, s.pv_done, H0 * item + k - 3)
                        nc.vector.tensor_copy(s.PT[:, k % 4], ps[:, T_BANK[k % 2]].rearrange("p (t k) -> p t k", t=TT)).then_inc(s.pt_dve, 1)
                    if step.front and slot == 0:
                        dve.wait_ge(s.x_in[pf], 16 * f_half + 16)
                        layernorm_stats(nc, dve, s.l1, s.xtok[:, pf], f)
                    if step.front and slot == 2:
                        layernorm_apply(nc, dve, s.l1, s.xtok[:, pf], f)
                        copy_mod(s.md_front, f_seq, 0, 2).then_inc(s.md_front_ready, 1)
                    if step.front and slot == 5:
                        dve.wait_ge(s.hx_full, f + 1)
                        nc.vector.tensor_scalar_mul(g.x2T[:, bass.ds(known(f * NT), NT)], ps[:, FRONT_BANK, NT:2 * NT], 1.0).then_inc(s.x_kept, 1)
                    if step.front and slot == 11:
                        dve.wait_ge(s.v_full, f + 1)
                        nc.vector.tensor_copy(s.V[:, pf], ps[:, FRONT_BANK, 0:NT].rearrange("p (t e) -> p t e", t=TT)).then_inc(s.v_ready, 1)
                    if step.tail and slot == 9:
                        dve.wait_ge(s.proj_full, t + 1)
                        nc.vector.tensor_scalar(s.tmp[:], ps[:, TAIL_BANK, 0:NT], g.bo[:], s.md_out[:], ALU.add, ALU.mult).then_inc(s.tmp_ready, 1)
                        dve.wait_ge(s.tmp_ready, t + 1)
                        nc.vector.tensor_tensor(s.x2s[:], s.tmp[:], g.x2T[:, bass.ds(known(t * NT), NT)], ALU.add).then_inc(s.x2s_ready, 1)
                    if step.tail and slot == 12:
                        dve.wait_ge(s.x2_full, t + 1)
                        nc.vector.tensor_copy(s.x2tok[:], ps[:, TAIL_BANK, 0:NT].rearrange("p (t e) -> p t e", t=TT)).then_inc(s.x2tok_ready, 1)
                        dve.wait_ge(s.x2tok_ready, t + 1)
                        layernorm_stats(nc, dve, s.l2, s.x2tok, t)
                    if step.tail and slot == 14:
                        layernorm_apply(nc, dve, s.l2, s.x2tok, t)

            phase_a_steps(dve, body)

        @block.gpsimd
        def _(pool):
            def body(step):
                n, f, t = step.n, step.n + 1, step.n - 1
                pf = 1 - step.odd
                if step.front:
                    layernorm_pool(nc, pool, s.l1, g, f)
                    heads = H0 // QM_PIECES
                    for i in range(QM_PIECES):
                        some = slice(i * heads, (i + 1) * heads)
                        pool.wait_ge(s.qk_ready, f + 1)
                        nc.gpsimd.tensor_tensor(s.qm[:, pf, some], s.qT[:].rearrange("p (o t) -> p o t", o=1).broadcast_to((P, heads, NT)),
                                                g.head_rows[:, some].rearrange("p (h o) -> p h o", o=1).broadcast_to((P, heads, NT)), ALU.mult).then_inc(s.qm_ready, 1)
                if step.tail:
                    x2_kept = t * NT if isinstance(t, int) else pool.snap(t * NT)
                    pool.wait_ge(s.x2s_ready, t + 1)
                    nc.gpsimd.tensor_copy(g.x2T[:, bass.ds(x2_kept, NT)], s.x2s[:]).then_inc(s.x2_kept, 1)
                    layernorm_pool(nc, pool, s.l2, g, t)

            phase_a_steps(pool, body)

        @block.scalar
        def _(act):
            def body(step):
                n, f, t, u = step.n, step.n + 1, step.n - 1, step.n - 2
                pf = 1 - step.odd
                if step.last:
                    x_start = u * NT if isinstance(u, int) else act.snap(u * NT)
                for slot in range(SLOTS):
                    item, k = started(step, slot, T_LAG)
                    if k in BY_ACT:
                        act.wait_ge(s.t_done, H0 * item + k + 1)
                        wait(act, s.pv_done, H0 * item + k - 3)
                        nc.scalar.activation(s.PT[:, k % 4], ps[:, T_BANK[k % 2]].rearrange("p (t k) -> p t k", t=TT), ACT.Copy).then_inc(s.pt_act, 1)
                    if step.heads:
                        h = slot
                        act.wait_ge(s.max_done, H0 * n + h + 1)
                        wait(act, s.t_done, H0 * n + h - 3)
                        for tt in range(TT):
                            last = nc.scalar.activation(s.Pr[:, h % 4, tt], ps[:, S_BANK[h % 2], tt * NT:(tt + 1) * NT], ACT.Exp,
                                                        bias=s.nm[:, h, tt:tt + 1], accum_out=s.ssum[:, step.odd, h, tt:tt + 1])
                        last.then_inc(s.exp_done, 1)
                    if step.last and slot == 2:
                        act.wait_ge(s.md_last_ready, u + 1)
                        act.wait_ge(s.h2_full, u + 1)
                        nc.scalar.activation(g.xT[:, bass.ds(x_start, NT)], ps[:, TAIL_BANK, 0:NT], ACT.Identity,
                                             bias=s.md_last[:, 0:1], scale=s.md_last[:, 1:2]).then_inc(s.seq_done, 1)
                    if step.front and slot == 5:
                        act.wait_ge(s.md_front_ready, f + 1)
                        act.wait_ge(s.x_kept, f + 1)
                        nc.scalar.activation(s.hT[:], ps[:, FRONT_BANK, 0:NT], ACT.Identity, bias=s.md_front[:, 0:1], scale=s.md_front[:, 1:2]).then_inc(s.hT_ready, 1)
                    if step.tail and slot == 6:
                        act.wait_ge(s.oT_full, t + 1)
                        nc.scalar.activation(s.oT[:], ps[:, TAIL_BANK, 0:NT], ACT.Copy).then_inc(s.oT_ready, 1)
                    if step.front and slot == 8:
                        act.wait_ge(s.qk_full, f + 1)
                        wait(act, s.qm_ready, QM_PIECES * f)
                        nc.scalar.activation(s.qT[:], ps[:, FRONT_BANK, 0:NT], ACT.Identity, bias=g.bqk[:, 0:1], scale=float(D0) ** -0.5)
                        nc.scalar.activation(s.kT[:, pf], ps[:, FRONT_BANK, NT:2 * NT], ACT.Identity, bias=g.bqk[:, 1:2]).then_inc(s.qk_ready, 1)

            phase_a_steps(act, body)

        @block.tensor
        def _(pe):
            def body(step):
                n, f, t, u = step.n, step.n + 1, step.n - 1, step.n - 2
                pf, pa = 1 - step.odd, step.odd
                for slot in range(SLOTS):
                    if step.heads:
                        h = slot
                        if h == 0:
                            pe.wait_ge(s.qm_ready, QM_PIECES * (n + 1))
                        wait(pe, s.exp_done, H0 * n + h - 1)
                        for tt in range(TT):
                            last = nc.tensor.matmul(ps[:, S_BANK[h % 2], tt * NT:(tt + 1) * NT], s.qm[:, pa, h, tt * P:(tt + 1) * P],
                                                    s.kT[:, pa], start=True, stop=True)
                        last.then_inc(s.s_done, 1)
                    item, k = started(step, slot, T_LAG)
                    if k is not None:
                        pe.wait_ge(s.exp_done, H0 * item + k + 1)
                        if k >= 2:
                            wait_pt(pe, item, k - 2)
                        elif step.tail:
                            wait_pt(pe, item - 1, k - 2 + H0)
                        for kb in range(TT):
                            for tt in range(TT):
                                last = nc.tensor.transpose(ps[:, T_BANK[k % 2], kb * NT + tt * P:kb * NT + (tt + 1) * P],
                                                           s.Pr[:, k % 4, tt, kb * P:(kb + 1) * P], g.ident[:])
                        last.then_inc(s.t_done, 1)
                    if step.last and slot == 1:
                        pe.wait_ge(s.l2.normed, u + 1)
                        for tt in range(TT):
                            last = nc.tensor.transpose(ps[:, TAIL_BANK, tt * P:(tt + 1) * P], s.l2.xn[:, tt], g.ident[:])
                        last.then_inc(s.h2_full, 1)
                    if step.front and slot == 4:
                        pe.wait_ge(s.l1.normed, f + 1)
                        wait(pe, s.v_ready, f)
                        for tt in range(TT):
                            nc.tensor.transpose(ps[:, FRONT_BANK, tt * P:(tt + 1) * P], s.l1.xn[:, tt], g.ident[:])
                            last = nc.tensor.transpose(ps[:, FRONT_BANK, NT + tt * P:NT + (tt + 1) * P], s.xtok[:, pf, tt], g.ident[:])
                        last.then_inc(s.hx_full, 1)
                    if step.tail and slot == 5:
                        pe.wait_ge(s.o_ready, t + 1)
                        wait(pe, s.seq_done, t)
                        for tt in range(TT):
                            last = nc.tensor.transpose(ps[:, TAIL_BANK, tt * P:(tt + 1) * P], s.o[:, tt].rearrange("p h e -> p (h e)"), g.ident[:])
                        last.then_inc(s.oT_full, 1)
                    if step.front and slot == 7:
                        pe.wait_ge(s.hT_ready, f + 1)
                        nc.tensor.matmul(ps[:, FRONT_BANK, 0:NT], g.wqT[:], s.hT[:], start=True, stop=True)
                        nc.tensor.matmul(ps[:, FRONT_BANK, NT:2 * NT], g.wkT[:], s.hT[:], start=True, stop=True).then_inc(s.qk_full, 1)
                    if step.tail and slot == 8:
                        pe.wait_ge(s.oT_ready, t + 1)
                        nc.tensor.matmul(ps[:, TAIL_BANK, 0:NT], g.woT[:], s.oT[:], start=True, stop=True).then_inc(s.proj_full, 1)
                    if step.front and slot == 10:
                        pe.wait_ge(s.qk_ready, f + 1)
                        for tt in range(TT):
                            nc.tensor.matmul(ps[:, FRONT_BANK, tt * P:(tt + 1) * P], g.ones_row[:], g.bv_row[:], start=True, stop=False)
                            last = nc.tensor.matmul(ps[:, FRONT_BANK, tt * P:(tt + 1) * P], s.hT[:, tt * P:(tt + 1) * P], g.wvT[:], start=False, stop=True)
                        last.then_inc(s.v_full, 1)
                    if step.tail and slot == 11:
                        pe.wait_ge(s.x2s_ready, t + 1)
                        for tt in range(TT):
                            last = nc.tensor.transpose(ps[:, TAIL_BANK, tt * P:(tt + 1) * P], s.x2s[:, tt * P:(tt + 1) * P], g.ident[:])
                        last.then_inc(s.x2_full, 1)
                    item, k = started(step, slot, PV_LAG)
                    if k is not None:
                        wait_pt(pe, item, k)
                        if k == 0:
                            pe.wait_ge(s.v_ready, item + 1)
                            wait(pe, s.o_ready, item - 1)
                        now = slot >= PV_LAG
                        bank, v = O_BANK[pa if now else 1 - pa], s.V[:, pa if now else 1 - pa]
                        for tt in range(TT):
                            for kb in range(TT):
                                c = tt * P + k * D0
                                last = nc.tensor.matmul(ps[:, bank, c:c + D0], s.PT[:, k % 4, kb, tt * P:(tt + 1) * P],
                                                        v[:, kb, k * D0:(k + 1) * D0], start=kb == 0, stop=kb == TT - 1)
                        last.then_inc(s.pv_done, 1)

            phase_a_steps(pe, body)



ITEMS = DEPTH * NB
WCHUNKS = 6
RAW = 3
PIECES = [(0, 0), (0, 1), (0, 2), (0, 3), (1, 0), (1, 1), (1, 2), (1, 3), (0, 4), (0, 5), (1, 4), (1, 5)]
QK = [slot for slot, (_, c) in enumerate(PIECES) if c < 4]
N_QK = len(QK)
POWER_SLOT = {3: 0, 7: 1}
POOL_NORM_SLOT, NORM_SLOT = {10: 1}, {7: 0}
TRANSPOSE_SLOT = {8: (0, 0), 10: (0, 2), 11: (0, 1), 12: (0, 3), 13: (1, 0), 14: (1, 2)}
LATE_SLOT = {1: (1, 1), 2: (1, 3)}
OUT_SLOT = {0: ((0, 0),), 2: ((1, 0),), 6: ((0, 1), (1, 1))}
WO_SLOT, RES_SLOT, XT_SLOT, STATS_SLOT, NORMED_SLOT, XN_SLOT = 8, 8, 10, 11, 14, 15
W1_SLOT = {3: 0, 5: 1, 7: 2}
GELU_SLOT, GATE_SLOT, W2_SLOT, END_SLOT, SPLIT_SLOT = 8, 9, 15, 15, 12


def spare_uses(front, attn, tail, ffn):
    uses = []
    for slot in range(SLOTS):
        if tail:
            uses += [("out", which) for which in OUT_SLOT.get(slot, ())]
            uses += [(kind, 0) for at, kind in ((WO_SLOT, "wo"), (XT_SLOT, "xt"), (XN_SLOT, "xn")) if slot == at]
        if ffn:
            uses += [("w1", W1_SLOT[slot])] if slot in W1_SLOT else []
            uses += [("w2", 0)] if slot == W2_SLOT else []
        if attn and slot in LATE_SLOT:
            uses.append(("tr", LATE_SLOT[slot]))
        if front and slot in TRANSPOSE_SLOT:
            uses.append(("tr", TRANSPOSE_SLOT[slot]))
    return uses


def stages_of(n):
    return n + 1 < ITEMS, 0 <= n < ITEMS, 0 <= n - 1 < ITEMS, 0 <= n - 2 < ITEMS


class Step:

    def __init__(self, n, odd, front, tail, ffn, half=None, convert=False):
        self.n, self.odd, self.front, self.tail, self.ffn, self.convert = n, odd, front, tail, ffn, convert
        every = len(spare_uses(True, True, True, True))
        if half is None:
            self.attn = stages_of(n)[1]
            self.uses, self.uses_before = spare_uses(*stages_of(n)), spare_uses(*stages_of(n - 1))
            self.halves, self.first = 0, sum(len(spare_uses(*stages_of(i))) for i in range(-1, n))
        else:
            self.attn = True
            self.uses = self.uses_before = spare_uses(True, True, True, True)
            start = sum(len(spare_uses(*stages_of(i))) for i in range(-1, 2))
            self.halves, self.first = every * half, start + (every if odd else 0) - 2 * every

    def spare(self, use):
        i = self.first + self.uses.index(use)
        return i % 2, self.halves + i // 2

    def spare_of_before(self, use):
        i = self.first - len(self.uses_before) + self.uses_before.index(use)
        return i % 2, self.halves + i // 2


def phase_b_steps(engine, body):
    def whole(n):
        stages = stages_of(n)
        items = [divmod(n + d, NB) if there else None for d, there in zip((1, 0, -1, -2), stages)]
        body(Step(n, n % 2, items[0], items[2], items[3], convert=n == -1))

    def inner(l):
        with engine.Fori(1, NB // 2 - 1) as pair:
            n, half = NB * l + 2 * pair + 1, NB // 2 * l + pair
            body(Step(n, 1, (l, 2 * pair + 2), (l, 2 * pair), (l, 2 * pair - 1), half))
            body(Step(n + 1, 0, (l, 2 * pair + 3), (l, 2 * pair + 1), (l, 2 * pair), half + 1))

    for n in range(-1, 3):
        whole(n)
    with engine.Fori(0, DEPTH - 1) as l:
        inner(l)
        n, half = NB * l + NB - 1, NB // 2 * l + NB // 2 - 1
        body(Step(n, 1, (l + 1, 0), (l, NB - 2), (l, NB - 3), half, convert=True))
        body(Step(n + 1, 0, (l + 1, 1), (l, NB - 1), (l, NB - 2), half + 1))
        body(Step(n + 2, 1, (l + 1, 2), (l + 1, 0), (l, NB - 1), half + 1))
        body(Step(n + 3, 0, (l + 1, 3), (l + 1, 1), (l + 1, 0), half + 2))
    inner(DEPTH - 1)
    for n in range(ITEMS - 1, ITEMS + 2):
        whole(n)


def phase_b(nc, g, d, ps):
    with ExitStack() as stack:
        s = Store(nc, stack, "b")
        s.Wraw = s.sb("Wraw", [P, RAW, 512])
        s.Whi = s.sb("Whi", [P, 3 * INNER], F32R); s.Wlo = s.sb("Wlo", [P, 3 * INNER], F32R)
        s.Wo = s.sb("Wo", [P, INNER // P, P]); s.W1 = s.sb("W1", [P, 2 * FF]); s.W2 = s.sb("W2", [P, 3, P])
        s.xhi = s.sb("xhi", [P, 2, NT], F32R); s.xlo = s.sb("xlo", [P, 2, NT], F32R)
        s.w = s.sb("w", [P, TT, 2 * INNER])
        s.vt = s.sb("vt", [P, 4, 512]); s.sq = s.sb("sq", [P, 2, 512])
        s.ss = s.sb("ss", [P, TT, 2 * HB]); s.ssm = s.sb("ssm", [P, TT, 2 * HB]); s.rn = s.sb("rn", [P, TT, 2 * HB])
        s.qkT = s.sb("qkT", [P, 2, 2 * INNER // P, NT])
        s.V = s.sb("V", [P, 2, TT, INNER])
        s.nm = s.sb("nm", [P, HB, TT]); s.ssum = s.sb("ssum", [P, HB, TT]); s.rinv = s.sb("rinv", [P, HB, TT])
        s.Pr = s.sb("Pr", [P, 4, P + KEYS])
        s.PT = s.sb("PT", [P, 4, 2 * P + WIN])
        s.o = s.sb("o", [P, TT, INNER]); s.oT = s.sb("oT", [P, INNER // P, NT])
        s.lp = s.sb("lp", [P, 7]); s.lnp = s.sb("lnp", [P, 2])
        s.xs2 = s.sb("xs2", [P, NT]); s.xtok = s.sb("xtok", [P, TT, P]); s.xnT = s.sb("xnT", [P, NT])
        s.ha = s.sb("ha", [P, 3, NT]); s.hgate = s.sb("hgate", [P, 3, NT])
        s.ff = LayerNorm(s, "ff")
        s.zeroed, s.wo_in, s.w1_in, s.w2_in, s.whi_done, s.w_ready = s.sems("zeroed wo_in w1_in w2_in whi_done w_ready")
        s.xhi_done, s.xs_ready, s.proj_done, s.act_front, s.dve_uv, s.dve_red, s.pool_add = s.sems(
            "xhi_done xs_ready proj_done act_front dve_uv dve_red pool_add")
        s.clamp_done, s.pool_r, s.s_done, s.max_done, s.exp_done, s.t_done, s.pt_ready, s.before_ready = s.sems(
            "clamp_done pool_r s_done max_done exp_done t_done pt_ready before_ready")
        s.pv_done, s.rinv_ready, s.onorm, s.lp_ready, s.lnp_ready, s.shifted, s.gelu_done, s.hg_ready, s.x_ready = s.sems(
            "pv_done rinv_ready onorm lp_ready lnp_ready shifted gelu_done hg_ready x_ready")
        s.wqkv_in = s.sems(" ".join(f"wqkv_in_{i}" for i in range(RAW)))
        s.normed = s.sems("normed_0 normed_1")
        s.spare_full = s.sems("spare_full_0 spare_full_1")
        s.spare_free = s.sems("spare_free_0 spare_free_1")
        block = stack.enter_context(nc.Block())
        S_BANK, F_BANK, T_BANK, PV_BANK, SPARE = (0, 1), (2, 3), 4, 5, (6, 7)
        OWN, BEFORE = slice(P + WIN, P + KEYS), slice(P, P + WIN)

        def started(step, slot, lag):
            if slot >= lag:
                return (step.n, slot - lag) if step.attn else (None, None)
            return (step.n - 1, slot - lag + SLOTS) if step.tail is not None else (None, None)

        @block.sync
        def _(sp):
            def load_chunks(l, pieces):
                for c in pieces:
                    wait(sp, s.w_ready, WCHUNKS * l + c + 1 - RAW)
                    sp.dma_start(s.Wraw[:, c % RAW], d["L0_ffn_Wqkv"][l, :, c * 512:(c + 1) * 512]).then_inc(s.wqkv_in[c % RAW], 16)

            for l in range(DEPTH):
                load_chunks(l, range(RAW if l == 0 else WCHUNKS))
                if l:
                    sp.wait_ge(s.shifted, NB * l)
                sp.dma_start(s.Wo[:], d["L0_ffn_Wo"][l].rearrange("(c p) n -> p c n", p=P)).then_inc(s.wo_in, 16)
                if l:
                    sp.wait_ge(s.gelu_done, NB * l)
                sp.dma_start(s.W1[:], d["L0_ffn_W1"][l]).then_inc(s.w1_in, 16)
                if l:
                    sp.wait_ge(s.x_ready, NB * l + NB)
                sp.dma_start(s.W2[:, 0:2], d["L0_ffn_W2"][l, 0:2 * P].rearrange("(c p) n -> p c n", p=P)).then_inc(s.w2_in, 16)
                sp.dma_start(s.W2[0:FF - 2 * P, 2], d["L0_ffn_W2"][l, 2 * P:FF]).then_inc(s.w2_in, 16)
                if l == 0:
                    load_chunks(0, range(RAW, WCHUNKS))
            for loaded in s.wqkv_in:
                sp.wait_ge(loaded, 16 * WCHUNKS // RAW * DEPTH)
            sp.wait_ge(s.wo_in, 16 * DEPTH)
            sp.wait_ge(s.w1_in, 16 * DEPTH)
            sp.wait_ge(s.w2_in, 32 * DEPTH)

        @block.tensor
        def _(pe):
            def body(step):
                n, f, t, u = step.n, step.n + 1, step.n - 1, step.n - 2
                pf, pa = 1 - step.odd, step.odd

                def take_spare(use):
                    bank, uses = step.spare(use)
                    wait(pe, s.spare_free[bank], uses)
                    return ps[:, SPARE[bank]]

                def give_spare(use, last):
                    last.then_inc(s.spare_full[step.spare(use)[0]], 1)

                def read_out(bank_uses):
                    bank, uses = bank_uses
                    pe.wait_ge(s.spare_free[bank], uses + 1)

                def transpose_qk(item, which):
                    tt, four = which
                    bank = take_spare(("tr", which))
                    pe.wait_ge(s.normed[tt], item + 1)
                    for i in range(4):
                        c = four * 4 + i
                        last = nc.tensor.transpose(bank[:, i * P:(i + 1) * P], s.w[:, tt, c * P:(c + 1) * P], g.ident[:])
                    give_spare(("tr", which), last)

                def values(slot):
                    item, k = started(step, slot, PV_LAG)
                    if k is None:
                        return
                    pe.wait_ge(s.pt_ready, HB * item + k + 1)
                    pe.wait_ge(s.before_ready, HB * item + k + 1)
                    if k == 0:
                        pe.wait_ge(s.act_front, len(PIECES) * (item + 1))
                    if k % 4 == 0:
                        wait(pe, s.onorm, 4 * item + k // 4)
                    pt, v, col = s.PT[:, k % 4], s.V[:, pa if slot >= PV_LAG else 1 - pa], k * DB
                    out = ps[:, PV_BANK].rearrange("p (h t e) -> p h t e", h=4, t=TT)[:, k % 4]
                    nc.tensor.matmul(out[:, 0], pt[:, 0:P], v[:, 0, col:col + DB], start=True, stop=True)
                    nc.tensor.matmul(out[:, 1], pt[:, P:2 * P], v[:, 1, col:col + DB], start=True, stop=False, skip_group_check=True)
                    nc.tensor.matmul(out[0:WIN, 1], pt[P - WIN:P, 2 * P:], v[P - WIN:P, 0, col:col + DB], start=False, stop=True,
                                     skip_group_check=True).then_inc(s.pv_done, 1)

                for slot in range(SLOTS):
                    if step.attn:
                        h = slot
                        bank, r, pair = S_BANK[h % 2], DB * (h % 2), h // 2
                        if h == 0:
                            read_out(step.spare_of_before(("tr", (1, 0))))
                            read_out(step.spare_of_before(("tr", (1, 2))))
                        if h == HB // 2:
                            read_out(step.spare(("tr", (1, 1))))
                            read_out(step.spare(("tr", (1, 3))))
                        wait(pe, s.exp_done, HB * n + h - 1)
                        q, k = s.qkT[r:r + DB, pa, pair], s.qkT[r:r + DB, pa, INNER // P + pair]
                        nc.tensor.matmul(ps[:, bank, 0:TT * KEYS], g.ident_bf[:], g.mask_bf[:], start=True, stop=False, skip_group_check=True)
                        nc.tensor.matmul(ps[:, bank, WIN:KEYS], q[:, 0:P], k[:, 0:P], start=False, stop=False, skip_group_check=True)
                        nc.tensor.matmul(ps[:, bank, KEYS:2 * KEYS], q[:, P:NT], k[:, P - WIN:NT], start=False, stop=True,
                                         skip_group_check=True).then_inc(s.s_done, 1)
                    if step.front is not None and slot < len(PIECES):
                        tt, c = PIECES[slot]
                        N = len(PIECES)
                        if slot == 0:
                            pe.wait_ge(s.xs_ready, f + 1)
                        if tt == 0:
                            pe.wait_ge(s.w_ready, WCHUNKS * step.front[0] + c + 1)
                        wait(pe, s.act_front, N * f + slot - 1)
                        if slot - 2 in QK:
                            pe.wait_ge(s.dve_uv, N_QK * f + QK.index(slot - 2) + 1)
                        rows, cols = slice(tt * P, (tt + 1) * P), slice(c * 512, (c + 1) * 512)
                        nc.tensor.matmul(ps[:, F_BANK[slot % 2]], s.xlo[:, pf, rows], s.Whi[:, cols], start=True, stop=False)
                        nc.tensor.matmul(ps[:, F_BANK[slot % 2]], s.xhi[:, pf, rows], s.Wlo[:, cols], start=False, stop=False)
                        nc.tensor.matmul(ps[:, F_BANK[slot % 2]], s.xhi[:, pf, rows], s.Whi[:, cols], start=False, stop=True).then_inc(s.proj_done, 1)
                    item, k = started(step, slot, T_LAG)
                    if k is not None:
                        pe.wait_ge(s.exp_done, HB * item + k + 1)
                        wait(pe, s.pt_ready, HB * item + k)
                        nc.tensor.transpose(ps[:, T_BANK, 0:P], s.Pr[:, k % 4, 0:P], g.ident[:])
                        nc.tensor.transpose(ps[:, T_BANK, P:2 * P], s.Pr[:, k % 4, OWN], g.ident[:]).then_inc(s.t_done, 1)
                    if step.tail is not None:
                        lt = step.tail[0]
                        for tt, half in OUT_SLOT.get(slot, ()):
                            use = ("out", (tt, half))
                            bank = take_spare(use)
                            pe.wait_ge(s.onorm, 4 * t + 2 * half + 2)
                            for i in range(4):
                                c = half * 4 + i
                                last = nc.tensor.transpose(bank[:, i * P:(i + 1) * P], s.o[:, tt, c * P:(c + 1) * P], g.ident[:])
                            give_spare(use, last)
                        if slot == WO_SLOT:
                            bank = take_spare(("wo", 0))
                            for tt in range(TT):
                                read_out(step.spare(("out", (tt, 1))))
                            pe.wait_ge(s.wo_in, 16 * lt + 16)
                            for c in range(INNER // P):
                                last = nc.tensor.matmul(bank[:, 0:NT], s.Wo[:, c], s.oT[:, c], start=c == 0, stop=c == INNER // P - 1)
                            give_spare(("wo", 0), last)
                        if slot == XT_SLOT:
                            bank = take_spare(("xt", 0))
                            pe.wait_ge(s.shifted, t + 1)
                            for tt in range(TT):
                                last = nc.tensor.transpose(bank[:, tt * P:(tt + 1) * P], s.xs2[:, tt * P:(tt + 1) * P], g.ident[:])
                            give_spare(("xt", 0), last)
                        if slot == XN_SLOT:
                            bank = take_spare(("xn", 0))
                            pe.wait_ge(s.ff.normed, t + 1)
                            for tt in range(TT):
                                last = nc.tensor.transpose(bank[:, tt * P:(tt + 1) * P], s.ff.xn[:, tt], g.ident[:])
                            give_spare(("xn", 0), last)
                    if step.ffn is not None:
                        lu = step.ffn[0]
                        if slot in W1_SLOT:
                            c = W1_SLOT[slot]
                            c0, width = FF_CHUNKS[c]
                            bank = take_spare(("w1", c))
                            if c == 0:
                                pe.wait_ge(s.w1_in, 16 * lu + 16)
                                read_out(step.spare_of_before(("xn", 0)))
                            for half in range(2):
                                last = nc.tensor.matmul(bank[0:width, half * NT:(half + 1) * NT],
                                                        s.W1[:, half * FF + c0:half * FF + c0 + width], s.xnT[:], start=True, stop=True)
                            give_spare(("w1", c), last)
                        if slot == W2_SLOT:
                            bank = take_spare(("w2", 0))
                            pe.wait_ge(s.w2_in, 32 * lu + 32)
                            pe.wait_ge(s.hg_ready, u + 1)
                            for c, (_, width) in enumerate(FF_CHUNKS):
                                last = nc.tensor.matmul(bank[:, 0:NT], s.W2[0:width, c], s.ha[0:width, c], start=c == 0, stop=c == 2)
                            give_spare(("w2", 0), last)
                    values(slot)
                    if step.attn and slot in LATE_SLOT:
                        transpose_qk(n, LATE_SLOT[slot])
                    if step.front is not None and slot in TRANSPOSE_SLOT:
                        transpose_qk(f, TRANSPOSE_SLOT[slot])

            phase_b_steps(pe, body)

        @block.scalar
        def _(act):
            act.wait_ge(s.zeroed, 1)

            def body(step):
                n, f, t, u = step.n, step.n + 1, step.n - 1, step.n - 2
                pf, pa = 1 - step.odd, step.odd

                def full_spare(use):
                    bank, uses = step.spare(use)
                    act.wait_ge(s.spare_full[bank], uses + 1)
                    return bank

                def store_qk(parity, which):
                    tt, four = which
                    bank = full_spare(("tr", which))
                    nc.scalar.activation(s.qkT[:, parity, four * 4:four * 4 + 4, tt * P:(tt + 1) * P],
                                         ps[:, SPARE[bank]].rearrange("p (c t) -> p c t", c=4), ACT.Copy).then_inc(s.spare_free[bank], 1)

                def exps(slot):
                    if not step.attn:
                        return
                    h = slot
                    bank = S_BANK[h % 2]
                    act.wait_ge(s.max_done, HB * n + h + 1)
                    wait(act, s.t_done, HB * n + h - 3)
                    wait(act, s.before_ready, HB * n + h - 3)
                    nc.scalar.activation(s.Pr[:, h % 4, 0:P], ps[:, bank, WIN:KEYS], ACT.Exp,
                                         bias=s.nm[:, h, 0:1], accum_out=s.ssum[:, h, 0:1])
                    nc.scalar.activation(s.Pr[:, h % 4, P:], ps[:, bank, KEYS:2 * KEYS], ACT.Exp,
                                         bias=s.nm[:, h, 1:2], accum_out=s.ssum[:, h, 1:2]).then_inc(s.exp_done, 1)

                for slot in range(SLOTS):
                    if step.convert:
                        for c in ((0, 1) if slot == 0 else (slot + 1,) if slot < WCHUNKS - 1 else ()):
                            act.wait_ge(s.wqkv_in[c % RAW], 16 * (WCHUNKS // RAW) * step.front[0] + 16 * (c // RAW) + 16)
                            if c == 0:
                                wait(act, s.proj_done, len(PIECES) * f)
                            nc.scalar.activation(s.Whi[:, c * 512:(c + 1) * 512], s.Wraw[:, c % RAW], ACT.Copy).then_inc(s.whi_done, 1)
                    if step.front is not None and slot < len(PIECES):
                        tt, c = PIECES[slot]
                        act.wait_ge(s.proj_done, len(PIECES) * f + slot + 1)
                        if c < 4:
                            i = QK.index(slot)
                            wait(act, s.dve_red, N_QK * f + i - 1)
                            nc.scalar.activation(s.sq[:, i % 2], ps[:, F_BANK[slot % 2]], ACT.Square).then_inc(s.act_front, 1)
                        else:
                            if (tt, c) == (0, 4):
                                wait(act, s.pv_done, HB * (f - 1))
                            nc.scalar.activation(s.V[:, pf, tt, (c - 4) * 512:(c - 3) * 512], ps[:, F_BANK[slot % 2]],
                                                 ACT.Copy).then_inc(s.act_front, 1)
                    item, k = started(step, slot, T_LAG)
                    if k is not None:
                        act.wait_ge(s.t_done, HB * item + k + 1)
                        wait(act, s.pv_done, HB * item + k - 3)
                        nc.scalar.activation(s.PT[:, k % 4, 0:2 * P], ps[:, T_BANK, 0:2 * P], ACT.Copy).then_inc(s.pt_ready, 1)
                    exps(slot)
                    if step.tail is not None:
                        for tt, half in OUT_SLOT.get(slot, ()):
                            bank = full_spare(("out", (tt, half)))
                            nc.scalar.activation(s.oT[:, half * 4:half * 4 + 4, tt * P:(tt + 1) * P],
                                                 ps[:, SPARE[bank]].rearrange("p (c t) -> p c t", c=4), ACT.Copy).then_inc(s.spare_free[bank], 1)
                        if slot == XN_SLOT:
                            bank = full_spare(("xn", 0))
                            act.wait_ge(s.lnp_ready, t + 1)
                            nc.scalar.activation(s.xnT[:], ps[:, SPARE[bank], 0:NT], ACT.Identity, bias=s.lnp[:, 1:2],
                                                 scale=s.lnp[:, 0:1]).then_inc(s.spare_free[bank], 1)
                    if step.ffn is not None:
                        if slot in W1_SLOT:
                            c = W1_SLOT[slot]
                            width = FF_CHUNKS[c][1]
                            act.wait_ge(s.lp_ready, u + 1)
                            bank = full_spare(("w1", c))
                            nc.scalar.activation(s.hgate[0:width, c], ps[0:width, SPARE[bank], NT:2 * NT], ACT.Identity, bias=s.lp[0:width, 4 + c:5 + c])
                            nc.scalar.activation(s.ha[0:width, c], ps[0:width, SPARE[bank], 0:NT], ACT.Identity,
                                                 bias=s.lp[0:width, 1 + c:2 + c]).then_inc(s.spare_free[bank], 1)
                        if slot == GELU_SLOT:
                            for c in range(3):
                                b, uses = step.spare(("w1", c))
                                act.wait_ge(s.spare_free[b], uses + 1)
                            nc.scalar.activation(s.hgate[:], s.hgate[:], ACT.Gelu).then_inc(s.gelu_done, 1)
                    if step.attn and slot in LATE_SLOT:
                        store_qk(pa, LATE_SLOT[slot])
                    if step.front is not None and slot in TRANSPOSE_SLOT:
                        if slot == min(TRANSPOSE_SLOT):
                            wait(act, s.s_done, HB * (f - 1))
                        store_qk(pf, TRANSPOSE_SLOT[slot])

            phase_b_steps(act, body)

        @block.vector
        def _(dve):
            for buffer in (s.xhi, s.xlo):
                nc.vector.memset(buffer[:].bitcast(F32), 0.0)
            for buffer in (s.xs2, s.ha):
                nc.vector.memset(buffer[:], 0.0)
            nc.vector.memset(s.hgate[:], 0.0).then_inc(s.zeroed, 1)
            dve.wait_ge(s.zeroed, 1)
            dve.sem_inc(s.x_ready, NB)
            lower, upper = slice(0, P // 2), slice(P // 2, P)

            def split_input(item, parity, src):
                dve.wait_ge(s.x_ready, item + 1)
                wait(dve, s.proj_done, len(PIECES) * (item - 1))
                own, shifted = g.xT[lower, bass.ds(src, NT)], g.xT[upper, bass.ds(src, NT - 1)]
                nc.vector.tensor_scalar_mul(s.xhi[lower, parity], own, 1.0)
                nc.vector.tensor_scalar_mul(s.xhi[upper, parity, 1:NT], shifted, 1.0).then_inc(s.xhi_done, 1)
                dve.wait_ge(s.xhi_done, item + 1)
                nc.vector.tensor_tensor(s.xlo[lower, parity], own, s.xhi[lower, parity].bitcast(F32), ALU.subtract)
                nc.vector.tensor_tensor(s.xlo[upper, parity, 1:NT], shifted, s.xhi[upper, parity, 1:NT].bitcast(F32), ALU.subtract).then_inc(s.xs_ready, 1)

            def body(step):
                n, f, t, u = step.n, step.n + 1, step.n - 1, step.n - 2

                def full_spare(use):
                    bank, uses = step.spare(use)
                    dve.wait_ge(s.spare_full[bank], uses + 1)
                    return bank

                def known(value):
                    return value if isinstance(value, int) else dve.snap(value)

                if step.front is not None:
                    lf = known(step.front[0])
                    next_src = known((step.front[1] + 1) % NB * NT)
                if step.tail is not None:
                    lt, dst = known(step.tail[0]), known(step.tail[1] * NT)
                    x_lower, x_upper, x_all = g.xT[lower, bass.ds(dst, NT)], g.xT[upper, bass.ds(dst, NT - 1)], g.xT[:, bass.ds(dst, NT)]
                if step.ffn is not None:
                    lu, end = known(step.ffn[0]), known(step.ffn[1] * NT)
                    x_end = g.xT[:, bass.ds(end, NT)]
                    nc.vector.tensor_scalar_mul(s.lp[:], g.lparam[:, bass.ds(lu, 1), 2:9].rearrange("p a k -> p (a k)"), 1.0).then_inc(s.lp_ready, 1)
                def divide(slot):
                    item, k = started(step, slot, PV_LAG + 1)
                    if k is None or k % 4 != 3:
                        return
                    i = k // 4
                    heads = slice(4 * i, 4 * i + 4)
                    dve.wait_ge(s.pv_done, HB * item + k + 1)
                    nc.vector.reciprocal(s.rinv[:, heads], s.ssum[:, heads]).then_inc(s.rinv_ready, 1)
                    if i == 0 and step.tail is not None:
                        full_spare(("out", (0, 1)))
                        full_spare(("out", (1, 1)))
                    dve.wait_ge(s.rinv_ready, 4 * item + i + 1)
                    pv = ps[:, PV_BANK].rearrange("p (h t e) -> p h t e", h=4, t=TT)
                    for tt in range(TT):
                        last = nc.vector.tensor_tensor(s.o[:, tt, i * 4 * DB:(i + 1) * 4 * DB].rearrange("p (h e) -> p h e", e=DB),
                                                       pv[:, :, tt], s.rinv[:, heads, tt:tt + 1].broadcast_to((P, 4, DB)), ALU.mult)
                    last.then_inc(s.onorm, 1)

                for slot in range(SLOTS):
                    if step.convert:
                        for c in ((0, 1) if slot == 0 else (slot + 1,) if slot < WCHUNKS - 1 else ()):
                            cols = slice(c * 512, (c + 1) * 512)
                            dve.wait_ge(s.whi_done, WCHUNKS * lf + c + 1)
                            nc.vector.tensor_tensor(s.Wlo[:, cols], s.Wraw[:, c % RAW], s.Whi[:, cols].bitcast(F32), ALU.subtract).then_inc(s.w_ready, 1)
                    divide(slot)
                    if step.attn:
                        h = slot
                        dve.wait_ge(s.s_done, HB * n + h + 1)
                        nc.vector.tensor_reduce(s.nm[:, h], ps[:, S_BANK[h % 2], 0:TT * KEYS].rearrange("p (t k) -> p t k", t=TT),
                                                AX.X, ALU.max, negate=True).then_inc(s.max_done, 1)
                    item, k = started(step, slot, T_LAG)
                    if k is not None:
                        dve.wait_ge(s.exp_done, HB * item + k + 1)
                        wait(dve, s.pv_done, HB * item + k - 3)
                        nc.vector.transpose(s.PT[P - WIN:P, k % 4, 2 * P:], s.Pr[0:WIN, k % 4, BEFORE]).then_inc(s.before_ready, 1)
                    if step.front is not None and slot in QK:
                        tt, c = PIECES[slot]
                        which, i = c // 2, QK.index(slot)
                        dve.wait_ge(s.act_front, len(PIECES) * f + slot + 1)
                        if step.attn and c == 0:
                            for use in ((0, 1), (0, 3)) if tt == 0 else ((1, 1), (1, 3)):
                                b, uses = step.spare_of_before(("tr", use)) if tt == 0 else step.spare(("tr", use))
                                dve.wait_ge(s.spare_full[b], uses + 1)
                        wait(dve, s.pool_add, N_QK * f + i - 3)
                        raw = ps[:, F_BANK[slot % 2]].rearrange("p (h z e) -> p h z e", z=2, e=DB // 2)
                        turned = s.vt[:, i % 4].rearrange("p (h z e) -> p h z e", z=2, e=DB // 2)
                        sin = g.rotab[:, bass.ds(lf, 1), 2 * which + 1, tt]
                        nc.vector.tensor_tensor(s.w[:, tt, c * 512:(c + 1) * 512].rearrange("p (h e) -> p h e", e=DB),
                                                ps[:, F_BANK[slot % 2]].rearrange("p (h e) -> p h e", e=DB),
                                                g.rotab[:, bass.ds(lf, 1), 2 * which, tt].broadcast_to((P, 8, DB)), ALU.mult)
                        for z in range(2):
                            last = nc.vector.tensor_tensor(turned[:, :, z], raw[:, :, 1 - z],
                                                           sin[:, :, z * (DB // 2):(z + 1) * (DB // 2)].broadcast_to((P, 8, DB // 2)), ALU.mult)
                        last.then_inc(s.dve_uv, 1)
                        nc.vector.tensor_reduce(s.ss[:, tt, c * 8:(c + 1) * 8], s.sq[:, i % 2].rearrange("p (h e) -> p h e", e=DB),
                                                AX.X, ALU.add).then_inc(s.dve_red, 1)
                        if c == 3:
                            dve.wait_ge(s.dve_red, N_QK * f + i + 1)
                            nc.vector.tensor_scalar_max(s.ssm[:, tt], s.ss[:, tt], 1e-24).then_inc(s.clamp_done, 1)
                    if step.tail is not None:
                        if slot == RES_SLOT:
                            bank = full_spare(("wo", 0))
                            nc.vector.tensor_tensor(x_all, ps[:, SPARE[bank], 0:NT], x_all, ALU.add).then_inc(s.spare_free[bank], 1)
                            dve.wait_ge(s.spare_free[bank], step.spare(("wo", 0))[1] + 1)
                            nc.vector.tensor_scalar_mul(s.xs2[lower], x_lower, 1.0)
                            nc.vector.tensor_scalar_mul(s.xs2[upper, 1:NT], x_upper, 1.0).then_inc(s.shifted, 1)
                        if slot == STATS_SLOT:
                            bank = full_spare(("xt", 0))
                            nc.vector.tensor_copy(s.xtok[:], ps[:, SPARE[bank], 0:NT].rearrange("p (t e) -> p t e", t=TT)).then_inc(s.spare_free[bank], 1)
                            dve.wait_ge(s.spare_free[bank], step.spare(("xt", 0))[1] + 1)
                            layernorm_stats(nc, dve, s.ff, s.xtok, t)
                        if slot == NORMED_SLOT:
                            layernorm_apply(nc, dve, s.ff, s.xtok, t)
                            nc.vector.tensor_scalar_mul(s.lnp[:], g.lparam[:, bass.ds(lt, 1), 0:2].rearrange("p a k -> p (a k)"), 1.0).then_inc(s.lnp_ready, 1)
                    if step.front is not None and slot in NORM_SLOT:
                        tt = NORM_SLOT[slot]
                        dve.wait_ge(s.pool_r, TT * f + tt + 1)
                        dve.wait_ge(s.pool_add, N_QK * f + 4 * tt + 4)
                        rows = s.w[:, tt].rearrange("p (h e) -> p h e", e=DB)
                        nc.vector.tensor_tensor(rows, rows, s.rn[:, tt].rearrange("p (h o) -> p h o", o=1).broadcast_to((P, 2 * HB, DB)),
                                                ALU.mult).then_inc(s.normed[tt], 1)
                    if step.front is not None and slot == SPLIT_SLOT:
                        split_input(f + 1, step.odd, next_src)
                    if step.ffn is not None and slot == END_SLOT:
                        bank = full_spare(("w2", 0))
                        nc.vector.scalar_tensor_tensor(out=x_end, in0=ps[:, SPARE[bank], 0:NT], scalar=s.lp[:, 0:1], in1=x_end,
                                                       op0=ALU.add, op1=ALU.add).then_inc(s.spare_free[bank], 1)
                        dve.wait_ge(s.spare_free[bank], step.spare(("w2", 0))[1] + 1)
                        dve.sem_inc(s.x_ready, 1)

            split_input(0, 0, 0)
            phase_b_steps(dve, body)

        @block.gpsimd
        def _(pool):
            def body(step):
                f, t, u = step.n + 1, step.n - 1, step.n - 2
                for slot in range(SLOTS):
                    if step.front is not None and slot in QK:
                        tt, c = PIECES[slot]
                        i = QK.index(slot)
                        pool.wait_ge(s.dve_uv, N_QK * f + i + 1)
                        rows = s.w[:, tt, c * 512:(c + 1) * 512]
                        nc.gpsimd.tensor_tensor(rows, rows, s.vt[:, i % 4], ALU.add).then_inc(s.pool_add, 1)
                    if step.front is not None and slot in POWER_SLOT:
                        tt = POWER_SLOT[slot]
                        pool.wait_ge(s.clamp_done, TT * f + tt + 1)
                        nc.gpsimd.tensor_tensor(s.rn[:, tt], s.ssm[:, tt], g.neg_half[:], ALU.pow).then_inc(s.pool_r, 1)
                    if step.front is not None and slot in POOL_NORM_SLOT:
                        tt = POOL_NORM_SLOT[slot]
                        pool.wait_ge(s.pool_r, TT * f + tt + 1)
                        pool.wait_ge(s.pool_add, N_QK * f + 4 * tt + 4)
                        rows = s.w[:, tt].rearrange("p (h e) -> p h e", e=DB)
                        nc.gpsimd.tensor_tensor(rows, rows, s.rn[:, tt].rearrange("p (h o) -> p h o", o=1).broadcast_to((P, 2 * HB, DB)),
                                                ALU.mult).then_inc(s.normed[tt], 1)
                    if step.ffn is not None and slot == GATE_SLOT:
                        pool.wait_ge(s.gelu_done, u + 1)
                        nc.gpsimd.tensor_tensor(s.ha[:], s.ha[:], s.hgate[:], ALU.mult).then_inc(s.hg_ready, 1)
                    if step.tail is not None and slot == STATS_SLOT:
                        layernorm_pool(nc, pool, s.ff, g, t)

            phase_b_steps(pool, body)



PAIRS = NS // 2
B_SLOT = {i: i for i in range(PAIRS)}
SCAN_SLOT = {5: 0, 9: 1}
C_SLOT = {8 + i: i for i in range(PAIRS)}
SUM_LAG = 10
X3_SLOT, X3_TR_SLOT, X3_TOK_SLOT, STATS1_SLOT, NORMED1_SLOT, H_TR_SLOT, HT_SLOT, IN_SLOT, XP_SLOT, CONV_SLOT, SILU_SLOT = 0, 2, 3, 4, 6, 9, 9, 9, 12, 14, 14
XD_SLOT, SPLIT_XD_SLOT, DL_SLOT, Z_SLOT, SOFTPLUS_SLOT, DELTA_SLOT = 0, 1, 3, 3, 5, 8
Y_SLOT, OP_SLOT, X4_SLOT, X4_TR_SLOT, X4_TOK_SLOT, STATS2_SLOT, NORMED2_SLOT, H2_TR_SLOT, HT2_SLOT, LIN_SLOT, X5_SLOT = 1, 5, 5, 6, 9, 9, 10, 12, 14, 15, 15
OUT_SLOT_C, XOUT_SLOT = 2, 2
POOL_B, POOL_C = (3, 4, 6), (1, 3, 5)
N_POOL = len(POOL_B) + len(POOL_C)
DVE_B = [i for i in range(PAIRS) if i not in POOL_B]
DVE_C = [i for i in range(PAIRS) if i not in POOL_C]
FACTOR_SLOT = {9: (0, 7), 10: (7, 14), 11: (14, 20), 12: (20, 26), 13: (26, 32)}


class StepC:

    def __init__(self, n, odd, inner, delta, states, tail, store):
        self.n, self.odd, self.inner, self.delta, self.states, self.tail, self.store = n, odd, inner, delta, states, tail, store


def phase_c_steps(engine, body):
    def whole(n):
        body(StepC(n, n % 2, *[0 <= n + d < NB for d in (2, 1, 0, -1, -2)]))

    for n in range(-2, 2):
        whole(n)
    with engine.Fori(1, NB // 2 - 1) as pair:
        for odd in range(2):
            body(StepC(2 * pair + odd, odd, True, True, True, True, True))
    for n in range(NB - 2, NB + 2):
        whole(n)


def phase_c(nc, g, d, ps, out):
    with ExitStack() as stack:
        s = Store(nc, stack, "c")
        s.Win = s.sb("Win", [P, 2 * CH]); s.Wout = s.sb("Wout", [P, CC, P])
        s.Wx = s.sb("Wx", [P, CC, P])
        s.Wdt = s.sb("Wdt", [P, CH])
        s.sel = s.sb("sel", [2 * XBC, XBC, P], F32R)
        s.conv_diag = s.sb("conv_diag", [P, CC, TAPS, P]); s.D_diag = s.sb("D_diag", [P, CC, P])
        s.md_x3 = s.sb("md_x3", [P, 1]); s.md_inner = s.sb("md_inner", [P, 2]); s.md_tail = s.sb("md_tail", [P, 4])
        s.x3T = s.sb("x3T", [P, NT]); s.x3tok = s.sb("x3tok", [P, TT, P]); s.hT = s.sb("hT", [P, NT]); s.hT2 = s.sb("hT2", [P, NT])
        s.xp = s.sb("xp", [P, CC, TAPS - 1 + NT]); s.h = s.sb("h", [P, 2, CC, NT]); s.sr = s.sb("sr", [P, 4, CC, NT])
        s.xbc = s.sb("xbc", [2 * XBC, 2, NT], F32R)
        s.dlt = s.sb("dlt", [P, NT]); s.zb = s.sb("zb", [P, CC, NT]); s.za = s.sb("za", [P, CC, NT]); s.delta = s.sb("delta", [P, CC, NT]); s.du = s.sb("du", [P, 2, CC, NT])
        s.dA = s.sb("dA", [P, 2, CC, NS, NT]); s.bu = s.sb("bu", [P, CC, NS, NT]); s.rows = s.sb("rows", [P, 2, 2, NT])
        s.y = s.sb("y", [P, CC, NT]); s.x4T = s.sb("x4T", [P, NT]); s.x4tok = s.sb("x4tok", [P, TT, P]); s.tmp = s.sb("tmp", [P, NT]); s.x5T = s.sb("x5T", [P, NT]); s.xout = s.sb("xout", [P, TT, P])
        s.l1 = LayerNorm(s, "l1"); s.l2 = LayerNorm(s, "l2")
        s.w_in, s.zeroed, s.built, s.md_ready, s.x3_ready, s.x3_kept, s.x3_full, s.x3tok_ready, s.h_full, s.hT_ready = s.sems(
            "w_in zeroed built md_ready x3_ready x3_kept x3_full x3tok_ready h_full hT_ready")
        s.in_full, s.xp_ready, s.conv_full, s.gate_ready, s.h_ready, s.xd_full, s.rounded, s.xd_ready, s.dl_full = s.sems(
            "in_full xp_ready conv_full gate_ready h_ready xd_full rounded xd_ready dl_full")
        s.zb_ready, s.abs_done, s.exp_done, s.sp_done, s.delta_ready, s.du_ready, s.dA_ready, s.b_full, s.c_full = s.sems(
            "zb_ready abs_done exp_done sp_done delta_ready du_ready dA_ready b_full c_full")
        s.bu_dve, s.yc_dve, s.pool_mult, s.rows_ready, s.scan_done, s.y_full, s.y_ready, s.op_full = s.sems(
            "bu_dve yc_dve pool_mult rows_ready scan_done y_full y_ready op_full")
        s.md_tail_ready, s.x4_ready, s.x4_full, s.x4tok_ready, s.h2_full, s.hT2_ready, s.lin_full, s.tmp_ready, s.x5_ready = s.sems(
            "md_tail_ready x4_ready x4_full x4tok_ready h2_full hT2_ready lin_full tmp_ready x5_ready")
        s.out_full, s.xout_ready, s.stored = s.sems("out_full xout_ready stored")
        block = stack.enter_context(nc.Block())
        B_BANK, C_BANK, Y_BANK, F_BANK, G_BANK, TAIL_BANK = (0, 1), (2, 3), 4, 5, 6, 7
        RANK_ROWS = slice(2 * XBC, 2 * XBC + RANK)

        def wait_bu(engine, item, i):
            if i in POOL_B:
                engine.wait_ge(s.pool_mult, N_POOL * item + POOL_B.index(i) + 1)
            else:
                engine.wait_ge(s.bu_dve, len(DVE_B) * item + DVE_B.index(i) + 1)

        def wait_yc(engine, item, i):
            if i in POOL_C:
                engine.wait_ge(s.pool_mult, N_POOL * item + len(POOL_B) + POOL_C.index(i) + 1)
            else:
                engine.wait_ge(s.yc_dve, len(DVE_C) * item + DVE_C.index(i) + 1)

        def copies(slot):
            found = [(POOL_B.index(i), False, i) for i in POOL_B if B_SLOT[i] == slot]
            return found + [(len(POOL_B) + POOL_C.index(C_SLOT[slot]), True, C_SLOT[slot])] if C_SLOT.get(slot) in POOL_C else found

        @block.sync
        def _(sp):
            wx = d["L1_attn_x_proj_w"].rearrange("(c p) n -> p c n", p=P)
            for dst, src in ((s.Win[:], d["L1_attn_in_proj_w"]), (s.Wx[:, :, 0:XBC], wx[:, :, RANK:XD]), (s.Wx[:, :, XBC:2 * XBC], wx[:, :, RANK:XD]),
                             (s.Wx[:, :, RANK_ROWS], wx[:, :, 0:RANK]), (s.Wdt[RANK_ROWS], d["L1_attn_dt_proj_w"]),
                             (s.Wout[:], d["L1_attn_out_proj_w"].rearrange("(c p) n -> p c n", p=P))):
                sp.dma_start(dst, src).then_inc(s.w_in, 16)
            with sp.Fori(0, NB) as n:
                sp.wait_ge(s.xout_ready, n + 1)
                sp.dma_start(out[bass.ds(n, 1)].rearrange("b (t p) e -> p (b t) e", p=P), s.xout[:]).then_inc(s.stored, 16)
            sp.wait_ge(s.stored, 16 * NB + 16)

        @block.vector
        def _(dve):
            nc.vector.memset(s.dA[:, :, :, :, 0:1], 0.0)
            nc.vector.memset(s.xp[:, :, 0:TAPS - 1], 0.0).then_inc(s.zeroed, 1)
            for c in range(CC):
                for k in range(TAPS):
                    nc.vector.tensor_scalar_mul(s.conv_diag[:, c, k], g.ident[:], g.conv_w[:, c, k:k + 1])
                nc.vector.tensor_scalar_mul(s.D_diag[:, c], g.ident[:], g.D[:, c:c + 1])
            once, again = (g.ident[0:2 * XBC, a:a + XBC].rearrange("p (k o) -> p k o", o=1).broadcast_to((2 * XBC, XBC, P)) for a in (0, XBC))
            nc.vector.tensor_tensor(s.sel[:], once, again, ALU.add).then_inc(s.built, 1)

            def body(step):
                n, m, f, t = step.n, step.n + 2, step.n + 1, step.n - 1
                own, other = step.odd, 1 - step.odd

                def known(value):
                    return value if isinstance(value, int) else dve.snap(value)

                def copy_mod(dst, l, seq, a, b):
                    return nc.vector.tensor_scalar_mul(dst[:], g.mod[:, l, bass.ds(seq, 1), a:b].rearrange("p a k -> p (a k)"), 1.0)

                if step.inner:
                    m_seq, m_at = known(m), known(m * NT)
                if step.tail:
                    t_at, gate = known(t * NT), known(t & 3)
                    copy_mod(s.md_tail, 1, known(t), 2, 6).then_inc(s.md_tail_ready, 1)
                for slot in range(SLOTS):
                    if step.inner and slot == X3_SLOT:
                        wait(dve, s.hT_ready, m)
                        copy_mod(s.md_inner, 1, m_seq, 0, 2)
                        copy_mod(s.md_x3, 0, m_seq, 5, 6).then_inc(s.md_ready, 1)
                        wait(dve, s.x3_kept, m)
                        dve.wait_ge(s.md_ready, m + 1)
                        nc.vector.scalar_tensor_tensor(out=s.x3T[:], in0=g.xT[:, bass.ds(m_at, NT)], scalar=s.md_x3[:], in1=g.x2T[:, bass.ds(m_at, NT)],
                                                       op0=ALU.mult, op1=ALU.add).then_inc(s.x3_ready, 1)
                    if step.states and slot in DVE_B:
                        dve.wait_ge(s.b_full, PAIRS * n + slot + 1)
                        dve.wait_ge(s.du_ready, n + 1)
                        for c in range(CC):
                            last = nc.vector.tensor_tensor(s.bu[:, c, 2 * slot:2 * slot + 2], s.du[:, own, c:c + 1].broadcast_to((P, 2, NT)),
                                                           ps[:, B_BANK[slot % 2]].rearrange("p (n t) -> p n t", n=2), ALU.mult)
                        last.then_inc(s.bu_dve, 1)
                    if step.delta and slot == SPLIT_XD_SLOT:
                        dve.wait_ge(s.xd_full, f + 1)
                        nc.vector.tensor_scalar_mul(s.xbc[:, other], ps[0:2 * XBC, G_BANK, 0:NT], 1.0).then_inc(s.rounded, 1)
                        dve.wait_ge(s.rounded, f + 1)
                        rest = slice(XBC, 2 * XBC)
                        nc.vector.tensor_tensor(s.xbc[rest, other], ps[rest, G_BANK, 0:NT], s.xbc[rest, other].bitcast(F32), ALU.subtract)
                        nc.vector.tensor_copy(s.dlt[RANK_ROWS], ps[RANK_ROWS, G_BANK, 0:NT]).then_inc(s.xd_ready, 1)
                    if step.tail and slot == Y_SLOT:
                        dve.wait_ge(s.y_full, t + 1)
                        nc.vector.tensor_tensor(s.y[:], ps[:, Y_BANK].rearrange("p (c t) -> p c t", c=CC),
                                                s.sr[:, bass.ds(gate, 1)].rearrange("p a c t -> p (a c) t"), ALU.mult).then_inc(s.y_ready, 1)
                    if step.inner and slot == STATS1_SLOT:
                        dve.wait_ge(s.x3tok_ready, m + 1)
                        layernorm_stats(nc, dve, s.l1, s.x3tok, m)
                    if step.tail and slot == X4_SLOT:
                        dve.wait_ge(s.op_full, t + 1)
                        nc.vector.scalar_tensor_tensor(out=s.x4T[:], in0=ps[:, TAIL_BANK, 0:NT], scalar=s.md_tail[:, 0:1], in1=g.xT[:, bass.ds(t_at, NT)],
                                                       op0=ALU.mult, op1=ALU.add).then_inc(s.x4_ready, 1)
                    if step.states and slot in SCAN_SLOT:
                        half = SCAN_SLOT[slot]
                        dve.wait_ge(s.dA_ready, 2 * n + half + 1)
                        for i in range(half * PAIRS // 2, (half + 1) * PAIRS // 2):
                            wait_bu(dve, n, i)
                        some = slice(half * NS // 2, (half + 1) * NS // 2)
                        for c in range(CC):
                            run = s.bu[:, c, some].rearrange("p n t -> p (n t)")
                            last = nc.vector.tensor_tensor_scan(run, s.dA[:, own, c, some].rearrange("p n t -> p (n t)"), run, 0.0, ALU.mult, ALU.add)
                        last.then_inc(s.scan_done, 1)
                    if step.inner and slot == NORMED1_SLOT:
                        layernorm_apply(nc, dve, s.l1, s.x3tok, m)
                    if step.delta and slot == DELTA_SLOT:
                        dve.wait_ge(s.sp_done, f + 1)
                        nc.vector.scalar_tensor_tensor(out=s.delta[:], in0=s.zb[:], scalar=0.0, in1=s.za[:], op0=ALU.max, op1=ALU.add).then_inc(s.delta_ready, 1)
                        dve.wait_ge(s.delta_ready, f + 1)
                        nc.vector.tensor_tensor(s.du[:, other], s.delta[:], s.h[:, other], ALU.mult).then_inc(s.du_ready, 1)
                    if step.states and C_SLOT.get(slot) in DVE_C:
                        i = C_SLOT[slot]
                        dve.wait_ge(s.scan_done, 2 * n + i // (PAIRS // 2) + 1)
                        dve.wait_ge(s.c_full, PAIRS * n + i + 1)
                        for c in range(CC):
                            both = s.bu[:, c, 2 * i:2 * i + 2]
                            last = nc.vector.tensor_tensor(both, both, ps[:, C_BANK[i % 2]].rearrange("p (n t) -> p n t", n=2), ALU.mult)
                        last.then_inc(s.yc_dve, 1)
                    if step.tail and slot == STATS2_SLOT:
                        dve.wait_ge(s.x4tok_ready, t + 1)
                        layernorm_stats(nc, dve, s.l2, s.x4tok, t)
                    if step.tail and slot == NORMED2_SLOT:
                        layernorm_apply(nc, dve, s.l2, s.x4tok, t)
                    if step.tail and slot == X5_SLOT:
                        dve.wait_ge(s.lin_full, t + 1)
                        nc.vector.tensor_scalar(s.tmp[:], ps[:, TAIL_BANK, 0:NT], g.blin[:], s.md_tail[:, 3:4], ALU.add, ALU.mult).then_inc(s.tmp_ready, 1)
                        dve.wait_ge(s.tmp_ready, t + 1)
                        nc.vector.tensor_tensor(s.x5T[:], s.tmp[:], s.x4T[:], ALU.add).then_inc(s.x5_ready, 1)

            phase_c_steps(dve, body)

        @block.gpsimd
        def _(pool):
            def body(step):
                n, m, t = step.n, step.n + 2, step.n - 1
                own = step.odd
                if step.inner:
                    m_at = m * NT if isinstance(m, int) else pool.snap(m * NT)
                for slot in range(SLOTS):
                    if step.inner and slot == X3_SLOT:
                        pool.wait_ge(s.x3_ready, m + 1)
                        nc.gpsimd.tensor_copy(g.xT[:, bass.ds(m_at, NT)], s.x3T[:]).then_inc(s.x3_kept, 1)
                    if step.states:
                        for j, is_c, i in copies(slot):
                            rows = s.rows[:, j % 2]
                            if is_c:
                                pool.wait_ge(s.scan_done, 2 * n + i // (PAIRS // 2) + 1)
                            else:
                                pool.wait_ge(s.du_ready, n + 1)
                            pool.wait_ge(s.rows_ready, N_POOL * n + j + 1)
                            for c in range(CC):
                                both = s.bu[:, c, 2 * i:2 * i + 2]
                                last = nc.gpsimd.tensor_tensor(both, both if is_c else s.du[:, own, c:c + 1].broadcast_to((P, 2, NT)), rows, ALU.mult)
                            last.then_inc(s.pool_mult, 1)
                    if step.inner and slot == STATS1_SLOT:
                        layernorm_pool(nc, pool, s.l1, g, m)
                    if step.tail and slot == STATS2_SLOT:
                        layernorm_pool(nc, pool, s.l2, g, t)

            phase_c_steps(pool, body)

        @block.scalar
        def _(act):
            act.wait_ge(s.zeroed, 1)
            act.sem_inc(s.stored, 16)

            def body(step):
                n, m, f, t, u = step.n, step.n + 2, step.n + 1, step.n - 1, step.n - 2
                own, other = step.odd, 1 - step.odd
                if step.inner:
                    gate = m & 3 if isinstance(m, int) else act.snap(m & 3)
                for slot in range(SLOTS):
                    if step.store and slot == XOUT_SLOT:
                        act.wait_ge(s.stored, 16 * u + 16)
                        act.wait_ge(s.out_full, u + 1)
                        nc.scalar.activation(s.xout[:], ps[:, TAIL_BANK, 0:NT].rearrange("p (t e) -> p t e", t=TT), ACT.Copy).then_inc(s.xout_ready, 1)
                    if step.states:
                        for j, is_c, i in copies(slot):
                            if j >= 2:
                                act.wait_ge(s.pool_mult, N_POOL * n + j - 1)
                            else:
                                wait(act, s.pool_mult, N_POOL * n + j - 1)
                            act.wait_ge(s.c_full if is_c else s.b_full, PAIRS * n + i + 1)
                            nc.scalar.activation(s.rows[:, j % 2], ps[:, (C_BANK if is_c else B_BANK)[i % 2]].rearrange("p (n t) -> p n t", n=2),
                                                 ACT.Copy).then_inc(s.rows_ready, 1)
                    if step.inner and slot == X3_TOK_SLOT:
                        act.wait_ge(s.x3_full, m + 1)
                        nc.scalar.activation(s.x3tok[:], ps[:, F_BANK, 0:NT].rearrange("p (t e) -> p t e", t=TT), ACT.Copy).then_inc(s.x3tok_ready, 1)
                    if step.delta and slot == Z_SLOT:
                        act.wait_ge(s.dl_full, f + 1)
                        for c in range(CC):
                            last = nc.scalar.activation(s.zb[:, c], ps[:, G_BANK, c * NT:(c + 1) * NT], ACT.Identity, bias=g.dt_b[:, c:c + 1])
                        last.then_inc(s.zb_ready, 1)
                        act.wait_ge(s.zb_ready, f + 1)
                        nc.scalar.activation(s.za[:], s.zb[:], ACT.Abs).then_inc(s.abs_done, 1)
                    if step.delta and slot == SOFTPLUS_SLOT:
                        act.wait_ge(s.abs_done, f + 1)
                        nc.scalar.activation(s.za[:], s.za[:], ACT.Exp, scale=-1.0).then_inc(s.exp_done, 1)
                        act.wait_ge(s.exp_done, f + 1)
                        nc.scalar.activation(s.za[:], s.za[:], ACT.Ln, bias=1.0).then_inc(s.sp_done, 1)
                    if step.tail and slot == X4_TOK_SLOT:
                        act.wait_ge(s.x4_full, t + 1)
                        nc.scalar.activation(s.x4tok[:], ps[:, TAIL_BANK, 0:NT].rearrange("p (t e) -> p t e", t=TT), ACT.Copy).then_inc(s.x4tok_ready, 1)
                    if step.inner and slot == HT_SLOT:
                        act.wait_ge(s.md_ready, m + 1)
                        act.wait_ge(s.h_full, m + 1)
                        nc.scalar.activation(s.hT[:], ps[:, F_BANK, NT:2 * NT], ACT.Identity, bias=s.md_inner[:, 0:1], scale=s.md_inner[:, 1:2]).then_inc(s.hT_ready, 1)
                    if step.delta and slot in FACTOR_SLOT:
                        if slot == min(FACTOR_SLOT):
                            act.wait_ge(s.delta_ready, f + 1)
                        for j in range(*FACTOR_SLOT[slot]):
                            half, c, i = j // NS, j % NS // (NS // 2), j // NS * (NS // 2) + j % (NS // 2)
                            last = nc.scalar.activation(s.dA[:, other, c, i, 1:NT], s.delta[:, c, 1:NT], ACT.Exp, scale=g.A[:, c, i:i + 1])
                            if j % NS == NS - 1:
                                last.then_inc(s.dA_ready, 1)
                    if step.inner and slot == XP_SLOT:
                        act.wait_ge(s.in_full, m + 1)
                        nc.scalar.activation(s.xp[:, :, TAPS - 1:], ps[:, G_BANK].rearrange("p (c t) -> p c t", c=CC), ACT.Copy).then_inc(s.xp_ready, 1)
                    if step.tail and slot == HT2_SLOT:
                        act.wait_ge(s.md_tail_ready, t + 1)
                        act.wait_ge(s.h2_full, t + 1)
                        nc.scalar.activation(s.hT2[:], ps[:, TAIL_BANK, 0:NT], ACT.Identity, bias=s.md_tail[:, 1:2], scale=s.md_tail[:, 2:3]).then_inc(s.hT2_ready, 1)
                    if step.inner and slot == SILU_SLOT:
                        act.wait_ge(s.conv_full, m + 1)
                        for c in range(CC):
                            last = nc.scalar.activation(s.h[:, own, c], ps[:, G_BANK, c * NT:(c + 1) * NT], ACT.Silu, bias=g.conv_b[:, c:c + 1])
                        last.then_inc(s.h_ready, 1)
                        nc.scalar.activation(s.sr[:, bass.ds(gate, 1)].rearrange("p a c t -> p (a c) t"), ps[:, F_BANK].rearrange("p (c t) -> p c t", c=CC),
                                             ACT.Silu).then_inc(s.gate_ready, 1)

            phase_c_steps(act, body)

        @block.tensor
        def _(pe):
            pe.wait_ge(s.w_in, 16 * 6)
            pe.wait_ge(s.built, 1)

            def body(step):
                n, m, f, t, u = step.n, step.n + 2, step.n + 1, step.n - 1, step.n - 2
                own, other = step.odd, 1 - step.odd

                def spread(bank, which, i):
                    for k in range(2):
                        last = nc.tensor.matmul(ps[:, bank, k * NT:(k + 1) * NT], s.sel[:, which * NS + 2 * i + k], s.xbc[:, own], start=True, stop=True)
                    return last

                def transpose_tokens(bank, src, at=0):
                    for tt in range(TT):
                        last = nc.tensor.transpose(ps[:, bank, at + tt * P:at + (tt + 1) * P], src[:, tt], g.ident[:])
                    return last

                def by_tile(buffer):
                    return buffer[:].rearrange("p (t e) -> p t e", t=TT)

                for slot in range(SLOTS):
                    if step.states and slot in B_SLOT:
                        if slot == 0:
                            pe.wait_ge(s.xd_ready, n + 1)
                        if slot >= 2 and slot - 2 in POOL_B:
                            pe.wait_ge(s.rows_ready, N_POOL * n + POOL_B.index(slot - 2) + 1)
                        elif slot >= 2:
                            pe.wait_ge(s.bu_dve, len(DVE_B) * n + DVE_B.index(slot - 2) + 1)
                        spread(B_BANK[slot % 2], 0, slot).then_inc(s.b_full, 1)
                    if step.states and slot in C_SLOT:
                        i = C_SLOT[slot]
                        if i >= 2 and i - 2 in POOL_C:
                            pe.wait_ge(s.rows_ready, N_POOL * n + len(POOL_B) + POOL_C.index(i - 2) + 1)
                        elif i >= 2:
                            pe.wait_ge(s.yc_dve, len(DVE_C) * n + DVE_C.index(i - 2) + 1)
                        spread(C_BANK[i % 2], 1, i).then_inc(s.c_full, 1)
                    if step.store and slot == OUT_SLOT_C:
                        pe.wait_ge(s.x5_ready, u + 1)
                        transpose_tokens(TAIL_BANK, by_tile(s.x5T)).then_inc(s.out_full, 1)
                    if step.delta and slot == XD_SLOT:
                        pe.wait_ge(s.h_ready, f + 1)
                        for c in range(CC):
                            last = nc.tensor.matmul(ps[:, G_BANK, 0:NT], s.Wx[:, c], s.h[:, other, c], start=c == 0, stop=c == CC - 1)
                        last.then_inc(s.xd_full, 1)
                    if step.inner and slot == X3_TR_SLOT:
                        pe.wait_ge(s.x3_ready, m + 1)
                        wait(pe, s.gate_ready, m)
                        transpose_tokens(F_BANK, by_tile(s.x3T)).then_inc(s.x3_full, 1)
                    if step.delta and slot == DL_SLOT:
                        pe.wait_ge(s.xd_ready, f + 1)
                        for c in range(CC):
                            last = nc.tensor.matmul(ps[:, G_BANK, c * NT:(c + 1) * NT], s.Wdt[RANK_ROWS, c * P:(c + 1) * P], s.dlt[RANK_ROWS], start=True, stop=True)
                        last.then_inc(s.dl_full, 1)
                    if step.tail and slot == OP_SLOT:
                        wait(pe, s.xout_ready, t)
                        pe.wait_ge(s.y_ready, t + 1)
                        for c in range(CC):
                            last = nc.tensor.matmul(ps[:, TAIL_BANK, 0:NT], s.Wout[:, c], s.y[:, c], start=c == 0, stop=c == CC - 1)
                        last.then_inc(s.op_full, 1)
                    if step.tail and slot == X4_TR_SLOT:
                        pe.wait_ge(s.x4_ready, t + 1)
                        transpose_tokens(TAIL_BANK, by_tile(s.x4T)).then_inc(s.x4_full, 1)
                    item, i = (n, slot - SUM_LAG) if slot >= SUM_LAG else (t, slot - SUM_LAG + SLOTS)
                    if (step.states if slot >= SUM_LAG else step.tail) and i < PAIRS:
                        if i == 0:
                            wait(pe, s.y_ready, item)
                        wait_yc(pe, item, i)
                        for k in (2 * i, 2 * i + 1):
                            last = nc.tensor.matmul(ps[:, Y_BANK], g.ident[:], s.bu[:, :, k], start=k == 0, stop=k == NS - 1, skip_group_check=True)
                        if i == 0:
                            for c in range(CC):
                                nc.tensor.matmul(ps[:, Y_BANK, c * NT:(c + 1) * NT], s.D_diag[:, c], s.h[:, own, c], start=False, stop=False, skip_group_check=True)
                        if i == PAIRS - 1:
                            last.then_inc(s.y_full, 1)
                    if step.inner and slot == H_TR_SLOT:
                        pe.wait_ge(s.l1.normed, m + 1)
                        transpose_tokens(F_BANK, s.l1.xn, NT).then_inc(s.h_full, 1)
                    if step.inner and slot == IN_SLOT:
                        if step.delta:
                            pe.wait_ge(s.zb_ready, f + 1)
                        pe.wait_ge(s.hT_ready, m + 1)
                        for c in range(2 * CC):
                            bank = G_BANK if c < CC else F_BANK
                            last = nc.tensor.matmul(ps[:, bank, c % CC * NT:(c % CC + 1) * NT], s.Win[:, c * P:(c + 1) * P], s.hT[:], start=True, stop=True)
                        last.then_inc(s.in_full, 1)
                    if step.tail and slot == H2_TR_SLOT:
                        pe.wait_ge(s.l2.normed, t + 1)
                        transpose_tokens(TAIL_BANK, s.l2.xn).then_inc(s.h2_full, 1)
                    if step.inner and slot == CONV_SLOT:
                        pe.wait_ge(s.xp_ready, m + 1)
                        for c in range(CC):
                            for k in range(TAPS):
                                last = nc.tensor.matmul(ps[:, G_BANK, c * NT:(c + 1) * NT], s.conv_diag[:, c, k], s.xp[:, c, k:k + NT], start=k == 0, stop=k == TAPS - 1)
                        last.then_inc(s.conv_full, 1)
                    if step.tail and slot == LIN_SLOT:
                        pe.wait_ge(s.hT2_ready, t + 1)
                        nc.tensor.matmul(ps[:, TAIL_BANK, 0:NT], g.wlinT[:], s.hT2[:], start=True, stop=True).then_inc(s.lin_full, 1)

            phase_c_steps(pe, body)



INPUTS = ["L0_attn_hidden_states", "L0_attn_Wq", "L0_attn_bq", "L0_attn_Wk", "L0_attn_bk", "L0_attn_Wv", "L0_attn_bv",
          "L0_attn_Wo", "L0_attn_bo", "L0_ffn_Wqkv", "L0_ffn_q_scale", "L0_ffn_k_scale", "L0_ffn_Wo", "L0_ffn_ln_g",
          "L0_ffn_ln_b", "L0_ffn_W1", "L0_ffn_b1", "L0_ffn_W2", "L0_ffn_b2", "L0_c", "L0_wmod", "L1_attn_in_proj_w",
          "L1_attn_conv_w", "L1_attn_conv_b", "L1_attn_x_proj_w", "L1_attn_dt_proj_w", "L1_attn_dt_proj_b", "L1_attn_A_log",
          "L1_attn_D_param", "L1_attn_out_proj_w", "L1_ffn_W", "L1_ffn_b", "L1_ffn_lora_down", "L1_ffn_lora_up",
          "L1_ffn_down_aux", "L1_ffn_up_aux", "L1_c", "L1_wmod"]


def build(nc, d, out):
    with ExitStack() as stack:
        g = Store(nc, stack, "all")
        g.ident = g.sb("ident", [P, P]); g.neg_half = g.sb("neg_half", [P, 2 * HB])
        g.xT = g.sb("xT", [P, NB * NT]); g.x2T = g.sb("x2T", [P, NB * NT])
        g.mod = g.sb("mod", [P, 2, NB, 6])
        g.wlinT = g.sb("wlinT", [P, P]); g.blin = g.sb("blin", [P, 1])
        g.conv_w = g.sb("conv_w", [P, CC, TAPS]); g.conv_b = g.sb("conv_b", [P, CC]); g.dt_b = g.sb("dt_b", [P, CC]); g.A = g.sb("A", [P, CC, NS]); g.D = g.sb("D", [P, CC])
        ps = stack.enter_context(nc.psum_tensor("ps", [P, 8, 512], F32))
        with ExitStack() as until_b:
            b = Store(nc, until_b, "until_b")
            g.ident_bf = b.sb("ident_bf", [P, P], BF16); g.mask_bf = b.sb("mask_bf", [P, TT * KEYS], BF16)
            g.rotab = b.sb("rotab", [P, DEPTH, 4, TT, DB]); g.lparam = b.sb("lparam", [P, DEPTH, 9])
            with ExitStack() as until_a:
                a = Store(nc, until_a, "until_a")
                g.mask_f = a.sb("mask_f", [P, TT * KEYS]); g.head_rows = a.sb("head_rows", [P, H0]); g.ones_row = a.sb("ones_row", [1, P])
                g.wqT = a.sb("wqT", [P, P]); g.wkT = a.sb("wkT", [P, P]); g.wvT = a.sb("wvT", [P, P]); g.woT = a.sb("woT", [P, P])
                g.bqk = a.sb("bqk", [P, 2]); g.bv_row = a.sb("bv_row", [1, P]); g.bo = a.sb("bo", [P, 1])
                setup(nc, g, d, ps)
                phase_a(nc, g, d, ps)
            phase_b(nc, g, d, ps)
        phase_c(nc, g, d, ps, out)


def shape_constants():
    i, c = np.arange(P)[:, None], np.arange(KEYS)[None, :]
    band = (c >= i) & (c <= i + WIN)
    mask = np.where(np.stack([band & (c >= WIN), band], 1), 0.0, MASKED).astype(np.float32).reshape(P, TT * KEYS)
    half = np.arange(0, DB, 2, dtype=np.float32)
    inv_freq = (np.float32(1.0) / np.float32(10000.0) ** (half / np.float32(DB))).astype(np.float32)
    t = np.arange(NT, dtype=np.float32)
    freqs = t[:, None] * inv_freq[None, :]
    base = ((half + np.float32(0.4 * DB)) / np.float32(1.4 * DB)).astype(np.float32)
    power = (t - NT // 2) / (WIN // 2)
    scale = base[None, :].astype(np.float64) ** power[:, None]
    cos, sin = np.cos(freqs.astype(np.float64)), np.sin(freqs.astype(np.float64))
    tables = []
    for factor in (8.0 * scale, 1.0 / scale):
        tables.append(np.concatenate([cos * factor, cos * factor], 1))
        tables.append(np.concatenate([-sin * factor, sin * factor], 1))
    rot = np.stack(tables, 0).astype(np.float32).reshape(4, TT, P, DB).transpose(2, 0, 1, 3)
    head_rows = np.kron(np.eye(H0, dtype=np.float32), np.ones((D0, 1), np.float32))
    return {"head_rows": head_rows, "ident": np.eye(P, dtype=np.float32), "mask": mask, "rot": np.ascontiguousarray(rot)}


def kernel(**inputs):
    import concourse.bacc as bacc
    from concourse.bass_utils import run_bass_kernel_spmd

    nc = bacc.Bacc("TRN2", target_bir_lowering=False, num_devices=1)
    arrays, d = {}, {}
    given = {name: np.ascontiguousarray(inputs[name]) for name in INPUTS}
    given.update(shape_constants())
    for name, a in given.items():
        arrays["in_" + name] = a
        d[name] = nc.dram_tensor("in_" + name, a.shape, mybir.dt.from_np(a.dtype), kind="ExternalInput").ap()
    out = nc.dram_tensor("out", (NB, NT, P), F32, kind="ExternalOutput").ap()
    build(nc, d, out)
    result = run_bass_kernel_spmd(nc, [arrays], core_ids=[0])
    return result.results[0]["out"]
```
